# Optimizing a Trainium2 kernel written in Bass

```python
import numpy as np
import jax
import jax.numpy as jnp

def _softmax(x, axis=-1):
    return jax.nn.softmax(x, axis=axis)

def _gelu(x):
    return jax.nn.gelu(x, approximate=True)

def _silu(x):
    return jax.nn.silu(x)

def _sigmoid(x):
    return jax.nn.sigmoid(x)

def _layernorm(x, axis=-1, eps=1e-05):
    m = jnp.mean(x, axis=axis, keepdims=True)
    v = jnp.var(x, axis=axis, keepdims=True)
    return (x - m) / jnp.sqrt(v + eps)

def _scatter_add(tgt, idx, src, axis=0):
    return tgt.at[idx].add(src)

def _segment_sum(src, seg, n):
    return jax.ops.segment_sum(src, seg, n)
kernel_name = 'mk_xattn_ffn_d2_seqx_r8_aa1641'

def setup_inputs(seed: int=0):
    np.random.seed(seed)
    _w = jnp.asarray

    def _rec_inputs():
        import jax
        import jax.numpy as jnp
        _rk = jax.random.key(seed)
        x = -0.000125 + 0.9999 * jax.random.normal(jax.random.fold_in(_rk, 1), (8, 256, 256), jnp.float32)
        _lenS = 256 - jax.random.randint(jax.random.fold_in(_rk, 7), (8,), 0, max(1, 256 // 4) + 1, jnp.int32)
        _lenS2 = 64 - jax.random.randint(jax.random.fold_in(_rk, 8), (8,), 0, max(1, 64 // 4) + 1, jnp.int32)
        _ctx_2048P = jax.random.normal(jax.random.fold_in(_rk, 11), (8, 16, 256), jnp.float32)
        _ctx_2048c = jax.random.dirichlet(jax.random.fold_in(_rk, 511), 0.3 * jnp.ones((16,), jnp.float32), (8, 64))
        _ctx_2048t = jnp.einsum('bsk,bkd->bsd', _ctx_2048c, _ctx_2048P)
        _ctx_2048t = _ctx_2048t * jax.lax.rsqrt(jnp.mean(jnp.square(_ctx_2048t)) + 1e-12) * 0.953939
        ctx_2048 = 0.00222621 + 0.99962 * (_ctx_2048t + 0.3 * jax.random.normal(jax.random.fold_in(_rk, 611), (8, 64, 256), jnp.float32))
        itok_Sx4_0_63 = jax.random.randint(jax.random.fold_in(_rk, 12), (256, 4), 0, 64, jnp.int32)
        return (x, ctx_2048, itok_Sx4_0_63)
    x, ctx_2048, itok_Sx4_0_63 = _rec_inputs()

    def _L0_xattn_setup():
        import math
        import jax, jax.numpy as jnp
        import numpy as np
        B, S, D, N, K, TOPK = (4, 512, 256, 64, 4, 2)
        key = jax.random.key(seed)
        k0, k1, k2, k3, k4 = jax.random.split(key, 5)
        token_states = jax.random.normal(k0, (B, S, D), dtype=jnp.float32)
        set_states = jax.random.normal(k1, (B, N, D), dtype=jnp.float32)
        desc_router = jax.random.normal(k2, (N, D), dtype=jnp.float32)
        token_to_sets = jax.random.randint(k3, (S, K), 0, N)
        bound = 1.0 / math.sqrt(D)
        W_q = jax.random.uniform(k4, (D, D), jnp.float32, -bound, bound)
        b_q = jnp.zeros((D,), jnp.float32)
        return {'token_states': token_states, 'set_states': set_states, 'desc_router': desc_router, 'W_q': W_q, 'b_q': b_q, 'token_to_sets': token_to_sets}
    _L0_xattn_all = _L0_xattn_setup()
    _L0_xattn_in = {k: v for k, v in _L0_xattn_all.items() if k in ('desc_router', 'W_q', 'b_q')}
    del _L0_xattn_all

    def _L0_ffn_setup():
        import jax, jax.numpy as jnp
        import numpy as np
        TOP_K = 4
        ROUTED_SCALE = 1.0
        NORM_TOPK = True
        B, S, H = (1, 256, 256)
        E, I = (16, 96)
        IS = 96
        key = jax.random.key(seed)
        ks = jax.random.split(key, 8)
        s = 0.02
        return {'hidden_states': jax.random.normal(ks[0], (B, S, H), jnp.float32), 'router_w': jax.random.normal(ks[1], (E, H), jnp.float32) * s, 'e_bias': jax.random.normal(ks[2], (E,), jnp.float32) * s, 'gate_up_proj': jax.random.normal(ks[3], (E, 2 * I, H), jnp.float32) * s, 'down_proj': jax.random.normal(ks[4], (E, H, I), jnp.float32) * s, 'shared_gate_w': jax.random.normal(ks[5], (IS, H), jnp.float32) * s, 'shared_up_w': jax.random.normal(ks[6], (IS, H), jnp.float32) * s, 'shared_down_w': jax.random.normal(ks[7], (H, IS), jnp.float32) * s}
    _L0_ffn_all = _L0_ffn_setup()
    _L0_ffn_in = {k: v for k, v in _L0_ffn_all.items() if k in ('router_w', 'e_bias', 'gate_up_proj', 'down_proj', 'shared_gate_w', 'shared_up_w', 'shared_down_w')}
    del _L0_ffn_all

    def _L1_xattn_setup():
        import jax, jax.numpy as jnp
        import numpy as np
        DIM = 256
        N_HEADS = 16
        HEAD_DIM = DIM // N_HEADS
        EPS = 1e-06
        IMG_LEN = 257

        def rms_norm(x, g, eps=EPS):
            var = jnp.mean(x * x, axis=-1, keepdims=True)
            return x * jax.lax.rsqrt(var + eps) * g

        def _attend(q, k, v, k_mask=None):
            scale = 1.0 / jnp.sqrt(jnp.asarray(HEAD_DIM, q.dtype))
            scores = jnp.einsum('bqnd,bknd->bnqk', q, k) * scale
            if k_mask is not None:
                neg = jnp.asarray(jnp.finfo(scores.dtype).min, scores.dtype)
                scores = jnp.where(k_mask[:, None, None, :], scores, neg)
            probs = jax.nn.softmax(scores, axis=-1)
            return jnp.einsum('bnqk,bknd->bqnd', probs, v)
        key = jax.random.key(seed)
        ks = jax.random.split(key, 16)
        B, L1, L2 = (1, 2048, 769)
        std = 0.02
        inp = {'x': jax.random.normal(ks[0], (B, L1, DIM), jnp.float32), 'context': jax.random.normal(ks[1], (B, L2, DIM), jnp.float32), 'context_lens': jax.random.randint(ks[2], (B,), 32, 513, jnp.int32), 'Wq': jax.random.normal(ks[3], (DIM, DIM), jnp.float32) * std, 'bq': jnp.zeros((DIM,), jnp.float32), 'gq': jnp.ones((DIM,), jnp.float32), 'Wk': jax.random.normal(ks[4], (DIM, DIM), jnp.float32) * std, 'bk': jnp.zeros((DIM,), jnp.float32), 'gk': jnp.ones((DIM,), jnp.float32), 'Wv': jax.random.normal(ks[5], (DIM, DIM), jnp.float32) * std, 'bv': jnp.zeros((DIM,), jnp.float32), 'Wk_img': jax.random.normal(ks[6], (DIM, DIM), jnp.float32) * std, 'bk_img': jnp.zeros((DIM,), jnp.float32), 'gk_img': jnp.ones((DIM,), jnp.float32), 'Wv_img': jax.random.normal(ks[7], (DIM, DIM), jnp.float32) * std, 'bv_img': jnp.zeros((DIM,), jnp.float32), 'Wo': jax.random.normal(ks[8], (DIM, DIM), jnp.float32) * std, 'bo': jnp.zeros((DIM,), jnp.float32)}
        return inp
    _L1_xattn_all = _L1_xattn_setup()
    _L1_xattn_in = {k: v for k, v in _L1_xattn_all.items() if k in ('context_lens', 'Wq', 'bq', 'gq', 'Wk', 'bk', 'gk', 'Wv', 'bv', 'Wk_img', 'bk_img', 'gk_img', 'Wv_img', 'bv_img', 'Wo', 'bo')}
    del _L1_xattn_all

    def _L1_ffn_setup():
        import jax, jax.numpy as jnp
        import numpy as np
        _Q_IN = 128
        _LUT_MIN = -128
        _Q_OUT = 1 << 16
        _TOP_K = 2
        _EXP_LUT = (jnp.exp(jnp.arange(_LUT_MIN, 1, dtype=jnp.float32) / _Q_IN) * _Q_OUT).astype(jnp.int32)

        def softmax_integer(logits):
            li = jnp.round(logits.astype(jnp.float32) * _Q_IN).astype(jnp.int32)
            shifted = jnp.clip(li - li.max(axis=-1, keepdims=True), _LUT_MIN, None)
            exp_vals = _EXP_LUT[shifted - _LUT_MIN]
            exp_sum = jnp.clip(exp_vals.sum(axis=-1, keepdims=True), 1, None)
            return exp_vals.astype(jnp.float32) / exp_sum.astype(jnp.float32)
        key = jax.random.key(seed)
        k0, k1, k2, k3, k4 = jax.random.split(key, 5)
        B, S, H, I, E = (4, 256, 256, 704, 8)
        x = jax.random.normal(k0, (B, S, H), dtype=jnp.float32)
        w_gate = jax.random.normal(k1, (E, H), dtype=jnp.float32) * 0.02
        w1 = jax.random.normal(k2, (E, I, H), dtype=jnp.float32) * 0.02
        w2 = jax.random.normal(k3, (E, H, I), dtype=jnp.float32) * 0.02
        w3 = jax.random.normal(k4, (E, I, H), dtype=jnp.float32) * 0.02
        return {'x': x, 'w_gate': w_gate, 'w1': w1, 'w2': w2, 'w3': w3}
    _L1_ffn_all = _L1_ffn_setup()
    _L1_ffn_in = {k: v for k, v in _L1_ffn_all.items() if k in ('w_gate', 'w1', 'w2', 'w3')}
    del _L1_ffn_all
    return {'x': x, 'ctx_2048': ctx_2048, 'itok_Sx4_0_63': itok_Sx4_0_63, 'L0_xattn_desc_router': _L0_xattn_in['desc_router'], 'L0_xattn_W_q': _L0_xattn_in['W_q'], 'L0_xattn_b_q': _L0_xattn_in['b_q'], 'L0_ffn_router_w': _L0_ffn_in['router_w'], 'L0_ffn_e_bias': _L0_ffn_in['e_bias'], 'L0_ffn_gate_up_proj': _L0_ffn_in['gate_up_proj'], 'L0_ffn_down_proj': _L0_ffn_in['down_proj'], 'L0_ffn_shared_gate_w': _L0_ffn_in['shared_gate_w'], 'L0_ffn_shared_up_w': _L0_ffn_in['shared_up_w'], 'L0_ffn_shared_down_w': _L0_ffn_in['shared_down_w'], 'L1_xattn_context_lens': _L1_xattn_in['context_lens'], 'L1_xattn_Wq': _L1_xattn_in['Wq'], 'L1_xattn_bq': _L1_xattn_in['bq'], 'L1_xattn_gq': _L1_xattn_in['gq'], 'L1_xattn_Wk': _L1_xattn_in['Wk'], 'L1_xattn_bk': _L1_xattn_in['bk'], 'L1_xattn_gk': _L1_xattn_in['gk'], 'L1_xattn_Wv': _L1_xattn_in['Wv'], 'L1_xattn_bv': _L1_xattn_in['bv'], 'L1_xattn_Wk_img': _L1_xattn_in['Wk_img'], 'L1_xattn_bk_img': _L1_xattn_in['bk_img'], 'L1_xattn_gk_img': _L1_xattn_in['gk_img'], 'L1_xattn_Wv_img': _L1_xattn_in['Wv_img'], 'L1_xattn_bv_img': _L1_xattn_in['bv_img'], 'L1_xattn_Wo': _L1_xattn_in['Wo'], 'L1_xattn_bo': _L1_xattn_in['bo'], 'L1_ffn_w_gate': _L1_ffn_in['w_gate'], 'L1_ffn_w1': _L1_ffn_in['w1'], 'L1_ffn_w2': _L1_ffn_in['w2'], 'L1_ffn_w3': _L1_ffn_in['w3']}

def reference(x, ctx_2048, itok_Sx4_0_63, L0_xattn_desc_router, L0_xattn_W_q, L0_xattn_b_q, L0_ffn_router_w, L0_ffn_e_bias, L0_ffn_gate_up_proj, L0_ffn_down_proj, L0_ffn_shared_gate_w, L0_ffn_shared_up_w, L0_ffn_shared_down_w, L1_xattn_context_lens, L1_xattn_Wq, L1_xattn_bq, L1_xattn_gq, L1_xattn_Wk, L1_xattn_bk, L1_xattn_gk, L1_xattn_Wv, L1_xattn_bv, L1_xattn_Wk_img, L1_xattn_bk_img, L1_xattn_gk_img, L1_xattn_Wv_img, L1_xattn_bv_img, L1_xattn_Wo, L1_xattn_bo, L1_ffn_w_gate, L1_ffn_w1, L1_ffn_w2, L1_ffn_w3):
    import jax
    import jax.numpy as jnp

    def _L0_xattn_ref(token_states, set_states, desc_router, W_q, b_q, token_to_sets):
        import math
        import jax, jax.numpy as jnp
        import numpy as np
        B, S, D, N, K, TOPK = (4, 512, 256, 64, 4, 2)
        batch, seq_len, d = token_states.shape
        num_sets = set_states.shape[1]
        scale = 1.0 / math.sqrt(d)
        q = jnp.einsum('bsd,ed->bse', token_states, W_q) + b_q
        scores = jnp.einsum('bse,ne->bsn', q, desc_router) * scale
        valid = token_to_sets >= 0
        mask = ((token_to_sets[:, :, None] == jnp.arange(num_sets)[None, None, :]) & valid[:, :, None]).any(axis=1)
        neg_inf = jnp.array(-jnp.inf, scores.dtype)
        scores = jnp.where(mask[None, :, :], scores, neg_inf)
        topk_vals, topk_idx = jax.lax.top_k(scores, TOPK)
        b_i = jnp.arange(batch)[:, None, None]
        s_i = jnp.arange(seq_len)[None, :, None]
        scores = jnp.full_like(scores, neg_inf).at[b_i, s_i, topk_idx].set(topk_vals)
        weights = jax.nn.softmax(scores, axis=-1)
        return jnp.einsum('bsn,bnd->bsd', weights, set_states)

    def _L0_ffn_ref(hidden_states, router_w, e_bias, gate_up_proj, down_proj, shared_gate_w, shared_up_w, shared_down_w):
        import jax, jax.numpy as jnp
        import numpy as np
        TOP_K = 4
        ROUTED_SCALE = 1.0
        NORM_TOPK = True
        B, S, H = (1, 256, 256)
        E, I = (16, 96)
        IS = 96
        orig_shape = hidden_states.shape
        x = hidden_states.reshape(-1, orig_shape[-1])
        T = x.shape[0]
        scores = jax.nn.sigmoid(x @ router_w.T)
        _, topk_idx = jax.lax.top_k(scores + e_bias[None, :], TOP_K)
        topk_w = jnp.take_along_axis(scores, topk_idx, axis=1)
        if NORM_TOPK:
            topk_w = topk_w / (topk_w.sum(axis=-1, keepdims=True) + 1e-20)
        topk_w = topk_w * ROUTED_SCALE
        combine = jnp.zeros((T, E), x.dtype).at[jnp.arange(T)[:, None], topk_idx].add(topk_w)

        def step(acc, xs):
            gu_w, d_w, c = xs
            gu = x @ gu_w.T
            g, u = jnp.split(gu, 2, axis=1)
            y = jax.nn.silu(g) * u @ d_w.T
            return (acc + c[:, None] * y, None)
        routed, _ = jax.lax.scan(step, jnp.zeros_like(x), (gate_up_proj, down_proj, combine.T))
        shared = jax.nn.silu(x @ shared_gate_w.T) * (x @ shared_up_w.T) @ shared_down_w.T
        return (routed + shared).reshape(orig_shape)

    def _L1_xattn_ref(x, context, context_lens, Wq, bq, gq, Wk, bk, gk, Wv, bv, Wk_img, bk_img, gk_img, Wv_img, bv_img, Wo, bo):
        import jax, jax.numpy as jnp
        import numpy as np
        DIM = 256
        N_HEADS = 16
        HEAD_DIM = DIM // N_HEADS
        EPS = 1e-06
        IMG_LEN = 257

        def rms_norm(x, g, eps=EPS):
            var = jnp.mean(x * x, axis=-1, keepdims=True)
            return x * jax.lax.rsqrt(var + eps) * g

        def _attend(q, k, v, k_mask=None):
            scale = 1.0 / jnp.sqrt(jnp.asarray(HEAD_DIM, q.dtype))
            scores = jnp.einsum('bqnd,bknd->bnqk', q, k) * scale
            if k_mask is not None:
                neg = jnp.asarray(jnp.finfo(scores.dtype).min, scores.dtype)
                scores = jnp.where(k_mask[:, None, None, :], scores, neg)
            probs = jax.nn.softmax(scores, axis=-1)
            return jnp.einsum('bnqk,bknd->bqnd', probs, v)
        b = x.shape[0]
        n, d = (N_HEADS, HEAD_DIM)
        ctx_img = context[:, :IMG_LEN]
        ctx_txt = context[:, IMG_LEN:]
        q = rms_norm(x @ Wq + bq, gq).reshape(b, -1, n, d)
        k = rms_norm(ctx_txt @ Wk + bk, gk).reshape(b, -1, n, d)
        v = (ctx_txt @ Wv + bv).reshape(b, -1, n, d)
        k_img = rms_norm(ctx_img @ Wk_img + bk_img, gk_img).reshape(b, -1, n, d)
        v_img = (ctx_img @ Wv_img + bv_img).reshape(b, -1, n, d)
        img_x = _attend(q, k_img, v_img)
        k_mask = jnp.arange(k.shape[1])[None, :] < context_lens[:, None]
        txt_x = _attend(q, k, v, k_mask)
        out = (txt_x + img_x).reshape(b, -1, n * d)
        return out @ Wo + bo

    def _L1_ffn_ref(x, w_gate, w1, w2, w3):
        import jax, jax.numpy as jnp
        import numpy as np
        _Q_IN = 128
        _LUT_MIN = -128
        _Q_OUT = 1 << 16
        _TOP_K = 2
        _EXP_LUT = (jnp.exp(jnp.arange(_LUT_MIN, 1, dtype=jnp.float32) / _Q_IN) * _Q_OUT).astype(jnp.int32)

        def softmax_integer(logits):
            li = jnp.round(logits.astype(jnp.float32) * _Q_IN).astype(jnp.int32)
            shifted = jnp.clip(li - li.max(axis=-1, keepdims=True), _LUT_MIN, None)
            exp_vals = _EXP_LUT[shifted - _LUT_MIN]
            exp_sum = jnp.clip(exp_vals.sum(axis=-1, keepdims=True), 1, None)
            return exp_vals.astype(jnp.float32) / exp_sum.astype(jnp.float32)
        orig_shape = x.shape
        H = orig_shape[-1]
        xf = x.reshape(-1, H)
        T = xf.shape[0]
        E = w_gate.shape[0]
        router_logits = xf @ w_gate.T
        routing_weights = softmax_integer(router_logits)
        top_w, top_i = jax.lax.top_k(routing_weights, _TOP_K)
        top_w = top_w / top_w.sum(axis=-1, keepdims=True)
        combine = jnp.zeros((T, E), xf.dtype).at[jnp.arange(T)[:, None], top_i].add(top_w)
        out = jnp.zeros_like(xf)
        for e in range(E):
            h = jax.nn.silu(xf @ w1[e].T) * (xf @ w3[e].T)
            out = out + combine[:, e:e + 1] * (h @ w2[e].T)
        return out.reshape(orig_shape)
    x = x + _L0_xattn_ref(_layernorm(x, axis=-1), ctx_2048, L0_xattn_desc_router, L0_xattn_W_q, L0_xattn_b_q, itok_Sx4_0_63)
    x = x + _L0_ffn_ref(_layernorm(x, axis=-1), L0_ffn_router_w, L0_ffn_e_bias, L0_ffn_gate_up_proj, L0_ffn_down_proj, L0_ffn_shared_gate_w, L0_ffn_shared_up_w, L0_ffn_shared_down_w)
    x = x + _L1_xattn_ref(_layernorm(x, axis=-1), ctx_2048, L1_xattn_context_lens, L1_xattn_Wq, L1_xattn_bq, L1_xattn_gq, L1_xattn_Wk, L1_xattn_bk, L1_xattn_gk, L1_xattn_Wv, L1_xattn_bv, L1_xattn_Wk_img, L1_xattn_bk_img, L1_xattn_gk_img, L1_xattn_Wv_img, L1_xattn_bv_img, L1_xattn_Wo, L1_xattn_bo)
    x = x + _L1_ffn_ref(_layernorm(x, axis=-1), L1_ffn_w_gate, L1_ffn_w1, L1_ffn_w2, L1_ffn_w3)
    return x

_drawn_inputs = setup_inputs


def setup_inputs(seed=0):
    import zlib

    import numpy as np

    out = dict(_drawn_inputs(seed))
    spreads = {'L0_xattn_b_q': (0.0, 0.1),
     'L1_xattn_bq': (0.0, 2.0),
     'L1_xattn_gq': (1.0, 0.6),
     'L1_xattn_bk': (0.0, 0.1),
     'L1_xattn_gk': (1.0, 0.2),
     'L1_xattn_bv': (0.0, 0.1),
     'L1_xattn_bk_img': (0.0, 2.0),
     'L1_xattn_gk_img': (1.0, 0.6),
     'L1_xattn_bv_img': (0.0, 1.073),
     'L1_xattn_bo': (0.0, 0.303)}
    factors = {'L0_ffn_router_w': 8.0,
     'L0_ffn_e_bias': 8.0,
     'L0_ffn_gate_up_proj': 8.0,
     'L0_ffn_down_proj': 8.0,
     'L0_ffn_shared_gate_w': 7.196,
     'L0_ffn_shared_up_w': 6.985,
     'L0_ffn_shared_down_w': 7.056,
     'L1_xattn_Wq': 16.93,
     'L1_xattn_Wk_img': 17.412,
     'L1_ffn_w_gate': 4.248,
     'L1_ffn_w1': 3.684,
     'L1_ffn_w2': 3.651,
     'L1_ffn_w3': 3.641,
     'L1_xattn_Wv_img': 2.806}
    for name, (base, spread) in spreads.items():
        noise = np.random.default_rng([zlib.crc32(name.encode()), seed]).standard_normal(out[name].shape)
        drawn = base * np.exp(spread * noise) if base else spread * noise
        out[name] = jnp.asarray(drawn.astype(out[name].dtype))
    for name, factor in factors.items():
        out[name] = (out[name] * factor).astype(out[name].dtype)
    return out
```

```python
import math
from contextlib import ExitStack

import numpy as np

import concourse.bass as bass
from concourse import mybir

F32 = mybir.dt.float32
BF16 = mybir.dt.bfloat16
I32 = mybir.dt.int32
ALU = mybir.AluOpType
ACT = mybir.ActivationFunctionType
AX = mybir.AxisListType

P = 128
B, S, D = 8, 256, 256
KD = D // P
NT = B * S // P
TB = S // P
NK = 64
TOPK_SETS = 4
E0, I0 = 16, 96
C0 = E0 * I0 // P + 1
E1, I1 = 8, 704
C1 = -(-I1 // P)
H, HD = 16, 16
NEG = -3.0e38
FOUND = 3.0e38
ROUND = 12582912.0
Q_IN = 128
Q_OUT = 65536.0
HALF1 = I1 // 2
W13 = 2 * I1
WE = KD * W13 + C1 * D


def exp_coefficients(degree=8):
    z = np.linspace(-1, 0, 4001)
    c = np.polynomial.chebyshev.Chebyshev.fit(z, np.exp(z), degree, domain=[-1, 0])
    return [float(v) for v in c.convert(kind=np.polynomial.Polynomial).coef]


def program(nc, x_in, ctx_in, ctxT_in, itok_in, descT_in, wq0_in, bq0_in, rw0_in, ebias_in,
            gu0_in, dn0_in, wq1_in, bq1_in, gq1_in, wk1_in, bk1_in, gk1_in, wv1_in, bv1_in,
            wo1_in, bo1_in, wg1_in, wexp_in, out):
    with ExitStack() as st:
        def sb(name, shape, dt=F32):
            return st.enter_context(nc.sbuf_tensor(name, shape, dt))

        def sem(name):
            return st.enter_context(nc.semaphore(name))

        x_sb = sb("x_sb", [P, NT, D])
        xnT = sb("xnT", [P, KD, NT * P])
        wexp = sb("wexp", [P, E1 * WE])
        arena = sb("arena", [P, 4224])

        def view(tensor, first, *shape):
            v = tensor[:, first:first + int(np.prod(shape))]
            names = "abcd"[:len(shape)]
            if len(shape) > 1:
                v = v.rearrange(f"p ({' '.join(names)}) -> p {' '.join(names)}",
                                **dict(zip(names[:-1], shape)))
            return v

        ctxT = view(wexp, 0, KD, B, 2, NK)
        wkv = view(wexp, 2048, KD, 2, D)
        ksq = view(wexp, 3072, KD, B * NK)
        kvar = view(wexp, 4096, B * NK)
        krst = view(wexp, 4608, B * NK)
        bv_row = wexp[0:1, 5120:5120 + D]
        ms = view(wexp, 5632, NT, NK)
        picked = view(wexp, 6656, NT, NK)
        ex = view(wexp, 7680, NT, NK)
        wT = wexp[0:NK, 8704:8704 + NT * P]
        ctx_sb = wexp[0:NK, 10752:10752 + B * D].rearrange("p (b d) -> p b d", b=B)
        wq0 = view(wexp, 12800, KD, D)
        descT = view(wexp, 13312, KD, NK)
        route0 = view(wexp, 13440, KD, NK)
        negmask = view(wexp, 13568, TB, NK)
        hit = view(wexp, 13696, TB, NK)
        brow = wexp[0:1, 13824:13824 + NK]
        late = 5 * WE
        GU0 = 2 * E0 * I0 + 2 * I0
        gu0 = view(wexp, late, KD, GU0)
        dn0 = view(wexp, late + KD * GU0, C0, D)
        sg0 = view(wexp, late + KD * GU0 + C0 * D, 2, 512)
        hm0 = view(wexp, late + KD * GU0 + C0 * D + 1024, 2, 512)
        h0 = view(wexp, late + KD * GU0 + C0 * D + 2048, 2, 512)
        last = 7 * WE
        kbd = view(wexp, last, 2, 1024)
        pT = view(wexp, last + 2048, 2, 8, P)
        xn = view(arena, 0, 2, TB, D)
        cT = arena[0:96, 0:1024].bitcast(BF16)
        c3 = arena[:, 1024:1792].bitcast(BF16).rearrange("p (t c) -> p t c", t=NT)
        spread = arena[0:96, 1792:2560].bitcast(BF16)
        sc0 = view(arena, 2560, NT, E0)
        sel0 = view(arena, 2816, NT, E0 + 4)
        rep0 = view(arena, 3136, NT, E0 + 4)
        cw0 = view(arena, 3456, NT, E0)
        res0 = view(arena, 3712, NT, E0)
        shift = view(arena, 0, H * NK)
        probs = view(arena, 1024, H * NK)
        sqT = view(arena, 2048, 2, KD, S)
        qt = view(arena, 3072, 2, KD, P)
        att = view(arena, 3584, D)
        attT = view(arena, 3840, KD, P)
        li = view(arena, 1024, NT, E1)
        sh = view(arena, 1152, NT, E1)
        key = view(arena, 1280, NT, E1)
        zz = view(arena, 1408, NT, E1)
        po = view(arena, 1536, NT, E1)
        xt1 = view(arena, 1664, 2, KD, P)
        sg1 = view(arena, 0, I1)
        h1 = view(arena, 704, I1)
        hT = view(arena, 2176, C1, P)
        ident = sb("ident", [P, P])
        identb = sb("identb", [P, P], BF16)
        ones = sb("ones", [P, P])
        st6 = sb("st6", [P, TB, 6])
        mv = sb("mv", [P, TB, 2])
        mean = sb("mean", [P, NT])
        carrier = sb("carrier", [P, 1])
        ve = sb("ve", [P, NT])
        rstd = sb("rstd", [P, NT])
        mhalf = sb("mhalf", [P, 1])
        m8 = sb("m8", [P, NT, 8])
        t8 = sb("t8", [P, NT, 8])
        negm = sb("negm", [P, NT])
        sums = sb("sums", [P, NT])
        recs = sb("recs", [P, NT])
        iota64 = sb("iota64", [P, NK])
        itok = sb("itok", [P, TB, TOPK_SETS], I32)
        bq0 = sb("bq0", [P, KD])
        rw0 = sb("rw0", [P, KD, E0])
        ebias = sb("ebias", [P, E0])
        wq1 = sb("wq1", [P, KD, D])
        wo1 = sb("wo1", [P, KD, D])
        bo_row = sb("bo_row", [1, D])
        vecs = sb("vecs", [P, 4, KD])
        gg = sb("gg", [P, KD])
        wg1 = sb("wg1", [P, KD, E1])
        kT = sb("kT", [P, KD, B * NK])
        vbd = sb("vbd", [P, B, H // 2, 2 * (HD + 1)])
        hmask = sb("hmask", [P, H // 2])
        pmask = sb("pmask", [P, 2])
        mx1 = sb("mx1", [P, H])
        rec1 = sb("rec1", [P, H])
        ssq = sb("ssq", [P, NT])
        rq = sb("rq", [P, NT])
        comb1 = sb("comb1", [P, NT, E1])
        m1 = sb("m1", [P, NT])

        ps = st.enter_context(nc.psum_tensor("ps", [P, 8 * 512], F32))

        def bank(i, n=1):
            return ps[:, 512 * i:512 * (i + n)]

        a_exp, a_masked, a_max, a_mixed = sem("a_exp"), sem("a_masked"), sem("a_max"), sem("a_mixed")
        a_picked, a_rec, a_route, a_routed = sem("a_picked"), sem("a_rec"), sem("a_route"), sem("a_routed")
        a_scored, a_top, a_turned, a_wT = sem("a_scored"), sem("a_top"), sem("a_turned"), sem("a_wT")
        a_wts = sem("a_wts")
        b_c3, b_cT, b_down, b_hidden = sem("b_c3"), sem("b_cT"), sem("b_down"), sem("b_hidden")
        b_logits, b_max, b_prod, b_sig = sem("b_logits"), sem("b_max"), sem("b_prod"), sem("b_sig")
        b_silu, b_spread, b_step, b_turned = sem("b_silu"), sem("b_spread"), sem("b_step"), sem("b_turned")
        b_up = sem("b_up")
        c_att, c_attT, c_attTc, c_kbd = sem("c_att"), sem("c_attT"), sem("c_attTc"), sem("c_kbd")
        c_max, c_pT, c_probs, c_proj = sem("c_max"), sem("c_pT"), sem("c_probs"), sem("c_proj")
        c_pv, c_q, c_qT, c_qt = sem("c_pv"), sem("c_q"), sem("c_qT"), sem("c_qt")
        c_rec, c_rq, c_scores, c_shift = sem("c_rec"), sem("c_rq"), sem("c_scores"), sem("c_shift")
        c_sq, c_ssq, c_turned, c_var = sem("c_sq"), sem("c_ssq"), sem("c_turned"), sem("c_var")
        d_added, d_down, d_hT, d_hidden = sem("d_added"), sem("d_down"), sem("d_hT"), sem("d_hidden")
        d_logits, d_max, d_silu, d_step = sem("d_logits"), sem("d_max"), sem("d_silu"), sem("d_step")
        d_turned, d_up, d_xt = sem("d_turned"), sem("d_up"), sem("d_xt")
        dve_const = sem("dve_const")
        gg_ready = sem("gg_ready")
        in_ctx, in_exp0, in_exp7, in_ffn0 = sem("in_ctx"), sem("in_exp0"), sem("in_exp7"), sem("in_ffn0")
        in_itok, in_kv, in_rest, in_set0 = sem("in_itok"), sem("in_kv"), sem("in_rest"), sem("in_set0")
        in_x0, in_x1 = sem("in_x0"), sem("in_x1")
        k_copied, k_pow, k_psum, k_scaled = sem("k_copied"), sem("k_pow"), sem("k_psum"), sem("k_scaled")
        k_sum, k_var = sem("k_sum"), sem("k_var")
        ln_copied, ln_mv, ln_rows, ln_rstd = sem("ln_copied"), sem("ln_mv"), sem("ln_rows"), sem("ln_rstd")
        ln_stats, ln_turned, ln_var = sem("ln_stats"), sem("ln_turned"), sem("ln_var")
        out_done = sem("out_done")
        pool_step = sem("pool_step")
        s_mask = sem("s_mask")
        v_psum, v_ready = sem("v_psum"), sem("v_ready")
        x_new = sem("x_new")

        XA, XB, XC = NT, NT + NT // 2, 2 * NT + NT // 2
        NG = NT // 4

        def each(eng, n, lead, step, body):
            for i in range(lead):
                body(i, i)
            with eng.Fori(0, (n - lead) // step) as turn:
                for j in range(step):
                    body(turn * step + (lead + j), lead + j)

        block = st.enter_context(nc.Block())

        @block.sync
        def _(sp):
            x_v = x_in.rearrange("b (j p) d -> p (b j) d", p=P)
            half = NT // 2
            sp.dma_start(x_sb[:, 0:half, :], x_v[:, 0:half, :]).then_inc(in_x0, 16)
            sp.dma_start(x_sb[:, half:NT, :], x_v[:, half:NT, :]).then_inc(in_x1, 16)
            sp.dma_start(wq0, wq0_in.rearrange("(k p) n -> p k n", p=P)).then_inc(in_set0, 16)
            sp.dma_start(descT, descT_in.rearrange("(k p) n -> p k n", p=P)).then_inc(in_set0, 16)
            sp.dma_start(bq0[:, :], bq0_in).then_inc(in_set0, 16)
            sp.dma_start(itok[:, :, :], itok_in.rearrange("(j p) k -> p j k", p=P)).then_inc(in_itok, 16)
            sp.dma_start(ctx_sb, ctx_in.rearrange("b n d -> n b d")).then_inc(in_ctx, 16)
            for k in range(KD):
                for m, src in enumerate((wk1_in, wv1_in)):
                    sp.dma_start(wkv[:, k, m, :], src[k * P:(k + 1) * P, :]).then_inc(in_kv, 16)
                for r in range(2):
                    sp.dma_start(ctxT[:, k, :, r, :], ctxT_in[k * P:(k + 1) * P, :].rearrange(
                        "p (b n) -> p b n", b=B)).then_inc(in_kv, 16)
            for m, src in enumerate((bq1_in, gq1_in, bk1_in, gk1_in)):
                sp.dma_start(vecs[:, m, :], src).then_inc(in_kv, 16)
            sp.dma_start(bv_row, bv1_in.unsqueeze(0)).then_inc(in_kv, 16)
            sp.dma_start(rw0[:, :, :], rw0_in.rearrange("(k p) n -> p k n", p=P)).then_inc(in_rest, 16)
            sp.dma_start(ebias[:, :], ebias_in.partition_broadcast(P)).then_inc(in_rest, 16)
            for k in range(KD):
                sp.dma_start(gu0[:, k, :], gu0_in[k * P:(k + 1) * P, :]).then_inc(in_ffn0, 16)
            sp.dma_start(dn0, dn0_in).then_inc(in_ffn0, 16)
            sp.dma_start(bo_row[:, :], bo1_in.unsqueeze(0)).then_inc(in_rest, 16)
            sp.dma_start(wq1[:, :, :], wq1_in.rearrange("(k p) n -> p k n", p=P)).then_inc(in_rest, 16)
            sp.dma_start(wo1[:, :, :], wo1_in.rearrange("(k p) n -> p k n", p=P)).then_inc(in_rest, 16)
            sp.dma_start(wg1[:, :, :], wg1_in.rearrange("(k p) n -> p k n", p=P)).then_inc(in_rest, 16)
            sp.wait_ge(x_new, XA)
            sp.wait_ge(v_ready, 2 * B)
            for e in range(5):
                sp.dma_start(wexp[:, e * WE:(e + 1) * WE], wexp_in[:, e, :]).then_inc(in_exp0, 16)
            sp.wait_ge(b_down, 4 * C0)
            for e in range(5, 7):
                sp.dma_start(wexp[:, e * WE:(e + 1) * WE], wexp_in[:, e, :]).then_inc(in_exp0, 16)
            sp.wait_ge(x_new, XC)
            sp.dma_start(wexp[:, last:last + WE], wexp_in[:, 7, :]).then_inc(in_exp7, 16)
            o_v = out.rearrange("b (j p) d -> p (b j) d", p=P)
            for t in range(NT):
                sp.wait_ge(d_added, E1 * (t + 1))
                sp.dma_start(o_v[:, t, :], x_sb[:, t, :]).then_inc(out_done, 16)
            sp.wait_ge(out_done, 16 * NT)

        @block.gpsimd
        def _(pool):
            pool.memset(ident[:, :], 0.0).then_inc(pool_step, 1)
            pool.memset(ones[:, :], 1.0).then_inc(pool_step, 1)
            pool.memset(hmask[:, :], 1.0).then_inc(pool_step, 1)
            pool.memset(mhalf[:, :], -0.5).then_inc(pool_step, 1)
            pool.iota(iota64[:, :], [[1, NK]], base=0, channel_multiplier=0,
                      allow_small_or_imprecise_dtypes=True).then_inc(pool_step, 1)
            pool.wait_ge(pool_step, 5)
            pool.affine_select(out=ident[:, :], in_=ident[:, :], compare_op=ALU.not_equal, fill=1.0,
                               base=0, pattern=[[-1, P]], channel_multiplier=1).then_inc(pool_step, 1)
            pool.affine_select(out=hmask[:, :], in_=hmask[:, :], compare_op=ALU.is_ge, fill=0.0,
                               base=0, pattern=[[-HD, H // 2]], channel_multiplier=1).then_inc(pool_step, 1)
            pool.wait_ge(pool_step, 7)
            pool.affine_select(out=hmask[:, :], in_=hmask[:, :], compare_op=ALU.is_ge, fill=0.0,
                               base=HD - 1, pattern=[[HD, H // 2]], channel_multiplier=-1).then_inc(pool_step, 1)
            pool.tensor_copy(identb[:, :], ident[:, :]).then_inc(pool_step, 1)
            def power(norm):
                def one(b, k):
                    pool.wait_ge(ln_var, norm * B + b + 1)
                    pool.tensor_tensor(rstd[:, bass.ds(b * TB, TB)], ve[:, bass.ds(b * TB, TB)],
                                       mhalf[:, 0:1].broadcast_to([P, TB]), ALU.pow).then_inc(ln_rstd, 1)
                each(pool, B, 0, 2, one)

            pool.wait_ge(pool_step, 9)
            power(0)
            pool.wait_ge(k_var, 1)
            pool.tensor_tensor(krst, kvar, mhalf[:, 0:1].broadcast_to([P, B * NK]), ALU.pow).then_inc(k_pow, 1)
            power(1)
            pool.memset(spread, 0.0).then_inc(pool_step, 1)
            v = spread.rearrange("p (e u) -> p e u", e=E0)
            for part in range(3):
                pool.wait_ge(pool_step, 10 + part)
                pool.affine_select(out=v, in_=v, compare_op=ALU.not_equal, fill=1.0, base=-32 * part,
                                   pattern=[[-1, E0], [0, I0]], channel_multiplier=1).then_inc(pool_step, 1)
            power(2)
            pool.wait_ge(c_var, 1)
            pool.tensor_tensor(rq[:, :], ssq[:, :], mhalf[:, 0:1].broadcast_to([P, NT]), ALU.pow).then_inc(c_rq, 1)

            def diagonal(b, k):
                if k >= 2:
                    pool.wait_ge(c_scores, (b - 1) * TB)
                for m in range(KD):
                    pool.tensor_tensor(
                        kbd[:, k % 2, m * 512:(m + 1) * 512].rearrange("p (h n) -> p h n", h=H // 2),
                        kT[:, m:m + 1, bass.ds(b * NK, NK)].broadcast_to([P, H // 2, NK]),
                        hmask[:, :].unsqueeze(2).broadcast_to([P, H // 2, NK]),
                        ALU.mult).then_inc(c_kbd, 1)
            pool.wait_ge(x_new, XB)
            pool.wait_ge(k_scaled, KD)
            each(pool, B, 2, 2, diagonal)
            power(3)

        @block.scalar
        def _(act):
            def copy_rows(norm):
                def one(b, k):
                    act.wait_ge(ln_turned, norm * B + b + 1)
                    act.activation(xnT[:, :, bass.ds(b * S, S)],
                                   bank(k % 2).rearrange("p (k n) -> p k n", k=KD),
                                   ACT.Copy).then_inc(ln_copied, 1)
                each(act, B, 0, 2, one)

            act.wait_ge(a_route, 1)
            act.activation(route0, bank(6)[:, 0:KD * NK].rearrange("p (k n) -> p k n", k=KD),
                           ACT.Copy, scale=1.0 / math.sqrt(D)).then_inc(a_routed, 1)
            act.activation(brow, bank(6)[0:1, 256:256 + NK], ACT.Copy,
                           scale=1.0 / math.sqrt(D)).then_inc(a_routed, 1)
            copy_rows(0)
            act.wait_ge(k_psum, 1)
            act.wait_ge(in_kv, 16 * 13)
            for m in range(KD):
                act.activation(kT[:, m, :], bank(6 + m), ACT.Identity, bias=vecs[:, 2, m:m + 1]).then_inc(k_copied, 1)
                act.activation(ksq[:, m, :], bank(6 + m), ACT.Square, bias=vecs[:, 2, m:m + 1]).then_inc(k_copied, 1)

            with act.Fori(0, B) as b:
                act.wait_ge(a_top, b * 2 + 2)
                for j in range(TB):
                    act.activation(ex[:, b * TB + j, :], ms[:, b * TB + j, :], ACT.Exp,
                                   bias=negm[:, bass.ds(b * TB + j, 1)]).then_inc(a_exp, 1)
            for q in range(NT // 4):
                act.wait_ge(a_turned, q + 1)
                act.activation(wT[:, q * 512:(q + 1) * 512], bank(4 + q % 2)[0:NK, :], ACT.Copy).then_inc(a_wT, 1)
            copy_rows(1)
            act.wait_ge(b_logits, 1)
            act.activation(sc0, bank(6)[:, 0:NT * E0].rearrange("p (t e) -> p t e", t=NT), ACT.Sigmoid).then_inc(b_sig, 1)
            for g in range(4):
                act.wait_ge(b_turned, g + 1)
                act.activation(cT[:, g * 512:(g + 1) * 512], bank(4 + g % 2).bitcast(BF16)[0:96, 0:512],
                               ACT.Copy).then_inc(b_cT, 1)

            def silu_group(g, k):
                for c in range(C0):
                    i, rows = g * C0 + c, P if c < C0 - 1 else I0
                    act.wait_ge(b_up, i + 1)
                    if k or c >= 2:
                        act.wait_ge(b_prod, i if c == 0 else i - 1)
                    act.activation(sg0[0:rows, c % 2, :], bank(c % 2)[0:rows, :], ACT.Silu).then_inc(b_silu, 1)
            each(act, NG, 1, 1, silu_group)
            copy_rows(2)
            act.wait_ge(in_rest, 16 * 6)

            def queries(b, k):
                act.wait_ge(c_q, b + 1)
                if k >= 2:
                    act.wait_ge(c_ssq, b - 1)
                for m in range(KD):
                    act.activation(sqT[:, k % 2, m, :], bank(2 + k % 2)[:, m * S:(m + 1) * S], ACT.Square,
                                   bias=vecs[:, 0, m:m + 1]).then_inc(c_sq, 1)
                    act.activation(xnT[:, m, bass.ds(b * S, S)], bank(2 + k % 2)[:, m * S:(m + 1) * S],
                                   ACT.Identity, bias=vecs[:, 0, m:m + 1]).then_inc(c_qT, 1)
            each(act, B, 2, 2, queries)

            def pick_tile(t, k):
                if k >= 2:
                    act.wait_ge(c_scores, t - 1)
                act.activation(qt[:, k % 2, :, :], xnT[:, :, bass.ds(t * P, P)], ACT.Copy).then_inc(c_qt, 1)

            def exp_scores(t, k):
                act.wait_ge(c_shift, t + 1)
                if k == 0:
                    act.wait_ge(c_rq, 1)
                if k >= 1:
                    act.wait_ge(c_turned, t)
                act.activation(probs, shift, ACT.Exp, scale=rq[:, bass.ds(t, 1)]).then_inc(c_probs, 1)

            def copy_probs(t, k):
                act.wait_ge(c_turned, t + 1)
                if k >= 2:
                    act.wait_ge(c_pv, t - 1)
                act.activation(pT[:, k % 2, :, :], bank(2, 2).rearrange("p (c n) -> p c n", c=8),
                               ACT.Copy).then_inc(c_pT, 1)

            def copy_att(t, k):
                act.wait_ge(c_attT, t + 1)
                act.activation(attT, bank(5)[:, 0:D].rearrange("p (k n) -> p k n", k=KD), ACT.Copy).then_inc(c_attTc, 1)

            act.wait_ge(c_qT, B * KD)

            def softmax_tile(t, k):
                pick_tile(t, k)
                exp_scores(t, k)
                if k >= 1:
                    copy_probs(t - 1, k - 1)
                if k >= 2:
                    copy_att(t - 2, k - 2)
            each(act, NT, 4, 4, softmax_tile)
            copy_probs(NT - 1, 3)
            copy_att(NT - 2, 2)
            copy_att(NT - 1, 3)
            copy_rows(3)

            def tile_rows(t, k):
                if k >= 2:
                    act.wait_ge(d_up, (t - 1) * E1)
                act.activation(xt1[:, k % 2, :, :], xnT[:, :, bass.ds(t * P, P)], ACT.Copy).then_inc(d_xt, 1)

            act.wait_ge(ln_copied, 4 * B)

            def block_act(t, k):
                tile_rows(t, k)
                for e in range(E1):
                    i = t * E1 + e
                    act.wait_ge(d_up, i + 1)
                    if k or e:
                        act.wait_ge(d_hidden, i)
                    act.activation(sg1.rearrange("p (a n) -> p a n", a=2),
                                   bank(0, 2).rearrange("p (a n) -> p a n", a=2)[:, :, 0:HALF1],
                                   ACT.Silu).then_inc(d_silu, 1)
                    act.wait_ge(d_turned, i + 1)
                    act.activation(hT[:, 0:C1 - 1, :], bank(4, 2)[:, 0:(C1 - 1) * P].rearrange("p (c n) -> p c n", n=P),
                                   ACT.Copy).then_inc(d_hT, 1)
                    act.activation(hT[0:64, C1 - 1, :], bank(4, 2)[0:64, (C1 - 1) * P:C1 * P], ACT.Copy).then_inc(d_hT, 1)
            each(act, NT, 2, 2, block_act)

        @block.tensor
        def _(pe):
            def turn_rows(norm):
                def one(b, k):
                    pe.wait_ge(ln_rows, norm * B + b + 1)
                    if k >= 2:
                        pe.wait_ge(ln_copied, norm * B + b - 1)
                    for m in range(KD):
                        for j in range(TB):
                            mm = pe.transpose(bank(k % 2)[:, m * S + j * P:m * S + (j + 1) * P],
                                              xn[:, k % 2, j, m * P:(m + 1) * P], ident[:, :])
                    mm.then_inc(ln_turned, 1)
                each(pe, B, 2, 2, one)

            pe.wait_ge(pool_step, 9)
            pe.wait_ge(in_set0, 48)
            for m in range(KD):
                for k in range(KD):
                    pe.matmul(bank(6)[:, m * NK:(m + 1) * NK], wq0[:, k, m * P:(m + 1) * P], descT[:, k, :],
                              start=(k == 0), stop=(k == KD - 1))
            for k in range(KD):
                mm = pe.matmul(bank(6)[0:1, 256:256 + NK], bq0[:, k:k + 1], descT[:, k, :],
                               start=(k == 0), stop=(k == KD - 1))
            mm.then_inc(a_route, 1)
            turn_rows(0)
            pe.wait_ge(a_routed, 2)
            for b in range(B):
                pe.wait_ge(ln_copied, b + 1)
                for t in range(b * TB, (b + 1) * TB):
                    o = bank(2, 2)[:, t * NK:(t + 1) * NK]
                    for k in range(KD):
                        pe.matmul(o, xnT[:, k, t * P:(t + 1) * P], route0[:, k, :], start=(k == 0), stop=False)
                    mm = pe.matmul(o, ones[0:1, :], brow, start=False, stop=True)
                mm.then_inc(a_scored, 1)
            pe.wait_ge(in_kv, 16 * 13)
            for m in range(KD):
                for k in range(KD):
                    mm = pe.matmul(bank(6 + m), wkv[:, k, 0, m * P:(m + 1) * P], ctxT[:, k, :, 0, :],
                                   start=(k == 0), stop=(k == KD - 1))
            mm.then_inc(k_psum, 1)
            pe.wait_ge(k_copied, 4)
            for k in range(KD):
                mm = pe.matmul(bank(4), ones[:, :], ksq[:, k, :], start=(k == 0), stop=(k == KD - 1))
            mm.then_inc(k_sum, 1)
            for b in range(B):
                o = bank(6 + b % 2)[:, 0:D]
                if b >= 2:
                    pe.wait_ge(v_ready, 2 * (b - 1))
                for k in range(KD):
                    pe.matmul(o, ctxT[:, k, b, :, :], wkv[:, k, 1, :], start=(k == 0), stop=False)
                pe.matmul(o, ones[0:1, :], bv_row, start=False, stop=True).then_inc(v_psum, 1)
            pe.wait_ge(k_var, 1)
            for q in range(NT // 4):
                pe.wait_ge(a_wts, 4 * (q + 1))
                if q >= 2:
                    pe.wait_ge(a_wT, q - 1)
                for t in range(4 * q, 4 * q + 4):
                    mm = pe.transpose(bank(4 + q % 2)[0:NK, (t % 4) * P:(t % 4 + 1) * P], ms[:, t, :], ident[:, :])
                mm.then_inc(a_turned, 1)
            pe.wait_ge(in_ctx, 16)
            pe.wait_ge(v_ready, 2 * B)
            for b in range(B):
                pe.wait_ge(a_wT, b // 2 + 1)
                if b >= 2:
                    pe.wait_ge(x_new, TB * (b - 1))
                for j in range(TB):
                    t = b * TB + j
                    mm = pe.matmul(bank(6 + b % 2)[:, j * D:(j + 1) * D], wT[:, t * P:(t + 1) * P], ctx_sb[:, b, :],
                                   start=True, stop=True)
                mm.then_inc(a_mixed, 1)
            turn_rows(1)
            pe.wait_ge(in_rest, 16 * 6)
            for t in range(NT):
                if t % TB == 0:
                    pe.wait_ge(ln_copied, B + t // TB + 1)
                for k in range(KD):
                    mm = pe.matmul(bank(6)[:, t * E0:(t + 1) * E0], xnT[:, k, t * P:(t + 1) * P], rw0[:, k, :],
                                   start=(k == 0), stop=(k == KD - 1))
            mm.then_inc(b_logits, 1)
            pe.wait_ge(in_ffn0, 48)

            def up0(g, c, k):
                i, rows = g * C0 + c, P if c < C0 - 1 else I0
                if k or c >= 2:
                    pe.wait_ge(b_prod, i if c == 0 else i - 1)
                for part in range(2):
                    for h in range(KD):
                        mm = pe.matmul(bank(2 * part + c % 2)[0:rows, :],
                                       gu0[:, h, c * 2 * P + part * rows:c * 2 * P + (part + 1) * rows],
                                       xnT[:, h, bass.ds(g * 512, 512)], start=(h == 0), stop=(h == KD - 1))
                mm.then_inc(b_up, 1)

            def down0(g, c, k):
                i, rows = g * C0 + c, P if c < C0 - 1 else I0
                pe.wait_ge(b_hidden, i + 1)
                if c == 0 and k:
                    pe.wait_ge(x_new, g * 2 + XA)
                for j in range(4):
                    mm = pe.matmul(bank(6, 2)[:, j * D:(j + 1) * D], h0[0:rows, c % 2, j * P:(j + 1) * P],
                                   dn0[0:rows, c, :], start=(c == 0 and j % 2 == 0), stop=(c == C0 - 1),
                                   skip_group_check=True)
                mm.then_inc(b_down, 1)

            def ffn0_group(g, k):
                if k:
                    up0(g, 0, k)
                    down0(g - 1, C0 - 1, k)
                for c in range(C0 - 1):
                    if k or c >= 2:
                        pe.wait_ge(b_hidden, g * C0 + c - 1)
                    pe.matmul(bank(4 + c % 2), spread[:, c * P:(c + 1) * P], cT[:, bass.ds(g * 512, 512)],
                              start=True, stop=True).then_inc(b_spread, 1)
                    up0(g, c + 1, k)
                    down0(g, c, k)

            up0(0, 0, 0)
            pe.wait_ge(b_c3, 3)
            for g in range(NG):
                if g >= 2:
                    pe.wait_ge(b_cT, g - 1)
                for t in range(4 * g, 4 * g + 4):
                    mm = pe.transpose(bank(4 + g % 2).bitcast(BF16)[0:96, (t % 4) * P:(t % 4 + 1) * P],
                                      c3[:, t, :], identb[:, :])
                mm.then_inc(b_turned, 1)
            pe.wait_ge(b_cT, NG)
            pe.wait_ge(b_sig, 1)
            pe.wait_ge(pool_step, 13)
            each(pe, NG, 1, 1, ffn0_group)
            down0(NG - 1, C0 - 1, 1)

            turn_rows(2)

            def queries(b, k):
                pe.wait_ge(ln_copied, 2 * B + b + 1)
                if k >= 2:
                    pe.wait_ge(c_qT, (b - 1) * KD)
                for m in range(KD):
                    for h in range(KD):
                        mm = pe.matmul(bank(2 + k % 2)[:, m * S:(m + 1) * S], wq1[:, h, m * P:(m + 1) * P],
                                       xnT[:, h, bass.ds(b * S, S)], start=(h == 0), stop=(h == KD - 1))
                mm.then_inc(c_q, 1)

            def squares(b, k):
                pe.wait_ge(c_sq, b * KD + KD)
                for j in range(TB):
                    for m in range(KD):
                        mm = pe.matmul(bank(7)[:, bass.ds(b * TB + j, 1)], sqT[:, k % 2, m, j * P:(j + 1) * P],
                                       ones[:, 0:1], start=(m == 0), stop=(m == KD - 1))
                mm.then_inc(c_ssq, 1)

            def queries_squares(b, k):
                queries(b, k)
                if k >= 1:
                    squares(b - 1, k - 1)
            pe.wait_ge(in_rest, 16 * 6)
            each(pe, B, 2, 2, queries_squares)
            squares(B - 1, 1)

            def scores(t, k):
                pe.wait_ge(c_qt, t + 1)
                if k % TB == 0:
                    pe.wait_ge(c_kbd, t + KD)
                if k:
                    pe.wait_ge(c_shift, t)
                for m in range(KD):
                    mm = pe.matmul(bank(m), qt[:, k % 2, m, :], kbd[:, (k // TB) % 2, m * 512:(m + 1) * 512],
                                   start=True, stop=True)
                mm.then_inc(c_scores, 1)

            def turn_probs(t, k):
                pe.wait_ge(c_probs, t + 1)
                if k:
                    pe.wait_ge(c_pT, t)
                for c in range(8):
                    mm = pe.transpose(bank(2, 2)[:, c * P:(c + 1) * P], probs[:, c * P:(c + 1) * P], ident[:, :])
                mm.then_inc(c_turned, 1)

            def values(t, k, b):
                pe.wait_ge(c_pT, t + 1)
                if k:
                    pe.wait_ge(c_att, t)
                for c in range(8):
                    mm = pe.matmul(bank(4)[:, c * 34:(c + 1) * 34], pT[:, k % 2, c, :], vbd[:, b, c, :],
                                   start=True, stop=True)
                mm.then_inc(c_pv, 1)

            def turn_att(t, k):
                pe.wait_ge(c_att, t + 1)
                if k:
                    pe.wait_ge(c_attTc, t)
                for m in range(KD):
                    mm = pe.transpose(bank(5)[:, m * P:(m + 1) * P], att[:, m * P:(m + 1) * P], ident[:, :])
                mm.then_inc(c_attT, 1)

            def project(t, k):
                pe.wait_ge(c_attTc, t + 1)
                if k:
                    pe.wait_ge(x_new, t + XB)
                for m in range(KD):
                    pe.matmul(bank(6)[:, 0:D], attT[:, m, :], wo1[:, m, :], start=(m == 0), stop=False)
                pe.matmul(bank(6)[:, 0:D], ones[0:1, :], bo_row[:, :], start=False, stop=True).then_inc(c_proj, 1)

            def attend(t, k, base=None, at_tile=0):
                b0 = 0 if base is None else base
                if k < NT:
                    scores(t, k)
                if k >= 1:
                    turn_probs(t - 1, k - 1)
                if k >= 2:
                    turn_att(t - 2, k - 2)
                if k >= 1:
                    values(t - 1, k - 1, b0 + (at_tile - 1) // TB)
                if k >= 2:
                    project(t - 2, k - 2)

            for t in range(4):
                attend(t, t, 0, t)
            with pe.Fori(0, B // 2 - 1) as pair:
                for j in range(4):
                    attend(pair * 4 + (4 + j), 4 + j, pair * 2 + 2, j)
            turn_probs(NT - 1, 3)
            turn_att(NT - 2, 2)
            values(NT - 1, 3, B - 1)
            project(NT - 2, 2)
            turn_att(NT - 1, 3)
            project(NT - 1, 3)

            turn_rows(3)
            for t in range(NT):
                if t % TB == 0:
                    pe.wait_ge(ln_copied, 3 * B + t // TB + 1)
                for h in range(KD):
                    mm = pe.matmul(bank(6)[:, t * E1:(t + 1) * E1], xnT[:, h, t * P:(t + 1) * P], wg1[:, h, :],
                                   start=(h == 0), stop=(h == KD - 1))
            mm.then_inc(d_logits, 1)

            def up1(i, k, e, first):
                if not first:
                    pe.wait_ge(d_hidden, i)
                for part in range(2):
                    for half in range(2):
                        for h in range(KD):
                            col = e * WE + h * W13 + part * I1 + half * HALF1
                            mm = pe.matmul(bank(2 * part + half)[:, 0:HALF1], xt1[:, k % 2, h, :],
                                           wexp[:, col:col + HALF1], start=(h == 0), stop=(h == KD - 1))
                mm.then_inc(d_up, 1)

            def turn_hidden(i, first):
                pe.wait_ge(d_hidden, i + 1)
                if not first:
                    pe.wait_ge(d_hT, i * 2)
                for c in range(C1):
                    n = min(P, I1 - c * P)
                    mm = pe.transpose(bank(4, 2)[0:n, c * P:(c + 1) * P], h1[:, c * P:c * P + n], ident[:, :])
                mm.then_inc(d_turned, 1)

            def down1(i, e, early):
                pe.wait_ge(d_hT, i * 2 + 2)
                if not early:
                    pe.wait_ge(d_added, i - 1)
                for c in range(C1):
                    n = min(P, I1 - c * P)
                    col = e * WE + KD * W13 + c * D
                    mm = pe.matmul(bank(6 + e % 2)[:, 0:D], hT[0:n, c, :], wexp[0:n, col:col + D],
                                   start=(c == 0), stop=(c == C1 - 1))
                mm.then_inc(d_down, 1)

            def tile1(t, k):
                pe.wait_ge(d_xt, t + 1)
                for e in range(E1):
                    i = t * E1 + e
                    if k == 0 and e == 7:
                        pe.wait_ge(in_exp7, 16)
                    up1(i, k, e, k == 0 and e == 0)
                    if k or e:
                        down1(i - 1, (e - 1) % E1, k == 0 and e < 3)
                    turn_hidden(i, k == 0 and e == 0)
            pe.wait_ge(in_exp0, 16 * 7)
            pe.wait_ge(d_step, 1)
            each(pe, NT, 2, 2, tile1)
            down1(NT * E1 - 1, E1 - 1, False)

        @block.vector
        def _(dve):
            def stats(norm, b):
                dve.memset(carrier[:, :], 0.0)
                for j in range(TB):
                    dve.bn_stats(st6[:, j, :], x_sb[:, b * TB + j, :]).then_inc(ln_stats, 1)
                dve.wait_ge(ln_stats, (norm * B + b) * TB + TB)
                dve.memset(carrier[:, :], 0.0)
                for j in range(TB):
                    dve.bn_aggr(mv[:, j, :], st6[:, j, :]).then_inc(ln_mv, 1)
                dve.wait_ge(ln_mv, (norm * B + b) * TB + TB)
                dve.tensor_copy(mean[:, bass.ds(b * TB, TB)], mv[:, :, 0])
                dve.tensor_scalar(ve[:, bass.ds(b * TB, TB)], mv[:, :, 1], 1e-5, None,
                                  ALU.add).then_inc(ln_var, 1)

            def rows(norm):
                def one(b, k):
                    dve.wait_ge(ln_rstd, norm * B + b + 1)
                    if k >= 2:
                        dve.wait_ge(ln_turned, norm * B + b - 1)
                    for j in range(TB):
                        t = b * TB + j
                        r = dve.tensor_scalar(xn[:, k % 2, j, :], x_sb[:, t, :], mean[:, bass.ds(t, 1)],
                                              rstd[:, bass.ds(t, 1)], ALU.subtract, ALU.mult)
                    r.then_inc(ln_rows, 1)
                each(dve, B, 2, 2, one)

            dve.memset(t8[:, :, :], NEG).then_inc(dve_const, 1)
            dve.memset(pmask[:, :], 0.0).then_inc(dve_const, 1)
            dve.wait_ge(dve_const, 2)
            dve.memset(pmask[0:NK, 0:1], 1.0).then_inc(dve_const, 1)
            dve.memset(pmask[NK:P, 1:2], 1.0).then_inc(dve_const, 1)
            dve.wait_ge(in_x0, 16)
            with dve.Fori(0, B // 2) as b:
                stats(0, b)
            dve.wait_ge(in_x1, 16)
            with dve.Fori(B // 2, B) as b:
                stats(0, b)
            rows(0)

            dve.wait_ge(in_itok, 16)
            dve.wait_ge(pool_step, 9)
            dve.tensor_copy(hit[:, 0, 0:TB * TOPK_SETS], itok[:, :, :].rearrange("p j k -> p (j k)")).then_inc(s_mask, 1)
            dve.wait_ge(s_mask, 1)
            for j in range(TB):
                dve.tensor_scalar(negmask[:, j, :], iota64[:, :], hit[:, 0, j * TOPK_SETS:j * TOPK_SETS + 1], None,
                                  ALU.is_equal).then_inc(s_mask, 1)
            for n in range(1, TOPK_SETS):
                dve.wait_ge(s_mask, 1 + TB * n)
                for j in range(TB):
                    o = j * TOPK_SETS + n
                    dve.scalar_tensor_tensor(out=negmask[:, j, :], in0=iota64[:, :], scalar=hit[:, 0, o:o + 1],
                                             in1=negmask[:, j, :], op0=ALU.is_equal, op1=ALU.max).then_inc(s_mask, 1)
            dve.wait_ge(s_mask, 1 + TB * TOPK_SETS)
            dve.tensor_scalar(negmask, negmask, 1.0, -NEG, ALU.subtract, ALU.mult).then_inc(s_mask, 1)
            dve.wait_ge(s_mask, 2 + TB * TOPK_SETS)

            def pick(b, k):
                dve.wait_ge(a_scored, 4 * (b // 4 + 1))
                pair = bass.ds(b * TB, TB)
                dve.tensor_tensor(ms[:, pair, :], bank(2, 2).rearrange("p (t n) -> p t n", t=NT)[:, pair, :],
                                  negmask, ALU.add).then_inc(a_masked, 1)
                dve.wait_ge(a_masked, b + 1)
                for j in range(TB):
                    dve.max(m8[:, b * TB + j, :], ms[:, b * TB + j, :]).then_inc(a_max, 1)
                dve.wait_ge(a_max, b * TB + TB)
                dve.tensor_copy(t8[:, pair, 0:2], m8[:, pair, 0:2]).then_inc(a_top, 1)
                dve.tensor_scalar(negm[:, pair], m8[:, pair, 0], -1.0, None, ALU.mult).then_inc(a_top, 1)
                dve.wait_ge(a_top, b * 2 + 2)
                for j in range(TB):
                    dve.match_replace(picked[:, b * TB + j, :], t8[:, b * TB + j, :], ms[:, b * TB + j, :],
                                      FOUND).then_inc(a_picked, 1)
            for b in range(B):
                pick(b, b)

            dve.wait_ge(in_kv, 16 * 13)
            dve.tensor_tensor(gg[:, :], vecs[:, 1, :], vecs[:, 3, :], ALU.mult).then_inc(gg_ready, 1)
            dve.wait_ge(k_sum, 1)
            dve.tensor_scalar(kvar, bank(4), 1.0 / D, 1e-6, ALU.mult, ALU.add).then_inc(k_var, 1)

            def mix_values(b, k):
                dve.wait_ge(v_psum, b + 1)
                o = vbd[:, b, :, :].rearrange("p a (r n) -> p a r n", r=2)
                half = pmask[:, :].unsqueeze(1)
                dve.tensor_tensor(o[:, :, :, 0:HD], bank(6 + k % 2)[:, 0:D].rearrange("p (a r n) -> p a r n", a=8, r=2),
                                  half.unsqueeze(3).broadcast_to([P, 8, 2, HD]), ALU.mult).then_inc(v_ready, 1)
                dve.tensor_copy(o[:, :, :, HD], half.broadcast_to([P, 8, 2])).then_inc(v_ready, 1)
            dve.wait_ge(dve_const, 4)
            each(dve, B, 0, 2, mix_values)
            dve.wait_ge(k_pow, 1)
            dve.wait_ge(k_copied, 4)
            dve.wait_ge(gg_ready, 1)
            for m in range(KD):
                dve.scalar_tensor_tensor(out=kT[:, m, :], in0=kT[:, m, :], scalar=gg[:, m:m + 1], in1=krst,
                                         op0=ALU.mult, op1=ALU.mult).then_inc(k_scaled, 1)

            with dve.Fori(0, NT) as t:
                dve.wait_ge(a_exp, t + 1)
                dve.wait_ge(a_picked, t + 1)
                dve.scalar_tensor_tensor(out=ms[:, t, :], in0=picked[:, t, :], scalar=1.0e38, in1=ex[:, t, :],
                                         op0=ALU.is_gt, op1=ALU.mult, accum_out=sums[:, bass.ds(t, 1)]).then_inc(a_wts, 1)
            dve.wait_ge(a_wts, NT)
            dve.reciprocal(recs[:, :], sums[:, :]).then_inc(a_rec, 1)
            dve.wait_ge(a_rec, 1)

            def mix_sets(b, k):
                dve.wait_ge(a_mixed, b + 1)
                for j in range(TB):
                    t = b * TB + j
                    dve.scalar_tensor_tensor(out=x_sb[:, t, :], in0=bank(6 + k % 2)[:, j * D:(j + 1) * D],
                                             scalar=recs[:, bass.ds(t, 1)], in1=x_sb[:, t, :],
                                             op0=ALU.mult, op1=ALU.add).then_inc(x_new, 1)
                dve.wait_ge(x_new, b * TB + TB)
                stats(1, b)
            each(dve, B, 0, 2, mix_sets)

            rows(1)
            dve.wait_ge(ln_turned, 2 * B)
            dve.wait_ge(in_rest, 16 * 6)
            dve.memset(sel0[:, :, E0:E0 + 4], NEG).then_inc(b_step, 1)
            dve.memset(arena[:, 1024:1792], 0.0).then_inc(b_step, 1)
            dve.wait_ge(b_sig, 1)
            dve.tensor_tensor(sel0[:, :, 0:E0], sc0, ebias[:, :].unsqueeze(1).broadcast_to([P, NT, E0]),
                              ALU.add).then_inc(b_step, 1)
            dve.wait_ge(b_step, 3)
            for t in range(NT):
                dve.max(m8[:, t, :], sel0[:, t, :]).then_inc(b_max, 1)
            dve.wait_ge(b_max, NT)
            dve.tensor_copy(t8[:, :, 0:4], m8[:, :, 0:4]).then_inc(b_step, 1)
            dve.wait_ge(b_step, 4)
            for t in range(NT):
                dve.match_replace(rep0[:, t, :], t8[:, t, :], sel0[:, t, :], FOUND).then_inc(b_max, 1)
            dve.wait_ge(b_max, 2 * NT)
            dve.scalar_tensor_tensor(out=cw0, in0=rep0[:, :, 0:E0], scalar=1.0e38, in1=sc0,
                                     op0=ALU.is_gt, op1=ALU.mult).then_inc(b_step, 1)
            dve.wait_ge(b_step, 5)
            dve.tensor_reduce(sums[:, :], cw0, AX.X, ALU.add).then_inc(b_step, 1)
            dve.wait_ge(b_step, 6)
            dve.tensor_scalar(sums[:, :], sums[:, :], 1e-20, None, ALU.add).then_inc(b_step, 1)
            dve.wait_ge(b_step, 7)
            dve.reciprocal(recs[:, :], sums[:, :]).then_inc(b_step, 1)
            dve.wait_ge(b_step, 8)
            dve.tensor_tensor(cw0, cw0, recs[:, :].unsqueeze(2).broadcast_to([P, NT, E0]), ALU.mult).then_inc(b_step, 1)
            dve.wait_ge(b_step, 9)
            dve.tensor_copy(c3[:, :, 0:E0], cw0).then_inc(b_c3, 1)
            dve.wait_ge(b_c3, 1)
            dve.tensor_tensor(res0, cw0, c3[:, :, 0:E0], ALU.subtract).then_inc(b_step, 1)
            dve.wait_ge(b_step, 10)
            dve.tensor_copy(c3[:, :, 32:32 + E0], res0).then_inc(b_c3, 1)
            dve.wait_ge(b_c3, 2)
            dve.tensor_tensor(c3[:, :, 64:64 + E0], res0, c3[:, :, 32:32 + E0], ALU.subtract).then_inc(b_c3, 1)

            def ffn0_group(g, k):
                for c in range(C0):
                    i, rows_ = g * C0 + c, P if c < C0 - 1 else I0
                    dve.wait_ge(b_silu, i + 1)
                    dve.tensor_tensor(hm0[0:rows_, c % 2, :], sg0[0:rows_, c % 2, :], bank(2 + c % 2)[0:rows_, :],
                                      ALU.mult).then_inc(b_prod, 1)
                    if k or c >= 2:
                        dve.wait_ge(b_down, i if c == 0 else i - 1)
                    dve.wait_ge(b_prod, i + 1)
                    if c < C0 - 1:
                        dve.wait_ge(b_spread, g * (C0 - 1) + c + 1)
                        dve.tensor_tensor(h0[:, c % 2, :], hm0[:, c % 2, :], bank(4 + c % 2), ALU.mult).then_inc(b_hidden, 1)
                    else:
                        dve.tensor_copy(h0[0:rows_, c % 2, :], hm0[0:rows_, c % 2, :]).then_inc(b_hidden, 1)

            def add_ffn0(g):
                dve.wait_ge(b_down, g * C0 + C0)
                for j in range(2):
                    t = g * 4 + j * 2
                    o = x_sb[:, bass.ds(t, 2), :].rearrange("p t d -> p (t d)")
                    dve.tensor_tensor(o, o, bank(6 + j), ALU.add).then_inc(x_new, 1)
                dve.wait_ge(x_new, g * 2 + XA + 2)
                for j in range(2):
                    stats(2, g * 2 + j)

            def group_and_sums(g, k):
                ffn0_group(g, k)
                add_ffn0(g)
            each(dve, NG, 1, 1, group_and_sums)

            rows(2)
            dve.wait_ge(c_ssq, B)
            dve.tensor_scalar(ssq[:, :], bank(7)[:, 0:NT], HD / D, HD * 1e-6, ALU.mult, ALU.add).then_inc(c_var, 1)

            def centre(t, k):
                dve.wait_ge(c_scores, t + 1)
                s = bank(0, 2).rearrange("p (h n) -> p h n", h=H)
                dve.tensor_reduce(mx1[:, :], s, AX.X, ALU.max).then_inc(c_max, 1)
                dve.wait_ge(c_max, t + 1)
                if k:
                    dve.wait_ge(c_probs, t)
                dve.tensor_tensor(shift.rearrange("p (h n) -> p h n", h=H), s,
                                  mx1[:, :].unsqueeze(2).broadcast_to([P, H, NK]), ALU.subtract).then_inc(c_shift, 1)

            def divide(t, k):
                dve.wait_ge(c_pv, t + 1)
                v = bank(4)[:, 0:H * (HD + 1)].rearrange("p (h n) -> p h n", h=H)
                dve.reciprocal(rec1[:, :], v[:, :, HD]).then_inc(c_rec, 1)
                dve.wait_ge(c_rec, t + 1)
                if k:
                    dve.wait_ge(c_attT, t)
                dve.tensor_tensor(att.rearrange("p (h n) -> p h n", h=H), v[:, :, 0:HD],
                                  rec1[:, :].unsqueeze(2).broadcast_to([P, H, HD]), ALU.mult).then_inc(c_att, 1)

            def add_att(t, k):
                dve.wait_ge(c_proj, t + 1)
                dve.tensor_tensor(x_sb[:, t, :], x_sb[:, t, :], bank(6)[:, 0:D], ALU.add).then_inc(x_new, 1)

            def attend(t, k, b0, j):
                centre(t, k)
                if k >= 1:
                    divide(t - 1, k - 1)
                if k >= 2:
                    add_att(t - 2, k - 2)
                    if k % TB == 1:
                        dve.wait_ge(x_new, t - 2 + XB + 1)
                        stats(3, b0 + (j - 2) // TB)
            for t in range(4):
                attend(t, t, 0, t)
            with dve.Fori(0, B // 2 - 1) as pair:
                for j in range(4):
                    attend(pair * 4 + (4 + j), 4 + j, pair * 2 + 2, j)
            divide(NT - 1, 3)
            add_att(NT - 2, 2)
            add_att(NT - 1, 3)
            dve.wait_ge(x_new, XC)
            stats(3, B - 1)

            rows(3)
            done = [0]

            def step(instruction):
                instruction.then_inc(d_step, 1)
                done[0] += 1
                dve.wait_ge(d_step, done[0])

            def over_experts(a):
                return a.unsqueeze(2).broadcast_to([P, NT, E1])

            dve.wait_ge(d_logits, 1)
            logits = bank(6)[:, 0:NT * E1].rearrange("p (t e) -> p t e", t=NT)
            step(dve.tensor_scalar(li, logits, float(Q_IN), ROUND, ALU.mult, ALU.add))
            step(dve.tensor_scalar(li, li, ROUND, None, ALU.subtract))
            step(dve.tensor_reduce(m1[:, :], li, AX.X, ALU.max))
            step(dve.tensor_tensor(sh, li, over_experts(m1[:, :]), ALU.subtract))
            step(dve.tensor_scalar(sh, sh, -float(Q_IN), None, ALU.max))
            step(dve.scalar_tensor_tensor(out=key, in0=sh, scalar=float(E1),
                                          in1=iota64[:, 0:E1].unsqueeze(1).broadcast_to([P, NT, E1]),
                                          op0=ALU.mult, op1=ALU.subtract))
            for t in range(NT):
                dve.max(m8[:, t, :], key[:, t, :]).then_inc(d_max, 1)
            dve.wait_ge(d_max, NT)
            step(dve.tensor_tensor(li, key, over_experts(m8[:, :, 1]), ALU.is_ge))
            step(dve.tensor_scalar(zz, sh, 1.0 / Q_IN, None, ALU.mult))
            coef = exp_coefficients()
            step(dve.tensor_scalar(po, zz, coef[-1], None, ALU.mult))
            for c in coef[-2:0:-1]:
                step(dve.scalar_tensor_tensor(out=po, in0=po, scalar=c, in1=zz, op0=ALU.add, op1=ALU.mult))
            step(dve.tensor_scalar(po, po, Q_OUT, Q_OUT - 0.5, ALU.mult, ALU.add))
            step(dve.tensor_scalar(po, po, ROUND, None, ALU.add))
            step(dve.tensor_scalar(po, po, ROUND, None, ALU.subtract))
            step(dve.tensor_tensor(po, po, li, ALU.mult))
            step(dve.tensor_reduce(m1[:, :], po, AX.X, ALU.add))
            step(dve.reciprocal(m1[:, :], m1[:, :]))
            step(dve.tensor_tensor(comb1[:, :, :], po, over_experts(m1[:, :]), ALU.mult))

            def add_expert(i, t, e, first):
                dve.wait_ge(d_down, i + 1)
                if not first:
                    dve.wait_ge(d_added, i)
                dve.scalar_tensor_tensor(out=x_sb[:, t, :], in0=bank(6 + e % 2)[:, 0:D],
                                         scalar=comb1[:, t, e:e + 1], in1=x_sb[:, t, :],
                                         op0=ALU.mult, op1=ALU.add).then_inc(d_added, 1)

            def tile1(t, k):
                for e in range(E1):
                    i = t * E1 + e
                    dve.wait_ge(d_silu, i + 1)
                    if k or e:
                        dve.wait_ge(d_turned, i)
                    dve.tensor_tensor(h1.rearrange("p (a n) -> p a n", a=2),
                                      sg1.rearrange("p (a n) -> p a n", a=2),
                                      bank(2, 2).rearrange("p (a n) -> p a n", a=2)[:, :, 0:HALF1],
                                      ALU.mult).then_inc(d_hidden, 1)
                    if k or e:
                        add_expert(i - 1, t if e else t - 1, (e - 1) % E1, k == 0 and e == 1)
            each(dve, NT, 2, 2, tile1)
            add_expert(NT * E1 - 1, NT - 1, E1 - 1, False)


def kernel(**inputs):
    import concourse.bacc as _bacc
    from concourse.bass_utils import run_bass_kernel_spmd as _run

    g = {name: np.asarray(a) for name, a in inputs.items()}
    gu, dn = g["L0_ffn_gate_up_proj"], g["L0_ffn_down_proj"]
    chunks = E0 * I0 // P
    gate = gu[:, 0:I0, :].reshape(chunks, P, D)
    up = gu[:, I0:2 * I0, :].reshape(chunks, P, D)
    gu0 = np.concatenate([np.stack([gate, up], 1).reshape(2 * E0 * I0, D),
                          g["L0_ffn_shared_gate_w"], g["L0_ffn_shared_up_w"]], 0).T
    dn0 = np.zeros((P, C0, D), dn.dtype)
    dn0[:, 0:chunks] = dn.transpose(0, 2, 1).reshape(chunks, P, D).transpose(1, 0, 2)
    dn0[0:I0, chunks] = g["L0_ffn_shared_down_w"].T
    w1, w2, w3 = g["L1_ffn_w1"], g["L1_ffn_w2"], g["L1_ffn_w3"]
    wexp = np.zeros((P, E1, WE), w1.dtype)
    for e in range(E1):
        for k in range(KD):
            wexp[:, e, k * W13:k * W13 + I1] = w1[e].T[k * P:(k + 1) * P]
            wexp[:, e, k * W13 + I1:(k + 1) * W13] = w3[e].T[k * P:(k + 1) * P]
        for c in range(C1):
            n = min(P, I1 - c * P)
            wexp[0:n, e, KD * W13 + c * D:KD * W13 + (c + 1) * D] = w2[e].T[c * P:c * P + n]
    def columns(vector):
        return vector.reshape(KD, P).T

    arrays = {
        "x": g["x"], "ctx": g["ctx_2048"], "ctxT": g["ctx_2048"].reshape(B * NK, D).T,
        "itok": g["itok_Sx4_0_63"], "descT": g["L0_xattn_desc_router"].T, "wq0": g["L0_xattn_W_q"],
        "bq0": columns(g["L0_xattn_b_q"]), "rw0": g["L0_ffn_router_w"].T, "ebias": g["L0_ffn_e_bias"],
        "gu0": gu0, "dn0": dn0, "wq1": g["L1_xattn_Wq"], "bq1": columns(g["L1_xattn_bq"]),
        "gq1": columns(g["L1_xattn_gq"]), "wk1": g["L1_xattn_Wk_img"], "bk1": columns(g["L1_xattn_bk_img"]),
        "gk1": columns(g["L1_xattn_gk_img"]), "wv1": g["L1_xattn_Wv_img"], "bv1": g["L1_xattn_bv_img"],
        "wo1": g["L1_xattn_Wo"], "bo1": g["L1_xattn_bo"], "wg1": g["L1_ffn_w_gate"].T, "wexp": wexp,
    }
    nc = _bacc.Bacc("TRN2", target_bir_lowering=False, num_devices=1)
    feed, args = {}, []
    for name, a in arrays.items():
        a = np.ascontiguousarray(a)
        feed[f"in_{name}"] = a
        args.append(nc.dram_tensor(f"in_{name}", a.shape, mybir.dt.from_np(a.dtype), kind="ExternalInput").ap())
    args.append(nc.dram_tensor("out_x", (B, S, D), F32, kind="ExternalOutput").ap())
    program(nc, *args)
    return _run(nc, [feed], core_ids=[0]).results[0]["out_x"]
```

```python
import math
from contextlib import ExitStack

import numpy as np

import concourse.bass as bass
from concourse import mybir

F32 = mybir.dt.float32
BF16 = mybir.dt.bfloat16
I32 = mybir.dt.int32
ALU = mybir.AluOpType
ACT = mybir.ActivationFunctionType
AX = mybir.AxisListType

P = 128
B, S, D = 8, 256, 256
KD = D // P
NT = B * S // P
TB = S // P
NK = 64
TOPK_SETS = 4
E0, I0 = 16, 96
C0 = E0 * I0 // P + 1
E1, I1 = 8, 704
C1 = -(-I1 // P)
H, HD = 16, 16
NEG = -3.0e38
FOUND = 3.0e38
ROUND = 12582912.0
Q_IN = 128
Q_OUT = 65536.0
HALF1 = I1 // 2
W13 = 2 * I1
WE = KD * W13 + C1 * D
TOP1 = 2
NBLK = (TOP1 * NT * P - E1) // P + E1
XW = D + 4


def exp_coefficients(degree=8):
    z = np.linspace(-1, 0, 4001)
    c = np.polynomial.chebyshev.Chebyshev.fit(z, np.exp(z), degree, domain=[-1, 0])
    return [float(v) for v in c.convert(kind=np.polynomial.Polynomial).coef]


def program(nc, x_in, ctx_in, ctxT_in, itok_in, descT_in, wq0_in, bq0_in, rw0_in, ebias_in,
            gu0_in, dn0_in, wq1_in, bq1_in, gq1_in, wk1_in, bk1_in, gk1_in, wv1_in, bv1_in,
            wo1_in, bo1_in, wg1_in, wexp_in, out_rows):
    with ExitStack() as st:
        def sb(name, shape, dt=F32):
            return st.enter_context(nc.sbuf_tensor(name, shape, dt))

        def sem(name):
            return st.enter_context(nc.semaphore(name))

        x_sb = sb("x_sb", [P, NT, D])
        xmem = sb("xmem", [P, NT * XW])
        wexp = sb("wexp", [P, E1 * WE])
        arena = sb("arena", [P, 4224])

        def view(tensor, first, *shape):
            v = tensor[:, first:first + int(np.prod(shape))]
            names = "abcd"[:len(shape)]
            if len(shape) > 1:
                v = v.rearrange(f"p ({' '.join(names)}) -> p {' '.join(names)}",
                                **dict(zip(names[:-1], shape)))
            return v

        xnT = view(xmem, 0, KD, NT * P)
        xr = view(xmem, 0, NT, XW)

        ctxT = view(wexp, 0, KD, B, 2, NK)
        wkv = view(wexp, 2048, KD, 2, D)
        ksq = view(wexp, 3072, KD, B * NK)
        kvar = view(wexp, 4096, B * NK // P)
        krst = view(wexp, 4100, B * NK // P)
        kdiag = view(wexp, 4608, B * NK // P, P)
        bv_row = wexp[0:1, 5120:5120 + D]
        ms = view(wexp, 5632, NT, NK)
        picked = view(wexp, 6656, NT, NK)
        ex = view(wexp, 7680, NT, NK)
        wT = wexp[0:NK, 8704:8704 + NT * P]
        ctx_sb = wexp[0:NK, 10752:10752 + B * D].rearrange("p (b d) -> p b d", b=B)
        wq0 = view(wexp, 12800, KD, D)
        descT = view(wexp, 13312, KD, NK)
        route0 = view(wexp, 13440, KD, NK)
        negmask = view(wexp, 13568, TB, NK)
        hit = view(wexp, 13696, TB, NK)
        brow = wexp[0:1, 13824:13824 + NK]
        late = 5 * WE
        GU0 = 2 * E0 * I0 + 2 * I0
        gu0 = view(wexp, late, KD, GU0)
        dn0 = view(wexp, late + KD * GU0, C0, D)
        sg0 = view(wexp, late + KD * GU0 + C0 * D, 2, 512)
        hm0 = view(wexp, late + KD * GU0 + C0 * D + 1024, 2, 512)
        h0 = view(wexp, late + KD * GU0 + C0 * D + 2048, 2, 512)
        last = 7 * WE
        kbd = view(wexp, last, 2, 1024)
        pT = view(wexp, last + 2048, 2, 8, P)
        xn = view(arena, 0, 2, TB, D)
        cT = arena[0:96, 0:1024].bitcast(BF16)
        c3 = arena[:, 1024:1792].bitcast(BF16).rearrange("p (t c) -> p t c", t=NT)
        spread = arena[0:96, 1792:2560].bitcast(BF16)
        sc0 = view(arena, 2560, NT, E0)
        sel0 = view(arena, 2816, NT, E0 + 4)
        rep0 = view(arena, 3136, NT, E0 + 4)
        cw0 = view(arena, 3456, NT, E0)
        res0 = view(arena, 3712, NT, E0)
        shift = view(arena, 0, H * NK)
        probs = view(arena, 1024, H * NK)
        sqT = view(arena, 2048, 2, KD, S)
        qt = view(arena, 3072, 2, KD, P)
        att = view(arena, 3584, D)
        attT = view(arena, 3840, KD, P)
        filler = view(arena, 1024, XW)
        li = view(arena, 1024, NT, E1)
        sh = view(arena, 1152, NT, E1)
        key = view(arena, 1280, NT, E1)
        zz = view(arena, 1408, NT, E1)
        po = view(arena, 1536, NT, E1)
        keep = view(arena, 1664, NT, E1)
        slot = view(arena, 1792, NT, E1)
        cum = view(arena, 1920, 2, NT, E1)
        xt1 = view(arena, 0, 2, KD, P)
        sg1 = view(arena, 512, I1)
        h1 = view(arena, 1216, I1)
        hT = view(arena, 2176, C1, P)
        xg = view(arena, 2944, 2, XW)
        yb = view(arena, 3464, 2, D)
        ident = sb("ident", [P, P])
        identb = sb("identb", [P, P], BF16)
        ones = sb("ones", [P, P])
        st6 = sb("st6", [P, TB, 6])
        mv = sb("mv", [P, TB, 2])
        mean = sb("mean", [P, NT])
        carrier = sb("carrier", [P, 1])
        ve = sb("ve", [P, NT])
        rstd = sb("rstd", [P, NT])
        mhalf = sb("mhalf", [P, 1])
        m8 = sb("m8", [P, NT, 8])
        t8 = sb("t8", [P, NT, 8])
        negm = sb("negm", [P, NT])
        sums = sb("sums", [P, NT])
        recs = sb("recs", [P, NT])
        iota64 = sb("iota64", [P, NK])
        itok = sb("itok", [P, TB, TOPK_SETS], I32)
        bq0 = sb("bq0", [P, KD])
        rw0 = sb("rw0", [P, KD, E0])
        ebias = sb("ebias", [P, E0])
        wq1 = sb("wq1", [P, KD, D])
        wo1 = sb("wo1", [P, KD, D])
        bo_row = sb("bo_row", [1, D])
        vecs = sb("vecs", [P, 4, KD])
        gg = sb("gg", [P, KD])
        wg1 = sb("wg1", [P, KD, E1])
        kT = sb("kT", [P, KD, B * NK])
        vbd = sb("vbd", [P, B, H // 2, 2 * (HD + 1)])
        hmask = sb("hmask", [P, H // 2])
        pmask = sb("pmask", [P, 2])
        mx1 = sb("mx1", [P, H])
        rec1 = sb("rec1", [P, H])
        ssq = sb("ssq", [P, NT])
        rq = sb("rq", [P, NT])
        nmr = sb("nmr", [P, NT])
        small8 = sb("small8", [P, 3, E1])
        slot_i = sb("slot_i", [P, 2, NT], I32)
        upper = sb("upper", [P, P])
        slotno = sb("slotno", [P, NBLK])
        blkno = sb("blkno", [P, NBLK])
        blk = sb("blk", [P, NBLK])
        blk_i = sb("blk_i", [P, NBLK], I32)
        wb = sb("wb", [P, 2])
        row_i = sb("row_i", [P, 2], I32)
        m1 = sb("m1", [P, NT])

        ps = st.enter_context(nc.psum_tensor("ps", [P, 8 * 512], F32))

        def bank(i, n=1):
            return ps[:, 512 * i:512 * (i + n)]

        a_exp, a_masked, a_max, a_mixed = sem("a_exp"), sem("a_masked"), sem("a_max"), sem("a_mixed")
        a_picked, a_rec, a_route, a_routed = sem("a_picked"), sem("a_rec"), sem("a_route"), sem("a_routed")
        a_scored, a_top, a_turned, a_wT = sem("a_scored"), sem("a_top"), sem("a_turned"), sem("a_wT")
        a_wts = sem("a_wts")
        b_c3, b_cT, b_down, b_hidden = sem("b_c3"), sem("b_cT"), sem("b_down"), sem("b_hidden")
        b_logits, b_max, b_prod, b_sig = sem("b_logits"), sem("b_max"), sem("b_prod"), sem("b_sig")
        b_silu, b_spread, b_step, b_turned = sem("b_silu"), sem("b_spread"), sem("b_step"), sem("b_turned")
        b_up = sem("b_up")
        blk_ready, counted, fill_done, gg_ready = sem("blk_ready"), sem("counted"), sem("fill_done"), sem("gg_ready")
        kept, logits_done, res_done, rest_done = sem("kept"), sem("logits_done"), sem("res_done"), sem("rest_done")
        scattered, slot_ready = sem("scattered"), sem("slot_ready")
        c_att, c_attT, c_attTc, c_kbd = sem("c_att"), sem("c_attT"), sem("c_attTc"), sem("c_kbd")
        c_max, c_pT, c_probs, c_proj = sem("c_max"), sem("c_pT"), sem("c_probs"), sem("c_proj")
        c_pv, c_q, c_qT, c_qt = sem("c_pv"), sem("c_q"), sem("c_qT"), sem("c_qt")
        c_rec, c_rq, c_scores, c_shift = sem("c_rec"), sem("c_rq"), sem("c_scores"), sem("c_shift")
        c_sq, c_ssq, c_turned, c_var = sem("c_sq"), sem("c_ssq"), sem("c_turned"), sem("c_var")
        d_added, d_down, d_hT, d_hidden = sem("d_added"), sem("d_down"), sem("d_hT"), sem("d_hidden")
        d_logits, d_max, d_silu, d_step = sem("d_logits"), sem("d_max"), sem("d_silu"), sem("d_step")
        d_turned, d_up, d_weight, d_wstep = sem("d_turned"), sem("d_up"), sem("d_weight"), sem("d_wstep")
        d_xt, d_xturned, d_y = sem("d_xt"), sem("d_xturned"), sem("d_y")
        dve_const = sem("dve_const")
        in_ctx, in_exp0, in_exp7, in_ffn0 = sem("in_ctx"), sem("in_exp0"), sem("in_exp7"), sem("in_ffn0")
        in_itok, in_kv, in_rest, in_set0 = sem("in_itok"), sem("in_kv"), sem("in_rest"), sem("in_set0")
        in_x0, in_x1 = sem("in_x0"), sem("in_x1")
        k_copied, k_diag, k_pow, k_psum = sem("k_copied"), sem("k_diag"), sem("k_pow"), sem("k_psum")
        k_scaled, k_spread, k_sum, k_var = sem("k_scaled"), sem("k_spread"), sem("k_sum"), sem("k_var")
        ln_copied, ln_mv, ln_rows, ln_rstd = sem("ln_copied"), sem("ln_mv"), sem("ln_rows"), sem("ln_rstd")
        ln_stats, ln_turned, ln_var = sem("ln_stats"), sem("ln_turned"), sem("ln_var")
        pool_fill, pool_slot, pool_step = sem("pool_fill"), sem("pool_slot"), sem("pool_step")
        s_mask = sem("s_mask")
        v_psum, v_ready = sem("v_psum"), sem("v_ready")
        x_new = sem("x_new")
        xr_extra, xr_id, xr_rows, xr_shift = sem("xr_extra"), sem("xr_id"), sem("xr_rows"), sem("xr_shift")

        slots_x = nc.dram_tensor("slots_x", (NBLK, P, XW), F32, kind="Internal").ap()
        xg_in = [sem("xg_in0"), sem("xg_in1")]
        XA, XB, XC = NT, NT + NT // 2, 2 * NT + NT // 2
        NG = NT // 4

        def each(eng, n, lead, step, body):
            for i in range(lead):
                body(i, i)
            with eng.Fori(0, (n - lead) // step) as turn:
                for j in range(step):
                    body(turn * step + (lead + j), lead + j)

        block = st.enter_context(nc.Block())

        @block.sync
        def _(sp):
            x_v = x_in.rearrange("b (j p) d -> p (b j) d", p=P)
            half = NT // 2
            rows_v = out_rows.rearrange("(t p) d -> p t d", p=P)
            sp.dma_start(x_sb[:, 0:half, :], x_v[:, 0:half, :]).then_inc(in_x0, 16)
            sp.dma_start(x_sb[:, half:NT, :], x_v[:, half:NT, :]).then_inc(in_x1, 16)
            sp.dma_start(wq0, wq0_in.rearrange("(k p) n -> p k n", p=P)).then_inc(in_set0, 16)
            sp.dma_start(descT, descT_in.rearrange("(k p) n -> p k n", p=P)).then_inc(in_set0, 16)
            sp.dma_start(bq0[:, :], bq0_in).then_inc(in_set0, 16)
            sp.dma_start(itok[:, :, :], itok_in.rearrange("(j p) k -> p j k", p=P)).then_inc(in_itok, 16)
            sp.dma_start(ctx_sb, ctx_in.rearrange("b n d -> n b d")).then_inc(in_ctx, 16)
            for k in range(KD):
                for m, src in enumerate((wk1_in, wv1_in)):
                    sp.dma_start(wkv[:, k, m, :], src[k * P:(k + 1) * P, :]).then_inc(in_kv, 16)
                for r in range(2):
                    sp.dma_start(ctxT[:, k, :, r, :], ctxT_in[k * P:(k + 1) * P, :].rearrange(
                        "p (b n) -> p b n", b=B)).then_inc(in_kv, 16)
            for m, src in enumerate((bq1_in, gq1_in, bk1_in, gk1_in)):
                sp.dma_start(vecs[:, m, :], src).then_inc(in_kv, 16)
            sp.dma_start(bv_row, bv1_in.unsqueeze(0)).then_inc(in_kv, 16)
            sp.dma_start(rw0[:, :, :], rw0_in.rearrange("(k p) n -> p k n", p=P)).then_inc(in_rest, 16)
            sp.dma_start(ebias[:, :], ebias_in.partition_broadcast(P)).then_inc(in_rest, 16)
            for k in range(KD):
                sp.dma_start(gu0[:, k, :], gu0_in[k * P:(k + 1) * P, :]).then_inc(in_ffn0, 16)
            sp.dma_start(dn0, dn0_in).then_inc(in_ffn0, 16)
            sp.dma_start(bo_row[:, :], bo1_in.unsqueeze(0)).then_inc(in_rest, 16)
            sp.dma_start(wq1[:, :, :], wq1_in.rearrange("(k p) n -> p k n", p=P)).then_inc(in_rest, 16)
            sp.dma_start(wo1[:, :, :], wo1_in.rearrange("(k p) n -> p k n", p=P)).then_inc(in_rest, 16)
            sp.dma_start(wg1[:, :, :], wg1_in.rearrange("(k p) n -> p k n", p=P)).then_inc(in_rest, 16)
            sp.wait_ge(pool_fill, 2)
            sp.dma_start(slots_x.rearrange("b p n -> p b n"),
                         filler.unsqueeze(1).broadcast_to([P, NBLK, XW])).then_inc(fill_done, 16)
            sp.dma_start(rows_v[:, NT, :], filler[:, 0:D]).then_inc(rest_done, 16)
            sp.wait_ge(x_new, XA)
            sp.wait_ge(v_ready, 2 * B)
            for e in range(5):
                sp.dma_start(wexp[:, e * WE:(e + 1) * WE], wexp_in[:, e, :]).then_inc(in_exp0, 16)
            sp.wait_ge(b_down, 4 * C0)
            for e in range(5, 7):
                sp.dma_start(wexp[:, e * WE:(e + 1) * WE], wexp_in[:, e, :]).then_inc(in_exp0, 16)
            sp.wait_ge(x_new, XC)
            sp.dma_start(wexp[:, last:last + WE], wexp_in[:, 7, :]).then_inc(in_exp7, 16)
            sp.dma_start(rows_v[:, 0:NT, :], x_sb[:, :, :]).then_inc(res_done, 16)

            def load_slots(i, k):
                if k >= 2:
                    sp.wait_ge(d_weight, (i - 1) * 2)
                    sp.wait_ge(d_xturned, i - 1)
                sp.dma_start(xg[:, k % 2, :], slots_x[i, :, :]).then_inc(xg_in[k % 2], 16)
            sp.wait_ge(scattered, 16 * 2 * NT)
            each(sp, NBLK - 1, 2, 2, load_slots)
            load_slots(NBLK - 1, 2)
            sp.wait_ge(rest_done, 16)
            sp.wait_ge(fill_done, 16)
            sp.wait_ge(res_done, 16)
            sp.wait_ge(d_added, 16 * NBLK)

        @block.gpsimd
        def _(pool):
            pool.memset(ident[:, :], 0.0).then_inc(pool_step, 1)
            pool.memset(ones[:, :], 1.0).then_inc(pool_step, 1)
            pool.memset(hmask[:, :], 1.0).then_inc(pool_step, 1)
            pool.memset(mhalf[:, :], -0.5).then_inc(pool_step, 1)
            pool.iota(iota64[:, :], [[1, NK]], base=0, channel_multiplier=0,
                      allow_small_or_imprecise_dtypes=True).then_inc(pool_step, 1)
            pool.wait_ge(pool_step, 5)
            pool.affine_select(out=ident[:, :], in_=ident[:, :], compare_op=ALU.not_equal, fill=1.0,
                               base=0, pattern=[[-1, P]], channel_multiplier=1).then_inc(pool_step, 1)
            pool.affine_select(out=hmask[:, :], in_=hmask[:, :], compare_op=ALU.is_ge, fill=0.0,
                               base=0, pattern=[[-HD, H // 2]], channel_multiplier=1).then_inc(pool_step, 1)
            pool.wait_ge(pool_step, 7)
            pool.affine_select(out=hmask[:, :], in_=hmask[:, :], compare_op=ALU.is_ge, fill=0.0,
                               base=HD - 1, pattern=[[HD, H // 2]], channel_multiplier=-1).then_inc(pool_step, 1)
            pool.tensor_copy(identb[:, :], ident[:, :]).then_inc(pool_step, 1)
            pool.memset(filler, 0.0).then_inc(pool_fill, 1)
            pool.wait_ge(pool_fill, 1)
            pool.iota(filler[:, D:D + 1].bitcast(I32), [[0, 1]], base=NT * P, channel_multiplier=1).then_inc(pool_fill, 1)
            pool.memset(upper[:, :], 1.0).then_inc(pool_slot, 1)
            pool.iota(slotno[:, :], [[P, NBLK]], base=0, channel_multiplier=1,
                      allow_small_or_imprecise_dtypes=True).then_inc(pool_slot, 1)
            pool.iota(blkno[:, :], [[1, NBLK]], base=0, channel_multiplier=0,
                      allow_small_or_imprecise_dtypes=True).then_inc(pool_slot, 1)
            pool.wait_ge(pool_slot, 1)
            pool.affine_select(out=upper[:, :], in_=upper[:, :], compare_op=ALU.is_ge, fill=0.0,
                               base=-1, pattern=[[1, P]], channel_multiplier=-1).then_inc(pool_slot, 1)

            def power(norm):
                def one(b, k):
                    pool.wait_ge(ln_var, norm * B + b + 1)
                    pool.tensor_tensor(rstd[:, bass.ds(b * TB, TB)], ve[:, bass.ds(b * TB, TB)],
                                       mhalf[:, 0:1].broadcast_to([P, TB]), ALU.pow).then_inc(ln_rstd, 1)
                each(pool, B, 0, 2, one)

            pool.wait_ge(pool_step, 9)
            power(0)
            pool.wait_ge(k_var, 1)
            pool.tensor_tensor(krst, kvar, mhalf[:, 0:1].broadcast_to([P, B * NK // P]), ALU.pow).then_inc(k_pow, 1)
            power(1)
            pool.memset(spread, 0.0).then_inc(pool_step, 1)
            v = spread.rearrange("p (e u) -> p e u", e=E0)
            for part in range(3):
                pool.wait_ge(pool_step, 10 + part)
                pool.affine_select(out=v, in_=v, compare_op=ALU.not_equal, fill=1.0, base=-32 * part,
                                   pattern=[[-1, E0], [0, I0]], channel_multiplier=1).then_inc(pool_step, 1)
            power(2)
            pool.wait_ge(c_var, 1)
            pool.tensor_tensor(rq[:, :], ssq[:, :], mhalf[:, 0:1].broadcast_to([P, NT]), ALU.pow).then_inc(c_rq, 1)

            def diagonal(b, k):
                if k >= 2:
                    pool.wait_ge(c_scores, (b - 1) * TB)
                for m in range(KD):
                    pool.tensor_tensor(
                        kbd[:, k % 2, m * 512:(m + 1) * 512].rearrange("p (h n) -> p h n", h=H // 2),
                        kT[:, m:m + 1, bass.ds(b * NK, NK)].broadcast_to([P, H // 2, NK]),
                        hmask[:, :].unsqueeze(2).broadcast_to([P, H // 2, NK]),
                        ALU.mult).then_inc(c_kbd, 1)
            pool.wait_ge(x_new, XB)
            pool.wait_ge(k_scaled, KD)
            each(pool, B, 2, 2, diagonal)
            power(3)

            pool.wait_ge(logits_done, 1)
            pool.iota(xr[:, :, D].bitcast(I32), [[P, NT]], base=0, channel_multiplier=1).then_inc(xr_id, 1)
            pool.wait_ge(fill_done, 16)
            pool.wait_ge(slot_ready, 2)
            pool.wait_ge(xr_extra, 3)
            pool.wait_ge(xr_id, 1)
            for t in range(NT):
                pool.wait_ge(xr_rows, t + 1)
                for w in range(2):
                    pool.indirect_dma_start(
                        out=slots_x.rearrange("b p n -> (b p) n"),
                        out_offset=bass.IndirectOffsetOnAxis(ap=slot_i[:, w, t:t + 1], axis=0),
                        in_=xr[:, t, :], in_offset=None).then_inc(scattered, 16)
            pool.wait_ge(res_done, 16)
            pool.wait_ge(rest_done, 16)
            for i in range(NBLK):
                pool.wait_ge(d_y, i + 1)
                if i:
                    pool.wait_ge(d_added, 16 * i)
                pool.indirect_dma_start(
                    out=out_rows, out_offset=bass.IndirectOffsetOnAxis(ap=row_i[:, i % 2:i % 2 + 1], axis=0),
                    in_=yb[:, i % 2, :], in_offset=None, compute_op=ALU.add).then_inc(d_added, 16)

        @block.scalar
        def _(act):
            def copy_rows(norm):
                def one(b, k):
                    act.wait_ge(ln_turned, norm * B + b + 1)
                    act.activation(xnT[:, :, bass.ds(b * S, S)],
                                   bank(k % 2).rearrange("p (k n) -> p k n", k=KD),
                                   ACT.Copy).then_inc(ln_copied, 1)
                each(act, B, 0, 2, one)

            act.wait_ge(a_route, 1)
            act.activation(route0, bank(6)[:, 0:KD * NK].rearrange("p (k n) -> p k n", k=KD),
                           ACT.Copy, scale=1.0 / math.sqrt(D)).then_inc(a_routed, 1)
            act.activation(brow, bank(6)[0:1, 256:256 + NK], ACT.Copy,
                           scale=1.0 / math.sqrt(D)).then_inc(a_routed, 1)
            copy_rows(0)
            act.wait_ge(k_psum, 1)
            act.wait_ge(in_kv, 16 * 13)
            for m in range(KD):
                act.activation(kT[:, m, :], bank(6 + m), ACT.Identity, bias=vecs[:, 2, m:m + 1]).then_inc(k_copied, 1)
                act.activation(ksq[:, m, :], bank(6 + m), ACT.Square, bias=vecs[:, 2, m:m + 1]).then_inc(k_copied, 1)

            with act.Fori(0, B) as b:
                act.wait_ge(a_top, b * 2 + 2)
                for j in range(TB):
                    act.activation(ex[:, b * TB + j, :], ms[:, b * TB + j, :], ACT.Exp,
                                   bias=negm[:, bass.ds(b * TB + j, 1)]).then_inc(a_exp, 1)
            for q in range(NT // 4):
                act.wait_ge(a_turned, q + 1)
                act.activation(wT[:, q * 512:(q + 1) * 512], bank(4 + q % 2)[0:NK, :], ACT.Copy).then_inc(a_wT, 1)
            copy_rows(1)
            act.wait_ge(b_logits, 1)
            act.activation(sc0, bank(6)[:, 0:NT * E0].rearrange("p (t e) -> p t e", t=NT), ACT.Sigmoid).then_inc(b_sig, 1)
            for g in range(4):
                act.wait_ge(b_turned, g + 1)
                act.activation(cT[:, g * 512:(g + 1) * 512], bank(4 + g % 2).bitcast(BF16)[0:96, 0:512],
                               ACT.Copy).then_inc(b_cT, 1)

            def silu_group(g, k):
                for c in range(C0):
                    i, rows = g * C0 + c, P if c < C0 - 1 else I0
                    act.wait_ge(b_up, i + 1)
                    if k or c >= 2:
                        act.wait_ge(b_prod, i if c == 0 else i - 1)
                    act.activation(sg0[0:rows, c % 2, :], bank(c % 2)[0:rows, :], ACT.Silu).then_inc(b_silu, 1)
            each(act, NG, 1, 1, silu_group)
            copy_rows(2)
            act.wait_ge(in_rest, 16 * 6)

            def queries(b, k):
                act.wait_ge(c_q, b + 1)
                if k >= 2:
                    act.wait_ge(c_ssq, b - 1)
                for m in range(KD):
                    act.activation(sqT[:, k % 2, m, :], bank(2 + k % 2)[:, m * S:(m + 1) * S], ACT.Square,
                                   bias=vecs[:, 0, m:m + 1]).then_inc(c_sq, 1)
                    act.activation(xnT[:, m, bass.ds(b * S, S)], bank(2 + k % 2)[:, m * S:(m + 1) * S],
                                   ACT.Identity, bias=vecs[:, 0, m:m + 1]).then_inc(c_qT, 1)
            each(act, B, 2, 2, queries)

            def pick_tile(t, k):
                if k >= 2:
                    act.wait_ge(c_scores, t - 1)
                act.activation(qt[:, k % 2, :, :], xnT[:, :, bass.ds(t * P, P)], ACT.Copy).then_inc(c_qt, 1)

            def exp_scores(t, k):
                act.wait_ge(c_shift, t + 1)
                if k == 0:
                    act.wait_ge(c_rq, 1)
                if k >= 1:
                    act.wait_ge(c_turned, t)
                act.activation(probs, shift, ACT.Exp, scale=rq[:, bass.ds(t, 1)]).then_inc(c_probs, 1)

            def copy_probs(t, k):
                act.wait_ge(c_turned, t + 1)
                if k >= 2:
                    act.wait_ge(c_pv, t - 1)
                act.activation(pT[:, k % 2, :, :], bank(2, 2).rearrange("p (c n) -> p c n", c=8),
                               ACT.Copy).then_inc(c_pT, 1)

            def copy_att(t, k):
                act.wait_ge(c_attT, t + 1)
                act.activation(attT, bank(5)[:, 0:D].rearrange("p (k n) -> p k n", k=KD), ACT.Copy).then_inc(c_attTc, 1)

            act.wait_ge(c_qT, B * KD)

            def softmax_tile(t, k, more=True):
                if k >= 1:
                    copy_probs(t - 1, k - 1)
                if k >= 2:
                    copy_att(t - 2, k - 2)
                if more:
                    pick_tile(t + 1, k + 1)
                exp_scores(t, k)
            pick_tile(0, 0)
            each(act, NT - 4, 4, 4, softmax_tile)
            for t in range(NT - 4, NT):
                softmax_tile(t, 4 + t % 4, t < NT - 1)
            copy_probs(NT - 1, 3)
            copy_att(NT - 2, 2)
            copy_att(NT - 1, 3)
            copy_rows(3)

            act.wait_ge(logits_done, 1)
            act.wait_ge(xr_shift, 1)
            with act.Fori(0, NT) as t:
                act.activation(xr[:, t, 0:D], x_sb[:, t, :], ACT.Identity, bias=nmr[:, bass.ds(t, 1)],
                               scale=rstd[:, bass.ds(t, 1)]).then_inc(xr_rows, 1)

            def copy_slot_rows(i, k):
                act.wait_ge(d_xturned, i + 1)
                act.activation(xt1[:, k % 2, :, :], bank(7)[:, 0:D].rearrange("p (k n) -> p k n", k=KD),
                               ACT.Copy).then_inc(d_xt, 1)

            def block_act(i, k, more=True):
                act.wait_ge(d_up, i + 1)
                if k:
                    act.wait_ge(d_hidden, i)
                act.activation(sg1.rearrange("p (a n) -> p a n", a=2),
                               bank(0, 2).rearrange("p (a n) -> p a n", a=2)[:, :, 0:HALF1],
                               ACT.Silu).then_inc(d_silu, 1)
                if more:
                    copy_slot_rows(i + 1, k + 1)
                act.wait_ge(d_turned, i + 1)
                act.activation(hT[:, 0:C1 - 1, :], bank(4, 2)[:, 0:(C1 - 1) * P].rearrange("p (c n) -> p c n", n=P),
                               ACT.Copy).then_inc(d_hT, 1)
                act.activation(hT[0:64, C1 - 1, :], bank(4, 2)[0:64, (C1 - 1) * P:C1 * P], ACT.Copy).then_inc(d_hT, 1)
            copy_slot_rows(0, 0)
            each(act, NBLK - 1, 2, 2, block_act)
            block_act(NBLK - 1, 2, False)

        @block.tensor
        def _(pe):
            def turn_rows(norm):
                def one(b, k):
                    pe.wait_ge(ln_rows, norm * B + b + 1)
                    if k >= 2:
                        pe.wait_ge(ln_copied, norm * B + b - 1)
                    for m in range(KD):
                        for j in range(TB):
                            mm = pe.transpose(bank(k % 2)[:, m * S + j * P:m * S + (j + 1) * P],
                                              xn[:, k % 2, j, m * P:(m + 1) * P], ident[:, :])
                    mm.then_inc(ln_turned, 1)
                each(pe, B, 2, 2, one)

            pe.wait_ge(pool_step, 9)
            pe.wait_ge(in_set0, 48)
            for m in range(KD):
                for k in range(KD):
                    pe.matmul(bank(6)[:, m * NK:(m + 1) * NK], wq0[:, k, m * P:(m + 1) * P], descT[:, k, :],
                              start=(k == 0), stop=(k == KD - 1))
            for k in range(KD):
                mm = pe.matmul(bank(6)[0:1, 256:256 + NK], bq0[:, k:k + 1], descT[:, k, :],
                               start=(k == 0), stop=(k == KD - 1))
            mm.then_inc(a_route, 1)
            turn_rows(0)
            pe.wait_ge(a_routed, 2)
            for b in range(B):
                pe.wait_ge(ln_copied, b + 1)
                for t in range(b * TB, (b + 1) * TB):
                    o = bank(2, 2)[:, t * NK:(t + 1) * NK]
                    for k in range(KD):
                        pe.matmul(o, xnT[:, k, t * P:(t + 1) * P], route0[:, k, :], start=(k == 0), stop=False)
                    mm = pe.matmul(o, ones[0:1, :], brow, start=False, stop=True)
                mm.then_inc(a_scored, 1)
            pe.wait_ge(in_kv, 16 * 13)
            for m in range(KD):
                for k in range(KD):
                    mm = pe.matmul(bank(6 + m), wkv[:, k, 0, m * P:(m + 1) * P], ctxT[:, k, :, 0, :],
                                   start=(k == 0), stop=(k == KD - 1))
            mm.then_inc(k_psum, 1)
            pe.wait_ge(k_copied, 4)
            for q in range(B * NK // P):
                for k in range(KD):
                    mm = pe.matmul(bank(4)[:, q:q + 1], ksq[:, k, q * P:(q + 1) * P], ones[:, 0:1],
                                   start=(k == 0), stop=(k == KD - 1))
            mm.then_inc(k_sum, 1)
            for b in range(B):
                o = bank(6 + b % 2)[:, 0:D]
                if b >= 2:
                    pe.wait_ge(v_ready, 2 * (b - 1))
                for k in range(KD):
                    pe.matmul(o, ctxT[:, k, b, :, :], wkv[:, k, 1, :], start=(k == 0), stop=False)
                pe.matmul(o, ones[0:1, :], bv_row, start=False, stop=True).then_inc(v_psum, 1)
            pe.wait_ge(k_diag, B * NK // P)
            for q in range(B * NK // P):
                mm = pe.matmul(bank(4)[:, q * P:(q + 1) * P], ones[:, :], kdiag[:, q, :], start=True, stop=True)
            mm.then_inc(k_spread, 1)
            pe.wait_ge(k_scaled, KD)
            for q in range(NT // 4):
                pe.wait_ge(a_wts, 4 * (q + 1))
                if q >= 2:
                    pe.wait_ge(a_wT, q - 1)
                for t in range(4 * q, 4 * q + 4):
                    mm = pe.transpose(bank(4 + q % 2)[0:NK, (t % 4) * P:(t % 4 + 1) * P], ms[:, t, :], ident[:, :])
                mm.then_inc(a_turned, 1)
            pe.wait_ge(in_ctx, 16)
            pe.wait_ge(v_ready, 2 * B)
            for b in range(B):
                pe.wait_ge(a_wT, b // 2 + 1)
                if b >= 2:
                    pe.wait_ge(x_new, TB * (b - 1))
                for j in range(TB):
                    t = b * TB + j
                    mm = pe.matmul(bank(6 + b % 2)[:, j * D:(j + 1) * D], wT[:, t * P:(t + 1) * P], ctx_sb[:, b, :],
                                   start=True, stop=True)
                mm.then_inc(a_mixed, 1)
            turn_rows(1)
            pe.wait_ge(in_rest, 16 * 6)
            for t in range(NT):
                if t % TB == 0:
                    pe.wait_ge(ln_copied, B + t // TB + 1)
                for k in range(KD):
                    mm = pe.matmul(bank(6)[:, t * E0:(t + 1) * E0], xnT[:, k, t * P:(t + 1) * P], rw0[:, k, :],
                                   start=(k == 0), stop=(k == KD - 1))
            mm.then_inc(b_logits, 1)
            pe.wait_ge(in_ffn0, 48)

            def up0(g, c, k):
                i, rows = g * C0 + c, P if c < C0 - 1 else I0
                if k or c >= 2:
                    pe.wait_ge(b_prod, i if c == 0 else i - 1)
                for part in range(2):
                    for h in range(KD):
                        mm = pe.matmul(bank(2 * part + c % 2)[0:rows, :],
                                       gu0[:, h, c * 2 * P + part * rows:c * 2 * P + (part + 1) * rows],
                                       xnT[:, h, bass.ds(g * 512, 512)], start=(h == 0), stop=(h == KD - 1))
                mm.then_inc(b_up, 1)

            def down0(g, c, k):
                i, rows = g * C0 + c, P if c < C0 - 1 else I0
                pe.wait_ge(b_hidden, i + 1)
                if c == 0 and k:
                    pe.wait_ge(x_new, g * 2 + XA)
                for j in range(4):
                    mm = pe.matmul(bank(6, 2)[:, j * D:(j + 1) * D], h0[0:rows, c % 2, j * P:(j + 1) * P],
                                   dn0[0:rows, c, :], start=(c == 0 and j % 2 == 0), stop=(c == C0 - 1),
                                   skip_group_check=True)
                mm.then_inc(b_down, 1)

            def ffn0_group(g, k):
                if k:
                    up0(g, 0, k)
                    down0(g - 1, C0 - 1, k)
                for c in range(C0 - 1):
                    if k or c >= 2:
                        pe.wait_ge(b_hidden, g * C0 + c - 1)
                    pe.matmul(bank(4 + c % 2), spread[:, c * P:(c + 1) * P], cT[:, bass.ds(g * 512, 512)],
                              start=True, stop=True).then_inc(b_spread, 1)
                    up0(g, c + 1, k)
                    down0(g, c, k)

            up0(0, 0, 0)
            pe.wait_ge(b_c3, 3)
            for g in range(NG):
                if g >= 2:
                    pe.wait_ge(b_cT, g - 1)
                for t in range(4 * g, 4 * g + 4):
                    mm = pe.transpose(bank(4 + g % 2).bitcast(BF16)[0:96, (t % 4) * P:(t % 4 + 1) * P],
                                      c3[:, t, :], identb[:, :])
                mm.then_inc(b_turned, 1)
            pe.wait_ge(b_cT, NG)
            pe.wait_ge(b_sig, 1)
            pe.wait_ge(pool_step, 13)
            each(pe, NG, 1, 1, ffn0_group)
            down0(NG - 1, C0 - 1, 1)

            turn_rows(2)

            def queries(b, k):
                pe.wait_ge(ln_copied, 2 * B + b + 1)
                if k >= 2:
                    pe.wait_ge(c_qT, (b - 1) * KD)
                for m in range(KD):
                    for h in range(KD):
                        mm = pe.matmul(bank(2 + k % 2)[:, m * S:(m + 1) * S], wq1[:, h, m * P:(m + 1) * P],
                                       xnT[:, h, bass.ds(b * S, S)], start=(h == 0), stop=(h == KD - 1))
                mm.then_inc(c_q, 1)

            def squares(b, k):
                pe.wait_ge(c_sq, b * KD + KD)
                for j in range(TB):
                    for m in range(KD):
                        mm = pe.matmul(bank(7)[:, bass.ds(b * TB + j, 1)], sqT[:, k % 2, m, j * P:(j + 1) * P],
                                       ones[:, 0:1], start=(m == 0), stop=(m == KD - 1))
                mm.then_inc(c_ssq, 1)

            def queries_squares(b, k):
                queries(b, k)
                if k >= 1:
                    squares(b - 1, k - 1)
            pe.wait_ge(in_rest, 16 * 6)
            each(pe, B, 2, 2, queries_squares)
            squares(B - 1, 1)

            def scores(t, k):
                pe.wait_ge(c_qt, t + 1)
                if k % TB == 0:
                    pe.wait_ge(c_kbd, t + KD)
                if k:
                    pe.wait_ge(c_shift, t)
                for m in range(KD):
                    mm = pe.matmul(bank(m), qt[:, k % 2, m, :], kbd[:, (k // TB) % 2, m * 512:(m + 1) * 512],
                                   start=True, stop=True)
                mm.then_inc(c_scores, 1)

            def turn_probs(t, k):
                pe.wait_ge(c_probs, t + 1)
                if k:
                    pe.wait_ge(c_pT, t)
                for c in range(8):
                    mm = pe.transpose(bank(2, 2)[:, c * P:(c + 1) * P], probs[:, c * P:(c + 1) * P], ident[:, :])
                mm.then_inc(c_turned, 1)

            def values(t, k, b):
                pe.wait_ge(c_pT, t + 1)
                if k:
                    pe.wait_ge(c_att, t)
                for c in range(8):
                    mm = pe.matmul(bank(4)[:, c * 34:(c + 1) * 34], pT[:, k % 2, c, :], vbd[:, b, c, :],
                                   start=True, stop=True)
                mm.then_inc(c_pv, 1)

            def turn_att(t, k):
                pe.wait_ge(c_att, t + 1)
                if k:
                    pe.wait_ge(c_attTc, t)
                for m in range(KD):
                    mm = pe.transpose(bank(5)[:, m * P:(m + 1) * P], att[:, m * P:(m + 1) * P], ident[:, :])
                mm.then_inc(c_attT, 1)

            def project(t, k):
                pe.wait_ge(c_attTc, t + 1)
                if k:
                    pe.wait_ge(x_new, t + XB)
                for m in range(KD):
                    pe.matmul(bank(6)[:, 0:D], attT[:, m, :], wo1[:, m, :], start=(m == 0), stop=False)
                pe.matmul(bank(6)[:, 0:D], ones[0:1, :], bo_row[:, :], start=False, stop=True).then_inc(c_proj, 1)

            def attend(t, k, base=None, at_tile=0):
                b0 = 0 if base is None else base
                if k < NT:
                    scores(t, k)
                if k >= 1:
                    turn_probs(t - 1, k - 1)
                if k >= 2:
                    turn_att(t - 2, k - 2)
                if k >= 1:
                    values(t - 1, k - 1, b0 + (at_tile - 1) // TB)
                if k >= 2:
                    project(t - 2, k - 2)

            for t in range(4):
                attend(t, t, 0, t)
            with pe.Fori(0, B // 2 - 1) as pair:
                for j in range(4):
                    attend(pair * 4 + (4 + j), 4 + j, pair * 2 + 2, j)
            turn_probs(NT - 1, 3)
            turn_att(NT - 2, 2)
            values(NT - 1, 3, B - 1)
            project(NT - 2, 2)
            turn_att(NT - 1, 3)
            project(NT - 1, 3)

            turn_rows(3)
            for t in range(NT):
                if t % TB == 0:
                    pe.wait_ge(ln_copied, 3 * B + t // TB + 1)
                for h in range(KD):
                    mm = pe.matmul(bank(6)[:, t * E1:(t + 1) * E1], xnT[:, h, t * P:(t + 1) * P], wg1[:, h, :],
                                   start=(h == 0), stop=(h == KD - 1))
            mm.then_inc(d_logits, 1)
            pe.wait_ge(pool_slot, 4)
            pe.wait_ge(kept, 1)
            pe.matmul(bank(4)[:, 0:NT * E1], upper[:, :], keep.rearrange("p t e -> p (t e)"), start=True, stop=True)
            pe.matmul(bank(5)[:, 0:NT * E1], ones[:, :], keep.rearrange("p t e -> p (t e)"),
                      start=True, stop=True).then_inc(counted, 1)

            def turn_slots(i, k):
                pe.wait_ge(xg_in[k % 2], ((i // 2) * 16 if isinstance(i, int) else (i - k % 2) * 8) + 16)
                if k:
                    pe.wait_ge(d_xt, i)
                for h in range(KD):
                    mm = pe.transpose(bank(7)[:, h * P:(h + 1) * P], xg[:, k % 2, h * P:(h + 1) * P], ident[:, :])
                mm.then_inc(d_xturned, 1)

            def up1(i, k, expert):
                pe.wait_ge(d_xt, i + 1)
                if k:
                    pe.wait_ge(d_hidden, i)
                for part in range(2):
                    for half in range(2):
                        for h in range(KD):
                            col = h * W13 + part * I1 + half * HALF1
                            mm = pe.matmul(bank(2 * part + half)[:, 0:HALF1], xt1[:, k % 2, h, :],
                                           wexp[:, bass.ds(expert + col, HALF1)], start=(h == 0), stop=(h == KD - 1))
                mm.then_inc(d_up, 1)

            def turn_hidden(i, k):
                pe.wait_ge(d_hidden, i + 1)
                if k:
                    pe.wait_ge(d_hT, i * 2)
                for c in range(C1):
                    n = min(P, I1 - c * P)
                    mm = pe.transpose(bank(4, 2)[0:n, c * P:(c + 1) * P], h1[:, c * P:c * P + n], ident[:, :])
                mm.then_inc(d_turned, 1)

            def down1(i, k, expert):
                pe.wait_ge(d_hT, i * 2 + 2)
                if k:
                    pe.wait_ge(d_y, i)
                for c in range(C1):
                    n = min(P, I1 - c * P)
                    mm = pe.matmul(bank(6)[:, 0:D], hT[0:n, c, :], wexp[0:n, bass.ds(expert + (KD * W13 + c * D), D)],
                                   start=(c == 0), stop=(c == C1 - 1))
                mm.then_inc(d_down, 1)

            def expert_of(i):
                at = blk_i[0:1, i:i + 1] if isinstance(i, int) else blk_i[0:1, bass.ds(i, 1)]
                return pe.value_load(at, min_val=0, max_val=(E1 - 1) * WE)

            def block_pe(i, k, more=True):
                up1(i, k, expert_of(i))
                if k:
                    down1(i - 1, k - 1, expert_of(i - 1))
                if more:
                    turn_slots(i + 1, k + 1)
                turn_hidden(i, k)
            pe.wait_ge(in_exp0, 16 * 7)
            pe.wait_ge(in_exp7, 16)
            pe.wait_ge(blk_ready, 1)
            pe.wait_ge(slot_ready, 2)
            turn_slots(0, 0)
            each(pe, NBLK - 1, 2, 2, block_pe)
            block_pe(NBLK - 1, 2, False)
            down1(NBLK - 1, 2, expert_of(NBLK - 1))

        @block.vector
        def _(dve):
            def stats(norm, b):
                dve.memset(carrier[:, :], 0.0)
                for j in range(TB):
                    dve.bn_stats(st6[:, j, :], x_sb[:, b * TB + j, :]).then_inc(ln_stats, 1)
                dve.wait_ge(ln_stats, (norm * B + b) * TB + TB)
                dve.memset(carrier[:, :], 0.0)
                for j in range(TB):
                    dve.bn_aggr(mv[:, j, :], st6[:, j, :]).then_inc(ln_mv, 1)
                dve.wait_ge(ln_mv, (norm * B + b) * TB + TB)
                dve.tensor_copy(mean[:, bass.ds(b * TB, TB)], mv[:, :, 0])
                dve.tensor_scalar(ve[:, bass.ds(b * TB, TB)], mv[:, :, 1], 1e-5, None,
                                  ALU.add).then_inc(ln_var, 1)

            def rows(norm):
                def one(b, k):
                    dve.wait_ge(ln_rstd, norm * B + b + 1)
                    if k >= 2:
                        dve.wait_ge(ln_turned, norm * B + b - 1)
                    for j in range(TB):
                        t = b * TB + j
                        r = dve.tensor_scalar(xn[:, k % 2, j, :], x_sb[:, t, :], mean[:, bass.ds(t, 1)],
                                              rstd[:, bass.ds(t, 1)], ALU.subtract, ALU.mult)
                    r.then_inc(ln_rows, 1)
                each(dve, B, 2, 2, one)

            dve.memset(t8[:, :, :], NEG).then_inc(dve_const, 1)
            dve.memset(pmask[:, :], 0.0).then_inc(dve_const, 1)
            dve.wait_ge(dve_const, 2)
            dve.memset(pmask[0:NK, 0:1], 1.0).then_inc(dve_const, 1)
            dve.memset(pmask[NK:P, 1:2], 1.0).then_inc(dve_const, 1)
            dve.wait_ge(in_x0, 16)
            with dve.Fori(0, B // 2) as b:
                stats(0, b)
            dve.wait_ge(in_x1, 16)
            with dve.Fori(B // 2, B) as b:
                stats(0, b)
            rows(0)

            dve.wait_ge(in_itok, 16)
            dve.wait_ge(pool_step, 9)
            dve.tensor_copy(hit[:, 0, 0:TB * TOPK_SETS], itok[:, :, :].rearrange("p j k -> p (j k)")).then_inc(s_mask, 1)
            dve.wait_ge(s_mask, 1)
            for j in range(TB):
                dve.tensor_scalar(negmask[:, j, :], iota64[:, :], hit[:, 0, j * TOPK_SETS:j * TOPK_SETS + 1], None,
                                  ALU.is_equal).then_inc(s_mask, 1)
            for n in range(1, TOPK_SETS):
                dve.wait_ge(s_mask, 1 + TB * n)
                for j in range(TB):
                    o = j * TOPK_SETS + n
                    dve.scalar_tensor_tensor(out=negmask[:, j, :], in0=iota64[:, :], scalar=hit[:, 0, o:o + 1],
                                             in1=negmask[:, j, :], op0=ALU.is_equal, op1=ALU.max).then_inc(s_mask, 1)
            dve.wait_ge(s_mask, 1 + TB * TOPK_SETS)
            dve.tensor_scalar(negmask, negmask, 1.0, -NEG, ALU.subtract, ALU.mult).then_inc(s_mask, 1)
            dve.wait_ge(s_mask, 2 + TB * TOPK_SETS)

            def pick(b, k):
                dve.wait_ge(a_scored, 4 * (b // 4 + 1))
                pair = bass.ds(b * TB, TB)
                dve.tensor_tensor(ms[:, pair, :], bank(2, 2).rearrange("p (t n) -> p t n", t=NT)[:, pair, :],
                                  negmask, ALU.add).then_inc(a_masked, 1)
                dve.wait_ge(a_masked, b + 1)
                for j in range(TB):
                    dve.max(m8[:, b * TB + j, :], ms[:, b * TB + j, :]).then_inc(a_max, 1)
                dve.wait_ge(a_max, b * TB + TB)
                dve.tensor_copy(t8[:, pair, 0:2], m8[:, pair, 0:2]).then_inc(a_top, 1)
                dve.tensor_scalar(negm[:, pair], m8[:, pair, 0], -1.0, None, ALU.mult).then_inc(a_top, 1)
                dve.wait_ge(a_top, b * 2 + 2)
                for j in range(TB):
                    dve.match_replace(picked[:, b * TB + j, :], t8[:, b * TB + j, :], ms[:, b * TB + j, :],
                                      FOUND).then_inc(a_picked, 1)
            for b in range(B):
                pick(b, b)

            dve.wait_ge(in_kv, 16 * 13)
            dve.tensor_tensor(gg[:, :], vecs[:, 1, :], vecs[:, 3, :], ALU.mult).then_inc(gg_ready, 1)
            dve.wait_ge(k_sum, 1)
            dve.tensor_scalar(kvar, bank(4)[:, 0:B * NK // P], 1.0 / D, 1e-6, ALU.mult, ALU.add).then_inc(k_var, 1)

            def mix_values(b, k):
                dve.wait_ge(v_psum, b + 1)
                o = vbd[:, b, :, :].rearrange("p a (r n) -> p a r n", r=2)
                half = pmask[:, :].unsqueeze(1)
                dve.tensor_tensor(o[:, :, :, 0:HD], bank(6 + k % 2)[:, 0:D].rearrange("p (a r n) -> p a r n", a=8, r=2),
                                  half.unsqueeze(3).broadcast_to([P, 8, 2, HD]), ALU.mult).then_inc(v_ready, 1)
                dve.tensor_copy(o[:, :, :, HD], half.broadcast_to([P, 8, 2])).then_inc(v_ready, 1)
            dve.wait_ge(dve_const, 4)
            each(dve, B, 0, 2, mix_values)
            dve.wait_ge(k_pow, 1)
            for q in range(B * NK // P):
                dve.tensor_scalar(kdiag[:, q, :], ident[:, :], krst[:, q:q + 1], None, ALU.mult).then_inc(k_diag, 1)
            dve.wait_ge(k_spread, 1)
            dve.wait_ge(k_copied, 4)
            dve.wait_ge(gg_ready, 1)
            for m in range(KD):
                dve.scalar_tensor_tensor(out=kT[:, m, :], in0=kT[:, m, :], scalar=gg[:, m:m + 1], in1=bank(4),
                                         op0=ALU.mult, op1=ALU.mult).then_inc(k_scaled, 1)

            with dve.Fori(0, NT) as t:
                dve.wait_ge(a_exp, t + 1)
                dve.wait_ge(a_picked, t + 1)
                dve.scalar_tensor_tensor(out=ms[:, t, :], in0=picked[:, t, :], scalar=1.0e38, in1=ex[:, t, :],
                                         op0=ALU.is_gt, op1=ALU.mult, accum_out=sums[:, bass.ds(t, 1)]).then_inc(a_wts, 1)
            dve.wait_ge(a_wts, NT)
            dve.reciprocal(recs[:, :], sums[:, :]).then_inc(a_rec, 1)
            dve.wait_ge(a_rec, 1)

            def mix_sets(b, k):
                dve.wait_ge(a_mixed, b + 1)
                for j in range(TB):
                    t = b * TB + j
                    dve.scalar_tensor_tensor(out=x_sb[:, t, :], in0=bank(6 + k % 2)[:, j * D:(j + 1) * D],
                                             scalar=recs[:, bass.ds(t, 1)], in1=x_sb[:, t, :],
                                             op0=ALU.mult, op1=ALU.add).then_inc(x_new, 1)
                dve.wait_ge(x_new, b * TB + TB)
                stats(1, b)
            each(dve, B, 0, 2, mix_sets)

            rows(1)
            dve.wait_ge(ln_turned, 2 * B)
            dve.wait_ge(in_rest, 16 * 6)
            dve.memset(sel0[:, :, E0:E0 + 4], NEG).then_inc(b_step, 1)
            dve.wait_ge(fill_done, 16)
            dve.wait_ge(rest_done, 16)
            dve.memset(arena[:, 1024:1792], 0.0).then_inc(b_step, 1)
            dve.wait_ge(b_sig, 1)
            dve.tensor_tensor(sel0[:, :, 0:E0], sc0, ebias[:, :].unsqueeze(1).broadcast_to([P, NT, E0]),
                              ALU.add).then_inc(b_step, 1)
            dve.wait_ge(b_step, 3)
            for t in range(NT):
                dve.max(m8[:, t, :], sel0[:, t, :]).then_inc(b_max, 1)
            dve.wait_ge(b_max, NT)
            dve.tensor_copy(t8[:, :, 0:4], m8[:, :, 0:4]).then_inc(b_step, 1)
            dve.wait_ge(b_step, 4)
            for t in range(NT):
                dve.match_replace(rep0[:, t, :], t8[:, t, :], sel0[:, t, :], FOUND).then_inc(b_max, 1)
            dve.wait_ge(b_max, 2 * NT)
            dve.scalar_tensor_tensor(out=cw0, in0=rep0[:, :, 0:E0], scalar=1.0e38, in1=sc0,
                                     op0=ALU.is_gt, op1=ALU.mult).then_inc(b_step, 1)
            dve.wait_ge(b_step, 5)
            dve.tensor_reduce(sums[:, :], cw0, AX.X, ALU.add).then_inc(b_step, 1)
            dve.wait_ge(b_step, 6)
            dve.tensor_scalar(sums[:, :], sums[:, :], 1e-20, None, ALU.add).then_inc(b_step, 1)
            dve.wait_ge(b_step, 7)
            dve.reciprocal(recs[:, :], sums[:, :]).then_inc(b_step, 1)
            dve.wait_ge(b_step, 8)
            dve.tensor_tensor(cw0, cw0, recs[:, :].unsqueeze(2).broadcast_to([P, NT, E0]), ALU.mult).then_inc(b_step, 1)
            dve.wait_ge(b_step, 9)
            dve.tensor_copy(c3[:, :, 0:E0], cw0).then_inc(b_c3, 1)
            dve.wait_ge(b_c3, 1)
            dve.tensor_tensor(res0, cw0, c3[:, :, 0:E0], ALU.subtract).then_inc(b_step, 1)
            dve.wait_ge(b_step, 10)
            dve.tensor_copy(c3[:, :, 32:32 + E0], res0).then_inc(b_c3, 1)
            dve.wait_ge(b_c3, 2)
            dve.tensor_tensor(c3[:, :, 64:64 + E0], res0, c3[:, :, 32:32 + E0], ALU.subtract).then_inc(b_c3, 1)

            def ffn0_group(g, k):
                for c in range(C0):
                    i, rows_ = g * C0 + c, P if c < C0 - 1 else I0
                    dve.wait_ge(b_silu, i + 1)
                    dve.tensor_tensor(hm0[0:rows_, c % 2, :], sg0[0:rows_, c % 2, :], bank(2 + c % 2)[0:rows_, :],
                                      ALU.mult).then_inc(b_prod, 1)
                    if k or c >= 2:
                        dve.wait_ge(b_down, i if c == 0 else i - 1)
                    dve.wait_ge(b_prod, i + 1)
                    if c < C0 - 1:
                        dve.wait_ge(b_spread, g * (C0 - 1) + c + 1)
                        dve.tensor_tensor(h0[:, c % 2, :], hm0[:, c % 2, :], bank(4 + c % 2), ALU.mult).then_inc(b_hidden, 1)
                    else:
                        dve.tensor_copy(h0[0:rows_, c % 2, :], hm0[0:rows_, c % 2, :]).then_inc(b_hidden, 1)

            def add_ffn0(g):
                dve.wait_ge(b_down, g * C0 + C0)
                for j in range(2):
                    t = g * 4 + j * 2
                    o = x_sb[:, bass.ds(t, 2), :].rearrange("p t d -> p (t d)")
                    dve.tensor_tensor(o, o, bank(6 + j), ALU.add).then_inc(x_new, 1)
                dve.wait_ge(x_new, g * 2 + XA + 2)
                for j in range(2):
                    stats(2, g * 2 + j)

            def group_and_sums(g, k):
                ffn0_group(g, k)
                add_ffn0(g)
            each(dve, NG, 1, 1, group_and_sums)

            rows(2)
            dve.wait_ge(c_ssq, B)
            dve.tensor_scalar(ssq[:, :], bank(7)[:, 0:NT], HD / D, HD * 1e-6, ALU.mult, ALU.add).then_inc(c_var, 1)

            def centre(t, k):
                dve.wait_ge(c_scores, t + 1)
                s = bank(0, 2).rearrange("p (h n) -> p h n", h=H)
                dve.tensor_reduce(mx1[:, :], s, AX.X, ALU.max).then_inc(c_max, 1)
                dve.wait_ge(c_max, t + 1)
                if k:
                    dve.wait_ge(c_probs, t)
                dve.tensor_tensor(shift.rearrange("p (h n) -> p h n", h=H), s,
                                  mx1[:, :].unsqueeze(2).broadcast_to([P, H, NK]), ALU.subtract).then_inc(c_shift, 1)

            def divide(t, k):
                dve.wait_ge(c_pv, t + 1)
                v = bank(4)[:, 0:H * (HD + 1)].rearrange("p (h n) -> p h n", h=H)
                dve.reciprocal(rec1[:, :], v[:, :, HD]).then_inc(c_rec, 1)
                dve.wait_ge(c_rec, t + 1)
                if k:
                    dve.wait_ge(c_attT, t)
                dve.tensor_tensor(att.rearrange("p (h n) -> p h n", h=H), v[:, :, 0:HD],
                                  rec1[:, :].unsqueeze(2).broadcast_to([P, H, HD]), ALU.mult).then_inc(c_att, 1)

            def add_att(t, k):
                dve.wait_ge(c_proj, t + 1)
                dve.tensor_tensor(x_sb[:, t, :], x_sb[:, t, :], bank(6)[:, 0:D], ALU.add).then_inc(x_new, 1)

            def attend(t, k, b0, j):
                centre(t, k)
                if k >= 1:
                    divide(t - 1, k - 1)
                if k >= 2:
                    add_att(t - 2, k - 2)
                    if k % TB == 1:
                        dve.wait_ge(x_new, t - 2 + XB + 1)
                        stats(3, b0 + (j - 2) // TB)
            for t in range(4):
                attend(t, t, 0, t)
            with dve.Fori(0, B // 2 - 1) as pair:
                for j in range(4):
                    attend(pair * 4 + (4 + j), 4 + j, pair * 2 + 2, j)
            divide(NT - 1, 3)
            add_att(NT - 2, 2)
            add_att(NT - 1, 3)
            dve.wait_ge(x_new, XC)
            stats(3, B - 1)

            rows(3)
            done = [0]

            def step(instruction):
                instruction.then_inc(d_step, 1)
                done[0] += 1
                dve.wait_ge(d_step, done[0])

            def over_experts(a):
                return a.unsqueeze(2).broadcast_to([P, NT, E1])

            dve.wait_ge(d_logits, 1)
            logits = bank(6)[:, 0:NT * E1].rearrange("p (t e) -> p t e", t=NT)
            step(dve.tensor_scalar(li, logits, float(Q_IN), ROUND, ALU.mult, ALU.add))
            dve.sem_inc(logits_done, 1)
            dve.scalar_tensor_tensor(out=nmr[:, :], in0=mean[:, :], scalar=-1.0, in1=rstd[:, :],
                                     op0=ALU.mult, op1=ALU.mult).then_inc(xr_shift, 1)
            step(dve.tensor_scalar(li, li, ROUND, None, ALU.subtract))
            step(dve.tensor_reduce(m1[:, :], li, AX.X, ALU.max))
            step(dve.tensor_tensor(sh, li, over_experts(m1[:, :]), ALU.subtract))
            step(dve.tensor_scalar(sh, sh, -float(Q_IN), None, ALU.max))
            step(dve.scalar_tensor_tensor(out=key, in0=sh, scalar=float(E1),
                                          in1=iota64[:, 0:E1].unsqueeze(1).broadcast_to([P, NT, E1]),
                                          op0=ALU.mult, op1=ALU.subtract))
            for t in range(NT):
                dve.max(m8[:, t, :], key[:, t, :]).then_inc(d_max, 1)
            dve.wait_ge(d_max, NT)
            dve.tensor_tensor(keep, key, over_experts(m8[:, :, 1]), ALU.is_ge).then_inc(kept, 1)
            dve.wait_ge(kept, 1)
            step(dve.tensor_scalar(zz, sh, 1.0 / Q_IN, None, ALU.mult))
            coef = exp_coefficients()
            step(dve.tensor_scalar(po, zz, coef[-1], None, ALU.mult))
            for c in coef[-2:0:-1]:
                step(dve.scalar_tensor_tensor(out=po, in0=po, scalar=c, in1=zz, op0=ALU.add, op1=ALU.mult))
            step(dve.tensor_scalar(po, po, Q_OUT, Q_OUT - 0.5, ALU.mult, ALU.add))
            step(dve.tensor_scalar(po, po, ROUND, None, ALU.add))
            step(dve.tensor_scalar(po, po, ROUND, None, ALU.subtract))
            step(dve.tensor_tensor(po, po, keep, ALU.mult))
            step(dve.tensor_reduce(m1[:, :], po, AX.X, ALU.add))
            step(dve.reciprocal(m1[:, :], m1[:, :]))
            step(dve.tensor_tensor(po, po, over_experts(m1[:, :]), ALU.mult))

            dve.wait_ge(counted, 1)
            step(dve.tensor_copy(cum[:, 0, :, :], bank(5)[:, 0:NT * E1].rearrange("p (t e) -> p t e", t=NT)))
            for n, d in enumerate((1, 2, 4, 8)):
                a, b = cum[:, n % 2, :, :], cum[:, 1 - n % 2, :, :]
                dve.tensor_copy(b[:, 0:d, :], a[:, 0:d, :])
                step(dve.tensor_tensor(b[:, d:NT, :], a[:, d:NT, :], a[:, 0:NT - d, :], ALU.add))
            cum0 = cum[:, 0, :, :]
            step(dve.tensor_tensor(slot, cum0, bank(5)[:, 0:NT * E1].rearrange("p (t e) -> p t e", t=NT), ALU.subtract))
            step(dve.tensor_tensor(slot, slot, bank(4)[:, 0:NT * E1].rearrange("p (t e) -> p t e", t=NT), ALU.add))
            nb, nbs = small8[:, 0, :], [small8[:, 1, :], small8[:, 2, :]]
            step(dve.tensor_scalar(nb, cum0[:, NT - 1, :], 1.0 / P, (P - 1.0) / P - 0.498, ALU.mult, ALU.add))
            step(dve.tensor_scalar(nb, nb, ROUND, None, ALU.add))
            step(dve.tensor_scalar(nb, nb, ROUND, None, ALU.subtract))
            step(dve.tensor_copy(nbs[0], nb))
            for n, d in enumerate((1, 2, 4)):
                a, b = nbs[n % 2], nbs[1 - n % 2]
                dve.tensor_copy(b[:, 0:d], a[:, 0:d])
                step(dve.tensor_tensor(b[:, d:E1], a[:, d:E1], a[:, 0:E1 - d], ALU.add))
            upto = nbs[1]
            step(dve.tensor_tensor(nb, upto, nb, ALU.subtract))
            step(dve.tensor_scalar(nb, nb, float(P), 1.0, ALU.mult, ALU.add))
            step(dve.tensor_tensor(slot, slot, nb.unsqueeze(1).broadcast_to([P, NT, E1]), ALU.add))
            step(dve.tensor_tensor(slot, slot, keep, ALU.mult))
            step(dve.tensor_reduce(m1[:, :], slot, AX.X, ALU.max))
            step(dve.tensor_reduce(sums[:, :], slot, AX.X, ALU.add))
            step(dve.tensor_tensor(sums[:, :], sums[:, :], m1[:, :], ALU.subtract))
            step(dve.tensor_tensor(slot, slot, over_experts(m1[:, :]), ALU.is_equal))
            dve.tensor_scalar(slot_i[:, 0, :], m1[:, :], -1.0, None, ALU.add).then_inc(slot_ready, 1)
            dve.tensor_scalar(slot_i[:, 1, :], sums[:, :], -1.0, None, ALU.add).then_inc(slot_ready, 1)
            step(dve.tensor_tensor(slot, slot, po, ALU.mult))
            step(dve.tensor_reduce(recs[:, :], slot, AX.X, ALU.add))
            step(dve.tensor_tensor(po, po, slot, ALU.subtract))
            dve.tensor_scalar(xr[:, :, D + 3], m1[:, :], -1.0, None, ALU.add).then_inc(xr_extra, 1)
            dve.tensor_reduce(xr[:, :, D + 1], po, AX.X, ALU.add).then_inc(xr_extra, 1)
            dve.wait_ge(xr_extra, 2)
            dve.tensor_tensor(xr[:, :, D + 2], recs[:, :], xr[:, :, D + 1], ALU.subtract).then_inc(xr_extra, 1)
            step(dve.tensor_scalar(blk[:, :], blkno[:, :], upto[:, 0:1], None, ALU.is_ge))
            for e in range(1, E1 - 1):
                step(dve.scalar_tensor_tensor(out=blk[:, :], in0=blkno[:, :], scalar=upto[:, e:e + 1], in1=blk[:, :],
                                              op0=ALU.is_ge, op1=ALU.add))
            dve.tensor_scalar(blk_i[:, :], blk[:, :], float(WE), None, ALU.mult).then_inc(blk_ready, 1)

            dve.wait_ge(pool_slot, 4)

            def weigh(i, k):
                dve.wait_ge(xg_in[k % 2], ((i // 2) * 16 if isinstance(i, int) else (i - k % 2) * 8) + 16)
                dve.tensor_scalar(wb[:, k % 2:k % 2 + 1], xg[:, k % 2, D + 3:D + 4], slotno[:, bass.ds(i, 1)],
                                  xg[:, k % 2, D + 2:D + 3], ALU.is_equal, ALU.mult).then_inc(d_wstep, 1)
                if k >= 2:
                    dve.wait_ge(d_added, (i - 1) * 16)
                dve.wait_ge(d_wstep, i + 1)
                dve.tensor_tensor(wb[:, k % 2:k % 2 + 1], wb[:, k % 2:k % 2 + 1], xg[:, k % 2, D + 1:D + 2],
                                  ALU.add).then_inc(d_weight, 1)
                dve.tensor_copy(row_i[:, k % 2:k % 2 + 1], xg[:, k % 2, D:D + 1].bitcast(I32)).then_inc(d_weight, 1)

            def weighted(i, k):
                dve.wait_ge(d_down, i + 1)
                dve.wait_ge(d_weight, i * 2 + 2)
                dve.tensor_scalar(yb[:, k % 2, :], bank(6)[:, 0:D], wb[:, k % 2:k % 2 + 1], None,
                                  ALU.mult).then_inc(d_y, 1)

            def block_dve(i, k):
                dve.wait_ge(d_silu, i + 1)
                if k:
                    dve.wait_ge(d_turned, i)
                dve.tensor_tensor(h1.rearrange("p (a n) -> p a n", a=2),
                                  sg1.rearrange("p (a n) -> p a n", a=2),
                                  bank(2, 2).rearrange("p (a n) -> p a n", a=2)[:, :, 0:HALF1],
                                  ALU.mult).then_inc(d_hidden, 1)
                if k:
                    weighted(i - 1, k - 1)
                weigh(i, k)
            each(dve, NBLK - 1, 2, 2, block_dve)
            block_dve(NBLK - 1, 2)
            weighted(NBLK - 1, 2)


def kernel(**inputs):
    import concourse.bacc as _bacc
    from concourse.bass_utils import run_bass_kernel_spmd as _run

    g = {name: np.asarray(a) for name, a in inputs.items()}
    gu, dn = g["L0_ffn_gate_up_proj"], g["L0_ffn_down_proj"]
    chunks = E0 * I0 // P
    gate = gu[:, 0:I0, :].reshape(chunks, P, D)
    up = gu[:, I0:2 * I0, :].reshape(chunks, P, D)
    gu0 = np.concatenate([np.stack([gate, up], 1).reshape(2 * E0 * I0, D),
                          g["L0_ffn_shared_gate_w"], g["L0_ffn_shared_up_w"]], 0).T
    dn0 = np.zeros((P, C0, D), dn.dtype)
    dn0[:, 0:chunks] = dn.transpose(0, 2, 1).reshape(chunks, P, D).transpose(1, 0, 2)
    dn0[0:I0, chunks] = g["L0_ffn_shared_down_w"].T
    w1, w2, w3 = g["L1_ffn_w1"], g["L1_ffn_w2"], g["L1_ffn_w3"]
    wexp = np.zeros((P, E1, WE), w1.dtype)
    for e in range(E1):
        for k in range(KD):
            wexp[:, e, k * W13:k * W13 + I1] = w1[e].T[k * P:(k + 1) * P]
            wexp[:, e, k * W13 + I1:(k + 1) * W13] = w3[e].T[k * P:(k + 1) * P]
        for c in range(C1):
            n = min(P, I1 - c * P)
            wexp[0:n, e, KD * W13 + c * D:KD * W13 + (c + 1) * D] = w2[e].T[c * P:c * P + n]
    def columns(vector):
        return vector.reshape(KD, P).T

    arrays = {
        "x": g["x"], "ctx": g["ctx_2048"], "ctxT": g["ctx_2048"].reshape(B * NK, D).T,
        "itok": g["itok_Sx4_0_63"], "descT": g["L0_xattn_desc_router"].T, "wq0": g["L0_xattn_W_q"],
        "bq0": columns(g["L0_xattn_b_q"]), "rw0": g["L0_ffn_router_w"].T, "ebias": g["L0_ffn_e_bias"],
        "gu0": gu0, "dn0": dn0, "wq1": g["L1_xattn_Wq"], "bq1": columns(g["L1_xattn_bq"]),
        "gq1": columns(g["L1_xattn_gq"]), "wk1": g["L1_xattn_Wk_img"], "bk1": columns(g["L1_xattn_bk_img"]),
        "gk1": columns(g["L1_xattn_gk_img"]), "wv1": g["L1_xattn_Wv_img"], "bv1": g["L1_xattn_bv_img"],
        "wo1": g["L1_xattn_Wo"], "bo1": g["L1_xattn_bo"], "wg1": g["L1_ffn_w_gate"].T, "wexp": wexp,
    }
    nc = _bacc.Bacc("TRN2", target_bir_lowering=False, num_devices=1)
    feed, args = {}, []
    for name, a in arrays.items():
        a = np.ascontiguousarray(a)
        feed[f"in_{name}"] = a
        args.append(nc.dram_tensor(f"in_{name}", a.shape, mybir.dt.from_np(a.dtype), kind="ExternalInput").ap())
    args.append(nc.dram_tensor("out_rows", ((NT + 1) * P, D), F32, kind="ExternalOutput").ap())
    program(nc, *args)
    return _run(nc, [feed], core_ids=[0]).results[0]["out_rows"][0:NT * P].reshape(B, S, D)
```

```python
import math
from contextlib import ExitStack

import numpy as np

import concourse.bass as bass
from concourse import mybir

F32 = mybir.dt.float32
BF16 = mybir.dt.bfloat16
F32R = mybir.dt.float32r
I32 = mybir.dt.int32
ALU = mybir.AluOpType
ACT = mybir.ActivationFunctionType
AX = mybir.AxisListType

P = 128
B, S, D = 8, 256, 256
KD = D // P
NT = B * S // P
TB = S // P
NK = 64
TOPK_SETS = 4
E0, I0 = 16, 96
C0 = E0 * I0 // P + 1
E1, I1 = 8, 704
C1 = -(-I1 // P)
H, HD = 16, 16
NEG = -3.0e38
FOUND = 3.0e38
ROUND = 12582912.0
Q_IN = 128
Q_OUT = 65536.0
HALF1 = I1 // 2
W13 = 2 * I1
WE = KD * W13 + C1 * D
TOP1 = 2
NBLK = (TOP1 * NT * P - E1) // P + E1
NSRC = TOP1 * NT
COLS = NBLK + NBLK % 2
BATCH = 4


def exp_coefficients(degree=8):
    z = np.linspace(-1, 0, 4001)
    c = np.polynomial.chebyshev.Chebyshev.fit(z, np.exp(z), degree, domain=[-1, 0])
    return [float(v) for v in c.convert(kind=np.polynomial.Polynomial).coef]


def program(nc, x_in, ctx_in, ctxT_in, itok_in, descT_in, wq0_in, bq0_in, rw0_in, ebias_in,
            gu0_in, dn0_in, wq1_in, bq1_in, gq1_in, wk1_in, bk1_in, gk1_in, wv1_in, bv1_in,
            wo1_in, bo1_in, wg1_in, wexp_in, out_rows):
    with ExitStack() as st:
        def sb(name, shape, dt=F32):
            return st.enter_context(nc.sbuf_tensor(name, shape, dt))

        def sem(name):
            return st.enter_context(nc.semaphore(name))

        x_sb = sb("x_sb", [P, NT, D])
        late = 5 * WE
        GU0 = 2 * E0 * I0 + 2 * I0

        def parts_over(*places):
            with ExitStack() as scope:
                found, at = [], 0
                for name, first, columns in places:
                    if first > at:
                        scope.enter_context(nc.sbuf_tensor(f"before_{name}", [P, first - at], F32))
                    found.append(scope.enter_context(nc.sbuf_tensor(name, [P, columns], F32R)))
                    at = first + columns
            return found

        xn_high_mem, = parts_over(("xn_high", 0, KD * NT * P))
        xmem = sb("xmem", [P, NT * D])
        xn_low_mem, dn_high_mem, h_low_mem, gu_high_mem, gu_low_mem, dn_low_mem, h_high_mem = parts_over(
            ("xn_low", 0, KD * NT * P), ("dn_high", 5120, C0 * D), ("h_low", 12800, 2 * 512),
            ("gu_high", 13888, KD * GU0), ("gu_low", late, KD * GU0), ("dn_low", late + KD * GU0, C0 * D),
            ("h_high", late + KD * GU0 + C0 * D + 2048, 2 * 512))
        wexp = sb("wexp", [P, E1 * WE])
        onehot_mem, placed_mem = parts_over(("onehot", 2176, 2 * BATCH * P), ("placed", 3200, 2 * BATCH * 3 * COLS))
        arena = sb("arena", [P, 4224])

        def view(tensor, first, *shape):
            v = tensor[:, first:first + int(np.prod(shape))]
            names = "abcd"[:len(shape)]
            if len(shape) > 1:
                v = v.rearrange(f"p ({' '.join(names)}) -> p {' '.join(names)}",
                                **dict(zip(names[:-1], shape)))
            return v

        xnT = view(xmem, 0, KD, NT * P)
        xr = view(xmem, 0, NT, D)

        ctxT = view(wexp, 0, KD, B, 2, NK)
        wkv = view(wexp, 2048, KD, 2, D)
        ksq = view(wexp, 3072, KD, B * NK)
        kvar = view(wexp, 4096, B * NK // P)
        krst = view(wexp, 4100, B * NK // P)
        kdiag = view(wexp, 4608, B * NK // P, P)
        bv_row = wexp[0:1, 5120:5120 + D]
        ms = view(wexp, 5632, NT, NK)
        picked = view(wexp, 6656, NT, NK)
        ex = view(wexp, 7680, NT, NK)
        wT = wexp[0:NK, 8704:8704 + NT * P]
        ctx_sb = wexp[0:NK, 10752:10752 + B * D].rearrange("p (b d) -> p b d", b=B)
        wq0 = view(wexp, 12800, KD, D)
        descT = view(wexp, 13312, KD, NK)
        route0 = view(wexp, 13440, KD, NK)
        negmask = view(wexp, 13568, TB, NK)
        hit = view(wexp, 13696, TB, NK)
        brow = wexp[0:1, 13824:13824 + NK]
        gu0 = view(wexp, late, KD, GU0)
        gu_high = view(gu_high_mem, 0, KD, GU0)
        gu_low = view(gu_low_mem, 0, KD, GU0)
        dn0 = view(wexp, late + KD * GU0, C0, D)
        dn_high = view(dn_high_mem, 0, C0, D)
        dn_low = view(dn_low_mem, 0, C0, D)
        xn_high = view(xn_high_mem, 0, KD, NT * P)
        xn_full = view(wexp, 0, KD, NT * P)
        xn_low = view(xn_low_mem, 0, KD, NT * P)
        sg0 = view(wexp, late + KD * GU0 + C0 * D, 2, 512)
        hm0 = view(wexp, late + KD * GU0 + C0 * D + 1024, 2, 512)
        h_high = view(h_high_mem, 0, 2, 512)
        h_low = view(h_low_mem, 0, 2, 512)
        last = 7 * WE
        kbd = view(wexp, last, 2, 1024)
        pT = view(wexp, last + 2048, 2, 8, P)
        bo_rows = view(wexp, last + 4096, D)
        xn = view(arena, 0, 2, TB, D)
        xn2 = view(arena, 2560, 2, TB, D)
        xn3 = view(arena, 2048, 2, TB, D)
        xn_of, bank_of = (xn, xn, xn2, xn3), (None, None, 5, 7)
        cT = arena[0:96, 0:1024].bitcast(BF16)
        c3 = arena[:, 1024:1792].bitcast(BF16).rearrange("p (t c) -> p t c", t=NT)
        spread = arena[0:96, 1792:2560].bitcast(BF16)
        sc0 = view(arena, 2560, NT, E0)
        sel0 = view(arena, 2816, NT, E0 + 4)
        rep0 = view(arena, 3136, NT, E0 + 4)
        cw0 = view(arena, 3456, NT, E0)
        res0 = view(arena, 3712, NT, E0)
        shift = view(arena, 0, H * NK)
        probs = view(arena, 1024, H * NK)
        sqT = view(arena, 1024, 2, KD, S)
        qt = view(arena, 3072, 2, KD, P)
        att = view(arena, 3584, D)
        attT = view(arena, 3840, KD, P)
        filler = view(arena, 1024, D)
        li = view(arena, 1024, NT, E1)
        sh = view(arena, 1152, NT, E1)
        key = view(arena, 1280, NT, E1)
        zz = view(arena, 1408, NT, E1)
        po = view(arena, 1536, NT, E1)
        keep = view(arena, 1664, NT, E1)
        slot = view(arena, 1792, NT, E1)
        cum = view(arena, 1920, 2, NT, E1)
        xt1 = view(arena, 0, 2, KD, P)
        sg1 = view(arena, 512, I1)
        h1 = view(arena, 1216, I1)
        hT = view(arena, 2176, C1, P)
        xg = view(arena, 2944, 2, D)
        yb = view(arena, 3456, 2, D)
        onehot = view(onehot_mem, 0, 2, BATCH, P)
        placed = view(placed_mem, 0, 2, BATCH, 3 * COLS)
        incolumn = view(arena, 0, 2, BATCH, COLS)
        ident = sb("ident", [P, P])
        identb = sb("identb", [P, P], BF16)
        ones = sb("ones", [P, P])
        st6 = sb("st6", [P, TB, 6])
        mv = sb("mv", [P, TB, 2])
        mean = sb("mean", [P, NT])
        carrier = sb("carrier", [P, 1])
        ve = sb("ve", [P, NT])
        rstd = sb("rstd", [P, NT])
        mhalf = sb("mhalf", [P, 1])
        m8 = sb("m8", [P, NT, 8])
        t8 = sb("t8", [P, NT, 8])
        negm = sb("negm", [P, NT])
        sums = sb("sums", [P, NT])
        recs = sb("recs", [P, NT])
        iota = sb("iota", [P, P])
        itok = sb("itok", [P, TB, TOPK_SETS], I32)
        bq0 = sb("bq0", [P, KD])
        rw0 = sb("rw0", [P, KD, E0])
        ebias = sb("ebias", [P, E0])
        wq1 = sb("wq1", [P, KD, D])
        wo1 = sb("wo1", [P, KD, D])
        vecs = sb("vecs", [P, 4, KD])
        gg = sb("gg", [P, KD])
        wg1 = sb("wg1", [P, KD, E1])
        kT = sb("kT", [P, KD, B * NK])
        vbd = sb("vbd", [P, B, H // 2, 2 * (HD + 1)])
        hmask = sb("hmask", [P, H // 2])
        pmask = sb("pmask", [P, 2])
        mx1 = sb("mx1", [P, H])
        rec1 = sb("rec1", [P, H])
        ssq = sb("ssq", [P, NT])
        rq = sb("rq", [P, NT])
        nmr = sb("nmr", [P, NT])
        small8 = sb("small8", [P, 3, E1])
        place = sb("place", [P, 2, NT])
        column = sb("column", [P, 2, NT])
        inblock = sb("inblock", [P, 2, NT])
        rowval = sb("rowval", [P, 2, NT])
        weight = sb("weight", [P, 2, NT])
        weight_high = sb("weight_high", [P, 2, NT], F32R)
        upper = sb("upper", [P, P])
        token = sb("token", [P, NT])
        norow = sb("norow", [P, 1])
        slot_w = sb("slot_w", [P, NBLK])
        slot_row = sb("slot_row", [P, NBLK], I32)
        blkno = sb("blkno", [P, COLS])
        blk = sb("blk", [P, NBLK])
        blk_i = sb("blk_i", [P, NBLK], I32)
        m1 = sb("m1", [P, NT])

        ps = st.enter_context(nc.psum_tensor("ps", [P, 8 * 512], F32))

        def bank(i, n=1):
            return ps[:, 512 * i:512 * (i + n)]

        a_bias, a_exp, a_masked, a_max = sem("a_bias"), sem("a_exp"), sem("a_masked"), sem("a_max")
        a_mixed, a_picked, a_rec, a_route = sem("a_mixed"), sem("a_picked"), sem("a_rec"), sem("a_route")
        a_routed, a_scored, a_top, a_turned = sem("a_routed"), sem("a_scored"), sem("a_top"), sem("a_turned")
        a_wT, a_wts = sem("a_wT"), sem("a_wts")
        b_c3, b_cT, b_down, b_hidden = sem("b_c3"), sem("b_cT"), sem("b_down"), sem("b_hidden")
        b_high, b_low, b_max, b_mult = sem("b_high"), sem("b_low"), sem("b_max"), sem("b_mult")
        b_prod, b_routed, b_sig, b_silu = sem("b_prod"), sem("b_routed"), sem("b_sig"), sem("b_silu")
        b_spread, b_step, b_turned, b_up = sem("b_spread"), sem("b_step"), sem("b_turned"), sem("b_up")
        blk_ready, counted, fill_done, gg_ready = sem("blk_ready"), sem("counted"), sem("fill_done"), sem("gg_ready")
        kept, res_done, rest_done, slots_known = sem("kept"), sem("res_done"), sem("rest_done"), sem("slots_known")
        w_high, w_low, xn_stored = sem("w_high"), sem("w_low"), sem("xn_stored")
        c_att, c_attT, c_attTc, c_biased = sem("c_att"), sem("c_attT"), sem("c_attTc"), sem("c_biased")
        c_kbd, c_max, c_pT, c_probs = sem("c_kbd"), sem("c_max"), sem("c_pT"), sem("c_probs")
        c_proj, c_pv, c_q, c_qT = sem("c_proj"), sem("c_pv"), sem("c_q"), sem("c_qT")
        c_qt, c_rec, c_rq, c_scores = sem("c_qt"), sem("c_rec"), sem("c_rq"), sem("c_scores")
        c_shift, c_sq, c_ssq, c_turned = sem("c_shift"), sem("c_sq"), sem("c_ssq"), sem("c_turned")
        c_var = sem("c_var")
        d_added, d_columns, d_down, d_hT = sem("d_added"), sem("d_columns"), sem("d_down"), sem("d_hT")
        d_hidden, d_logits, d_max, d_onehot = sem("d_hidden"), sem("d_logits"), sem("d_max"), sem("d_onehot")
        d_placed, d_silu, d_step, d_turned = sem("d_placed"), sem("d_silu"), sem("d_step"), sem("d_turned")
        d_up, d_values, d_xt, d_xturned = sem("d_up"), sem("d_values"), sem("d_xt"), sem("d_xturned")
        d_y = sem("d_y")
        dve_const = sem("dve_const")
        in_bo, in_ctx, in_exp0, in_exp7 = sem("in_bo"), sem("in_ctx"), sem("in_exp0"), sem("in_exp7")
        in_ffn0, in_itok, in_kv, in_rest = sem("in_ffn0"), sem("in_itok"), sem("in_kv"), sem("in_rest")
        in_set0, in_x0, in_x1 = sem("in_set0"), sem("in_x0"), sem("in_x1")
        k_copied, k_diag, k_pow, k_psum = sem("k_copied"), sem("k_diag"), sem("k_pow"), sem("k_psum")
        k_scaled, k_spread, k_sum, k_var = sem("k_scaled"), sem("k_spread"), sem("k_sum"), sem("k_var")
        ln_copied, ln_mv, ln_rows, ln_rstd = sem("ln_copied"), sem("ln_mv"), sem("ln_rows"), sem("ln_rstd")
        ln_stats, ln_turned, ln_var = sem("ln_stats"), sem("ln_turned"), sem("ln_var")
        pool_fill, pool_slot, pool_step = sem("pool_fill"), sem("pool_slot"), sem("pool_step")
        s_mask = sem("s_mask")
        v_psum, v_ready = sem("v_psum"), sem("v_ready")
        x_new = sem("x_new")
        xr_rows, xr_shift = sem("xr_rows"), sem("xr_shift")

        xn_rows = nc.dram_tensor("xn_rows", ((NT + 1) * P, D), F32, kind="Internal").ap()
        xg_in = [sem("xg_in0"), sem("xg_in1")]
        XA, XB, XC = NT, NT + NT // 2, 2 * NT + NT // 2
        NG = NT // 4

        def each(eng, n, lead, step, body):
            for i in range(lead):
                body(i, i)
            with eng.Fori(0, (n - lead) // step) as turn:
                for j in range(step):
                    body(turn * step + (lead + j), lead + j)

        block = st.enter_context(nc.Block())

        @block.sync
        def _(sp):
            x_v = x_in.rearrange("b (j p) d -> p (b j) d", p=P)
            half = 2 * TB
            rows_v = out_rows.rearrange("(t p) d -> p t d", p=P)
            sp.dma_start(x_sb[:, 0:half, :], x_v[:, 0:half, :]).then_inc(in_x0, 16)
            sp.dma_start(x_sb[:, half:NT, :], x_v[:, half:NT, :]).then_inc(in_x1, 16)
            sp.dma_start(wq0, wq0_in.rearrange("(k p) n -> p k n", p=P)).then_inc(in_set0, 16)
            sp.dma_start(descT, descT_in.rearrange("(k p) n -> p k n", p=P)).then_inc(in_set0, 16)
            sp.dma_start(bq0[:, :], bq0_in).then_inc(in_set0, 16)
            sp.dma_start(itok[:, :, :], itok_in.rearrange("(j p) k -> p j k", p=P)).then_inc(in_itok, 16)
            sp.dma_start(ctx_sb, ctx_in.rearrange("b n d -> n b d")).then_inc(in_ctx, 16)
            for k in range(KD):
                for m, src in enumerate((wk1_in, wv1_in)):
                    sp.dma_start(wkv[:, k, m, :], src[k * P:(k + 1) * P, :]).then_inc(in_kv, 16)
                for r in range(2):
                    sp.dma_start(ctxT[:, k, :, r, :], ctxT_in[k * P:(k + 1) * P, :].rearrange(
                        "p (b n) -> p b n", b=B)).then_inc(in_kv, 16)
            for m, src in enumerate((bq1_in, gq1_in, bk1_in, gk1_in)):
                sp.dma_start(vecs[:, m, :], src).then_inc(in_kv, 16)
            sp.dma_start(bv_row, bv1_in.unsqueeze(0)).then_inc(in_kv, 16)
            sp.dma_start(rw0[:, :, :], rw0_in.rearrange("(k p) n -> p k n", p=P)).then_inc(in_rest, 16)
            sp.dma_start(ebias[:, :], ebias_in.partition_broadcast(P)).then_inc(in_rest, 16)
            for k in range(KD):
                sp.dma_start(gu0[:, k, :], gu0_in[k * P:(k + 1) * P, :]).then_inc(in_ffn0, 16)
            sp.dma_start(dn0, dn0_in).then_inc(in_ffn0, 16)
            sp.dma_start(wq1[:, :, :], wq1_in.rearrange("(k p) n -> p k n", p=P)).then_inc(in_rest, 16)
            sp.dma_start(wo1[:, :, :], wo1_in.rearrange("(k p) n -> p k n", p=P)).then_inc(in_rest, 16)
            sp.dma_start(wg1[:, :, :], wg1_in.rearrange("(k p) n -> p k n", p=P)).then_inc(in_rest, 16)
            xn_v = xn_rows.rearrange("(t p) d -> p t d", p=P)
            sp.wait_ge(pool_fill, 1)
            sp.dma_start(xn_v[:, NT, :], filler).then_inc(fill_done, 16)
            sp.dma_start(rows_v[:, NT, :], filler).then_inc(rest_done, 16)
            sp.wait_ge(b_down, 4 * C0)
            sp.dma_start(bo_rows, bo1_in.partition_broadcast(P)).then_inc(in_bo, 16)
            for e in range(7):
                sp.dma_start(wexp[:, e * WE:(e + 1) * WE], wexp_in[:, e, :]).then_inc(in_exp0, 16)
            sp.wait_ge(x_new, XC)
            sp.dma_start(wexp[:, last:last + WE], wexp_in[:, 7, :]).then_inc(in_exp7, 16)
            sp.dma_start(rows_v[:, 0:NT, :], x_sb[:, :, :]).then_inc(res_done, 16)
            for q in range(NT // 4):
                sp.wait_ge(xr_rows, 4 * (q + 1))
                sp.dma_start(xn_v[:, 4 * q:4 * (q + 1), :], xr[:, 4 * q:4 * (q + 1), :]).then_inc(xn_stored, 16)
            sp.wait_ge(rest_done, 16)
            sp.wait_ge(fill_done, 16)
            sp.wait_ge(res_done, 16)
            sp.wait_ge(xn_stored, 16 * NT // 4)
            sp.wait_ge(d_added, 16 * NBLK)

        @block.gpsimd
        def _(pool):
            pool.memset(ident[:, :], 0.0).then_inc(pool_step, 1)
            pool.memset(ones[:, :], 1.0).then_inc(pool_step, 1)
            pool.memset(hmask[:, :], 1.0).then_inc(pool_step, 1)
            pool.memset(mhalf[:, :], -0.5).then_inc(pool_step, 1)
            pool.iota(iota[:, :], [[1, P]], base=0, channel_multiplier=0,
                      allow_small_or_imprecise_dtypes=True).then_inc(pool_step, 1)
            pool.wait_ge(pool_step, 5)
            pool.affine_select(out=ident[:, :], in_=ident[:, :], compare_op=ALU.not_equal, fill=1.0,
                               base=0, pattern=[[-1, P]], channel_multiplier=1).then_inc(pool_step, 1)
            pool.affine_select(out=hmask[:, :], in_=hmask[:, :], compare_op=ALU.is_ge, fill=0.0,
                               base=0, pattern=[[-HD, H // 2]], channel_multiplier=1).then_inc(pool_step, 1)
            pool.wait_ge(pool_step, 7)
            pool.affine_select(out=hmask[:, :], in_=hmask[:, :], compare_op=ALU.is_ge, fill=0.0,
                               base=HD - 1, pattern=[[HD, H // 2]], channel_multiplier=-1).then_inc(pool_step, 1)
            pool.tensor_copy(identb[:, :], ident[:, :]).then_inc(pool_step, 1)
            pool.memset(filler, 0.0).then_inc(pool_fill, 1)
            pool.memset(upper[:, :], 1.0).then_inc(pool_slot, 1)
            pool.iota(token[:, :], [[P, NT]], base=-NT * P, channel_multiplier=1,
                      allow_small_or_imprecise_dtypes=True).then_inc(pool_slot, 1)
            pool.iota(norow[:, :], [[0, 1]], base=NT * P, channel_multiplier=1,
                      allow_small_or_imprecise_dtypes=True).then_inc(pool_slot, 1)
            pool.iota(blkno[:, :], [[1, COLS]], base=0, channel_multiplier=0,
                      allow_small_or_imprecise_dtypes=True).then_inc(pool_slot, 1)
            pool.wait_ge(pool_slot, 1)
            pool.affine_select(out=upper[:, :], in_=upper[:, :], compare_op=ALU.is_ge, fill=0.0,
                               base=-1, pattern=[[1, P]], channel_multiplier=-1).then_inc(pool_slot, 1)

            def power_of(norm, b):
                pool.wait_ge(ln_var, norm * B + b + 1)
                pool.tensor_tensor(rstd[:, bass.ds(b * TB, TB)], ve[:, bass.ds(b * TB, TB)],
                                   mhalf[:, 0:1].broadcast_to([P, TB]), ALU.pow).then_inc(ln_rstd, 1)

            def power(norm):
                each(pool, B, 0, 2, lambda b, k: power_of(norm, b))

            pool.wait_ge(pool_step, 9)
            power(0)
            pool.memset(spread, 0.0).then_inc(pool_step, 1)
            v = spread.rearrange("p (e u) -> p e u", e=E0)
            for part in range(3):
                pool.wait_ge(pool_step, 10 + part)
                pool.affine_select(out=v, in_=v, compare_op=ALU.not_equal, fill=1.0, base=-32 * part,
                                   pattern=[[-1, E0], [0, I0]], channel_multiplier=1).then_inc(pool_step, 1)
            for k in range(KD):
                pool.wait_ge(w_high, k + 1)
                pool.tensor_tensor(gu_low[:, k, :], gu0[:, k, :], gu_high[:, k, :].bitcast(F32),
                                   ALU.subtract).then_inc(w_low, 1)
            pool.wait_ge(k_var, 1)
            pool.tensor_tensor(krst, kvar, mhalf[:, 0:1].broadcast_to([P, B * NK // P]), ALU.pow).then_inc(k_pow, 1)
            power(1)

            def low_rows(b):
                pool.wait_ge(b_routed, b + 1)
                pair = slice(b * S, (b + 1) * S)
                pool.tensor_tensor(xn_low[:, :, pair], xn_full[:, :, pair], xn_high[:, :, pair].bitcast(F32),
                                   ALU.subtract).then_inc(b_low, 1)
            for b in range(2):
                low_rows(b)
            pool.wait_ge(w_high, KD + 1)
            pool.tensor_tensor(dn_low, dn0, dn_high.bitcast(F32), ALU.subtract).then_inc(w_low, 1)
            for b in range(2, B):
                low_rows(b)
            power(2)
            def diagonal(b, k):
                if k >= 2:
                    pool.wait_ge(c_scores, (b - 1) * TB)
                for m in range(KD):
                    pool.tensor_tensor(
                        kbd[:, k % 2, m * 512:(m + 1) * 512].rearrange("p (h n) -> p h n", h=H // 2),
                        kT[:, m:m + 1, bass.ds(b * NK, NK)].broadcast_to([P, H // 2, NK]),
                        hmask[:, :].unsqueeze(2).broadcast_to([P, H // 2, NK]),
                        ALU.mult).then_inc(c_kbd, 1)
            pool.wait_ge(x_new, XB)
            pool.wait_ge(k_scaled, KD)
            for b in range(2):
                diagonal(b, b)
            pool.wait_ge(in_bo, 16)

            def add_bias(b, k):
                pool.wait_ge(ln_rows, 2 * B + b + 1)
                o = x_sb[:, bass.ds(b * TB, TB), :]
                pool.tensor_tensor(o, o, bo_rows.unsqueeze(1).broadcast_to([P, TB, D]), ALU.add).then_inc(c_biased, 1)
            each(pool, B, 0, 2, add_bias)
            pool.wait_ge(c_var, 1)
            pool.tensor_tensor(rq[:, :], ssq[:, :], mhalf[:, 0:1].broadcast_to([P, NT]), ALU.pow).then_inc(c_rq, 1)
            for b in range(2, 4):
                diagonal(b, b)
            power_of(3, 0)
            with pool.Fori(2, B // 2) as pair:
                for k in range(2):
                    diagonal(pair * 2 + k, 2 + k)
                    power_of(3, pair * 2 + k - 3)
            for b in range(B - 3, B):
                power_of(3, b)
            for n in range(NSRC // BATCH):
                def over(a):
                    return a[:, :, :].bitcast(F32).rearrange("p w t -> p (w t)")[:, n * BATCH:(n + 1) * BATCH].unsqueeze(
                        2).broadcast_to([P, BATCH, COLS])
                pool.wait_ge(d_columns, n + 1)
                if n >= 2:
                    pool.wait_ge(d_placed, n - 1)
                for m, a in enumerate((rowval, weight_high, weight)):
                    pool.tensor_tensor(placed[:, n % 2, :, m * COLS:(m + 1) * COLS], incolumn[:, n % 2, :, :],
                                       over(a), ALU.mult).then_inc(d_values, 1)

            def fetch(i):
                if i >= 2:
                    pool.wait_ge(d_xturned, i - 1)
                pool.indirect_dma_start(
                    out=xg[:, i % 2, :], out_offset=None, in_=xn_rows,
                    in_offset=bass.IndirectOffsetOnAxis(ap=slot_row[:, i:i + 1], axis=0)).then_inc(xg_in[i % 2], 16)

            def add_rows(i):
                pool.wait_ge(d_y, i + 1)
                if i:
                    pool.wait_ge(d_added, 16 * i)
                pool.indirect_dma_start(
                    out=out_rows, out_offset=bass.IndirectOffsetOnAxis(ap=slot_row[:, i:i + 1], axis=0),
                    in_=yb[:, i % 2, :], in_offset=None, compute_op=ALU.add).then_inc(d_added, 16)

            pool.wait_ge(fill_done, 16)
            pool.wait_ge(xn_stored, 16 * NT // 4)
            pool.wait_ge(slots_known, 2)
            for i in range(4):
                fetch(i)
            pool.wait_ge(res_done, 16)
            pool.wait_ge(rest_done, 16)
            for i in range(NBLK):
                add_rows(i)
                if i + 4 < NBLK:
                    fetch(i + 4)

        @block.scalar
        def _(act):
            def copy_batch(norm, b, k):
                act.wait_ge(ln_turned, norm * B + b + 1)
                act.activation(xnT[:, :, bass.ds(b * S, S)],
                               bank(bank_of[norm] or k % 2).rearrange("p (k n) -> p k n", k=KD),
                               ACT.Copy).then_inc(ln_copied, 1)

            def copy_rows(norm):
                each(act, B, 0, 2, lambda b, k: copy_batch(norm, b, k))

            act.wait_ge(a_route, 1)
            act.activation(route0, bank(6)[:, 0:KD * NK].rearrange("p (k n) -> p k n", k=KD),
                           ACT.Copy, scale=1.0 / math.sqrt(D)).then_inc(a_routed, 1)
            act.activation(brow, bank(6)[0:1, 256:256 + NK], ACT.Copy,
                           scale=1.0 / math.sqrt(D)).then_inc(a_routed, 1)
            copy_rows(0)
            act.wait_ge(in_ffn0, 48)
            for k in range(KD):
                act.activation(gu_high[:, k, :], gu0[:, k, :], ACT.Copy).then_inc(w_high, 1)
            act.wait_ge(k_psum, 1)
            act.wait_ge(in_kv, 16 * 13)
            for m in range(KD):
                act.activation(kT[:, m, :], bank(6 + m), ACT.Identity, bias=vecs[:, 2, m:m + 1]).then_inc(k_copied, 1)
                act.activation(ksq[:, m, :], bank(6 + m), ACT.Square, bias=vecs[:, 2, m:m + 1]).then_inc(k_copied, 1)

            with act.Fori(0, B) as b:
                act.wait_ge(a_top, b * 2 + 2)
                for j in range(TB):
                    act.activation(ex[:, b * TB + j, :], ms[:, b * TB + j, :], ACT.Exp,
                                   bias=negm[:, bass.ds(b * TB + j, 1)]).then_inc(a_exp, 1)
            for q in range(NT // 4):
                act.wait_ge(a_turned, q + 1)
                act.activation(wT[:, q * 512:(q + 1) * 512], bank(4 + q % 2)[0:NK, :], ACT.Copy).then_inc(a_wT, 1)
            act.activation(dn_high, dn0, ACT.Copy).then_inc(w_high, 1)

            def copy_parts(b, k):
                act.wait_ge(ln_turned, B + b + 1)
                rows = bank(k % 2).rearrange("p (k n) -> p k n", k=KD)
                act.activation(xn_full[:, :, bass.ds(b * S, S)], rows, ACT.Copy)
                act.activation(xn_high[:, :, bass.ds(b * S, S)], rows, ACT.Copy).then_inc(ln_copied, 1)
            each(act, B, 0, 2, copy_parts)
            act.wait_ge(b_routed, B)
            act.activation(sc0, bank(3)[:, 0:NT * E0].rearrange("p (t e) -> p t e", t=NT), ACT.Sigmoid).then_inc(b_sig, 1)
            for g in range(4):
                act.wait_ge(b_turned, g + 1)
                act.activation(cT[:, g * 512:(g + 1) * 512], bank(4 + g % 2).bitcast(BF16)[0:96, 0:512],
                               ACT.Copy).then_inc(b_cT, 1)

            def silu_group(g, k):
                for c in range(C0):
                    i, rows = g * C0 + c, P if c < C0 - 1 else I0
                    act.wait_ge(b_up, i + 1)
                    if k or c >= 2:
                        act.wait_ge(b_prod, i if c == 0 else i - 1)
                    act.activation(sg0[0:rows, c % 2, :], bank(c % 2)[0:rows, :], ACT.Silu).then_inc(b_silu, 1)
                    if k and c in (9, 11):
                        copy_batch(2, g * 2 - 2 + (c - 9) // 2, 0)
            each(act, NG, 1, 1, silu_group)
            act.wait_ge(in_rest, 16 * 5)

            def queries(b, k):
                act.wait_ge(c_q, b + 1)
                if k >= 2:
                    act.wait_ge(c_ssq, b - 1)
                for m in range(KD):
                    act.activation(sqT[:, k % 2, m, :], bank(2 + k % 2)[:, m * S:(m + 1) * S], ACT.Square,
                                   bias=vecs[:, 0, m:m + 1]).then_inc(c_sq, 1)
                    act.activation(xnT[:, m, bass.ds(b * S, S)], bank(2 + k % 2)[:, m * S:(m + 1) * S],
                                   ACT.Identity, bias=vecs[:, 0, m:m + 1]).then_inc(c_qT, 1)
            for b in range(2):
                queries(b, b)
            for b in range(B - 2, B):
                copy_batch(2, b, 0)
            with act.Fori(1, B // 2) as pair:
                for j in range(2):
                    queries(pair * 2 + j, 2 + j)

            def pick_tile(t, k):
                if k >= 2:
                    act.wait_ge(c_scores, t - 1)
                act.activation(qt[:, k % 2, :, :], xnT[:, :, bass.ds(t * P, P)], ACT.Copy).then_inc(c_qt, 1)

            def exp_scores(t, k):
                act.wait_ge(c_shift, t + 1)
                if k == 0:
                    act.wait_ge(c_rq, 1)
                if k >= 1:
                    act.wait_ge(c_turned, t)
                act.activation(probs, shift, ACT.Exp, scale=rq[:, bass.ds(t, 1)]).then_inc(c_probs, 1)

            def copy_probs(t, k):
                act.wait_ge(c_turned, t + 1)
                if k >= 2:
                    act.wait_ge(c_pv, t - 1)
                act.activation(pT[:, k % 2, :, :], bank(2, 2).rearrange("p (c n) -> p c n", c=8),
                               ACT.Copy).then_inc(c_pT, 1)

            def copy_att(t, k):
                act.wait_ge(c_attT, t + 1)
                act.activation(attT, bank(5)[:, 0:D].rearrange("p (k n) -> p k n", k=KD), ACT.Copy).then_inc(c_attTc, 1)

            act.wait_ge(c_qT, B * KD)

            def softmax_tile(t, k, more=True):
                if k >= 2:
                    copy_att(t - 2, k - 2)
                if k >= 1:
                    copy_probs(t - 1, k - 1)
                if more:
                    pick_tile(t + 1, k + 1)
                exp_scores(t, k)
            pick_tile(0, 0)
            for t in range(4):
                softmax_tile(t, t)
            with act.Fori(0, NT // 4 - 2) as quad:
                for j in range(4):
                    softmax_tile(quad * 4 + (4 + j), 4 + j)
                    if j % 2:
                        copy_batch(3, quad * 2 + j // 2, j // 2)
            for t in range(NT - 4, NT):
                softmax_tile(t, 4 + t % 4, t < NT - 1)
                if t % 2:
                    copy_batch(3, (t - 5) // 2, 0)
            copy_att(NT - 2, 2)
            copy_probs(NT - 1, 3)
            copy_att(NT - 1, 3)
            copy_batch(3, B - 2, 0)
            copy_batch(3, B - 1, 1)

            act.wait_ge(d_logits, 1)
            act.wait_ge(xr_shift, 1)
            with act.Fori(0, NT) as t:
                act.activation(xr[:, t, 0:D], x_sb[:, t, :], ACT.Identity, bias=nmr[:, bass.ds(t, 1)],
                               scale=rstd[:, bass.ds(t, 1)]).then_inc(xr_rows, 1)

            def copy_slot_rows(i, k):
                act.wait_ge(d_xturned, i + 1)
                act.activation(xt1[:, k % 2, :, :], bank(7)[:, 0:D].rearrange("p (k n) -> p k n", k=KD),
                               ACT.Copy).then_inc(d_xt, 1)

            def block_act(i, k, more=True):
                act.wait_ge(d_up, i + 1)
                if k:
                    act.wait_ge(d_hidden, i)
                act.activation(sg1.rearrange("p (a n) -> p a n", a=2),
                               bank(0, 2).rearrange("p (a n) -> p a n", a=2)[:, :, 0:HALF1],
                               ACT.Silu).then_inc(d_silu, 1)
                if more:
                    copy_slot_rows(i + 1, k + 1)
                act.wait_ge(d_turned, i + 1)
                act.activation(hT[:, 0:C1 - 1, :], bank(4, 2)[:, 0:(C1 - 1) * P].rearrange("p (c n) -> p c n", n=P),
                               ACT.Copy).then_inc(d_hT, 1)
                act.activation(hT[0:64, C1 - 1, :], bank(4, 2)[0:64, (C1 - 1) * P:C1 * P], ACT.Copy).then_inc(d_hT, 1)
            copy_slot_rows(0, 0)
            each(act, NBLK - 1, 2, 2, block_act)
            block_act(NBLK - 1, 2, False)

        @block.tensor
        def _(pe):
            def turn_rows(norm, b, k):
                pe.wait_ge(ln_rows, norm * B + b + 1)
                if norm >= 2:
                    pe.wait_ge(ln_copied, norm * B + b)
                elif k >= 2:
                    pe.wait_ge(ln_copied, norm * B + b - 1)
                for m in range(KD):
                    for j in range(TB):
                        mm = pe.transpose(bank(bank_of[norm] or k % 2)[:, m * S + j * P:m * S + (j + 1) * P],
                                          xn_of[norm][:, k % 2, j, m * P:(m + 1) * P], ident[:, :])
                mm.then_inc(ln_turned, 1)

            pe.wait_ge(pool_step, 9)
            pe.wait_ge(in_set0, 48)
            for m in range(KD):
                for k in range(KD):
                    pe.matmul(bank(6)[:, m * NK:(m + 1) * NK], wq0[:, k, m * P:(m + 1) * P], descT[:, k, :],
                              start=(k == 0), stop=(k == KD - 1))
            for k in range(KD):
                mm = pe.matmul(bank(6)[0:1, 256:256 + NK], bq0[:, k:k + 1], descT[:, k, :],
                               start=(k == 0), stop=(k == KD - 1))
            mm.then_inc(a_route, 1)
            pe.wait_ge(a_routed, 2)
            pe.matmul(bank(7)[:, 0:NK], ones[0:1, :], brow, start=True, stop=True).then_inc(a_bias, 1)
            for b in range(B + 1):
                if b < B:
                    turn_rows(0, b, b)
                if b:
                    pe.wait_ge(ln_copied, b)
                    for t in range((b - 1) * TB, b * TB):
                        o = bank(2, 2)[:, t * NK:(t + 1) * NK]
                        for k in range(KD):
                            mm = pe.matmul(o, xnT[:, k, t * P:(t + 1) * P], route0[:, k, :],
                                           start=(k == 0), stop=(k == KD - 1))
                    mm.then_inc(a_scored, 1)
            pe.wait_ge(in_kv, 16 * 13)
            pe.wait_ge(s_mask, 3 + TB * TOPK_SETS)
            for m in range(KD):
                for k in range(KD):
                    mm = pe.matmul(bank(6 + m), wkv[:, k, 0, m * P:(m + 1) * P], ctxT[:, k, :, 0, :],
                                   start=(k == 0), stop=(k == KD - 1))
            mm.then_inc(k_psum, 1)
            for b in range(B):
                o = bank(4 + b % 2)[:, 0:D]
                if b >= 2:
                    pe.wait_ge(v_ready, 2 * (b - 1))
                for k in range(KD):
                    pe.matmul(o, ctxT[:, k, b, :, :], wkv[:, k, 1, :], start=(k == 0), stop=False)
                pe.matmul(o, ones[0:1, :], bv_row, start=False, stop=True).then_inc(v_psum, 1)
            pe.wait_ge(k_copied, 4)
            for q in range(B * NK // P):
                for k in range(KD):
                    mm = pe.matmul(bank(0)[:, q:q + 1], ksq[:, k, q * P:(q + 1) * P], ones[:, 0:1],
                                   start=(k == 0), stop=(k == KD - 1))
            mm.then_inc(k_sum, 1)
            pe.wait_ge(v_ready, 2 * B)
            for q in range(NT // 4):
                pe.wait_ge(a_wts, 4 * (q + 1))
                if q >= 2:
                    pe.wait_ge(a_wT, q - 1)
                for t in range(4 * q, 4 * q + 4):
                    mm = pe.transpose(bank(4 + q % 2)[0:NK, (t % 4) * P:(t % 4 + 1) * P], ms[:, t, :], ident[:, :])
                mm.then_inc(a_turned, 1)
            pe.wait_ge(k_diag, B * NK // P)
            for q in range(B * NK // P):
                mm = pe.matmul(bank(1)[:, q * P:(q + 1) * P], ones[:, :], kdiag[:, q, :], start=True, stop=True)
            mm.then_inc(k_spread, 1)

            def mix(b):
                pe.wait_ge(a_wT, b // 2 + 1)
                if b >= 2:
                    pe.wait_ge(x_new, TB * (b - 1))
                for j in range(TB):
                    t = b * TB + j
                    mm = pe.matmul(bank(6 + b % 2)[:, j * D:(j + 1) * D], wT[:, t * P:(t + 1) * P], ctx_sb[:, b, :],
                                   start=True, stop=True)
                mm.then_inc(a_mixed, 1)

            def route(b):
                pe.wait_ge(ln_copied, B + b + 1)
                for t in range(b * TB, (b + 1) * TB):
                    for k in range(KD):
                        mm = pe.matmul(bank(3)[:, t * E0:(t + 1) * E0], xn_full[:, k, t * P:(t + 1) * P], rw0[:, k, :],
                                       start=(k == 0), stop=(k == KD - 1))
                mm.then_inc(b_routed, 1)

            pe.wait_ge(in_ctx, 16)
            pe.wait_ge(in_rest, 16 * 5)
            pe.wait_ge(k_scaled, KD)
            for b in range(B + 3):
                if b < B:
                    mix(b)
                if 2 <= b < B + 2:
                    turn_rows(1, b - 2, b - 2)
                if b >= 3:
                    route(b - 3)
            pe.wait_ge(w_low, KD)
            pe.wait_ge(b_low, 2)

            def in_parts(out, high, low, rows_high, rows_low, start, stop):
                pe.matmul(out, high, rows_high, start=start, stop=False, skip_group_check=True)
                pe.matmul(out, high, rows_low, start=False, stop=False, skip_group_check=True)
                return pe.matmul(out, low, rows_high, start=False, stop=stop, skip_group_check=True)

            def up0(g, c, k):
                i, rows = g * C0 + c, P if c < C0 - 1 else I0
                if k or c >= 2:
                    pe.wait_ge(b_prod, i if c == 0 else i - 1)
                for part in range(2):
                    for h in range(KD):
                        cols = slice(c * 2 * P + part * rows, c * 2 * P + (part + 1) * rows)
                        mm = in_parts(bank(2 * part + c % 2)[0:rows, :], gu_high[:, h, cols], gu_low[:, h, cols],
                                      xn_high[:, h, bass.ds(g * 512, 512)], xn_low[:, h, bass.ds(g * 512, 512)],
                                      h == 0, h == KD - 1)
                mm.then_inc(b_up, 1)

            def down0(g, c, k):
                i, rows = g * C0 + c, P if c < C0 - 1 else I0
                if c == 0 and k:
                    pe.wait_ge(x_new, g * 2 + XA)
                for j in range(4):
                    if j % 2 == 0:
                        pe.wait_ge(b_hidden, i * 2 + 1 + j // 2)
                    cols = slice(j * P, (j + 1) * P)
                    mm = in_parts(bank(6, 2)[:, j * D:(j + 1) * D], h_high[0:rows, c % 2, cols], h_low[0:rows, c % 2, cols],
                                  dn_high[0:rows, c, :], dn_low[0:rows, c, :], c == 0 and j % 2 == 0, c == C0 - 1)
                mm.then_inc(b_down, 1)

            def ffn0_group(g, k):
                if k:
                    up0(g, 0, k)
                    down0(g - 1, C0 - 1, k)
                for c in range(C0 - 1):
                    if k or c >= 1:
                        pe.wait_ge(b_mult, g * (C0 - 1) + c)
                    pe.matmul(bank(4), spread[:, c * P:(c + 1) * P], cT[:, bass.ds(g * 512, 512)],
                              start=True, stop=True).then_inc(b_spread, 1)
                    up0(g, c + 1, k)
                    down0(g, c, k)
                    if k and c in (8, 10):
                        turn_rows(2, g * 2 - 2 + (c - 8) // 2, (c - 8) // 2)

            up0(0, 0, 0)
            pe.wait_ge(b_c3, 3)
            for g in range(NG):
                if g >= 2:
                    pe.wait_ge(b_cT, g - 1)
                for t in range(4 * g, 4 * g + 4):
                    mm = pe.transpose(bank(4 + g % 2).bitcast(BF16)[0:96, (t % 4) * P:(t % 4 + 1) * P],
                                      c3[:, t, :], identb[:, :])
                mm.then_inc(b_turned, 1)
            pe.wait_ge(b_cT, NG)
            pe.wait_ge(b_sig, 1)
            pe.wait_ge(pool_step, 13)
            pe.wait_ge(w_low, KD + 1)
            pe.wait_ge(b_low, B)
            each(pe, NG, 1, 1, ffn0_group)
            down0(NG - 1, C0 - 1, 1)


            def queries(b, k):
                pe.wait_ge(ln_copied, 2 * B + b + 1)
                if k >= 2:
                    pe.wait_ge(c_qT, (b - 1) * KD)
                for m in range(KD):
                    for h in range(KD):
                        mm = pe.matmul(bank(2 + k % 2)[:, m * S:(m + 1) * S], wq1[:, h, m * P:(m + 1) * P],
                                       xnT[:, h, bass.ds(b * S, S)], start=(h == 0), stop=(h == KD - 1))
                mm.then_inc(c_q, 1)

            def squares(b, k):
                pe.wait_ge(c_sq, b * KD + KD)
                for j in range(TB):
                    for m in range(KD):
                        mm = pe.matmul(bank(7)[:, bass.ds(b * TB + j, 1)], sqT[:, k % 2, m, j * P:(j + 1) * P],
                                       ones[:, 0:1], start=(m == 0), stop=(m == KD - 1))
                mm.then_inc(c_ssq, 1)

            def queries_squares(b, k):
                queries(b, k)
                if k == 1:
                    pe.wait_ge(x_new, XB)
                if k >= 1:
                    squares(b - 1, k - 1)
            pe.wait_ge(in_rest, 16 * 5)
            for b in range(2):
                queries_squares(b, b)
            for b in range(B - 2, B):
                turn_rows(2, b, b % 2)
            with pe.Fori(1, B // 2) as pair:
                for j in range(2):
                    queries_squares(pair * 2 + j, 2 + j)
            squares(B - 1, 1)

            def scores(t, k):
                pe.wait_ge(c_qt, t + 1)
                if k % TB == 0:
                    pe.wait_ge(c_kbd, t + KD)
                if k:
                    pe.wait_ge(c_shift, t)
                for m in range(KD):
                    mm = pe.matmul(bank(m), qt[:, k % 2, m, :], kbd[:, (k // TB) % 2, m * 512:(m + 1) * 512],
                                   start=True, stop=True)
                mm.then_inc(c_scores, 1)

            def turn_probs(t, k):
                pe.wait_ge(c_probs, t + 1)
                if k:
                    pe.wait_ge(c_pT, t)
                for c in range(8):
                    mm = pe.transpose(bank(2, 2)[:, c * P:(c + 1) * P], probs[:, c * P:(c + 1) * P], ident[:, :])
                mm.then_inc(c_turned, 1)

            def values(t, k, b):
                pe.wait_ge(c_pT, t + 1)
                if k:
                    pe.wait_ge(c_att, t)
                for c in range(8):
                    mm = pe.matmul(bank(4)[:, c * 34:(c + 1) * 34], pT[:, k % 2, c, :], vbd[:, b, c, :],
                                   start=True, stop=True)
                mm.then_inc(c_pv, 1)

            def turn_att(t, k):
                pe.wait_ge(c_att, t + 1)
                if k:
                    pe.wait_ge(c_attTc, t)
                for m in range(KD):
                    mm = pe.transpose(bank(5)[:, m * P:(m + 1) * P], att[:, m * P:(m + 1) * P], ident[:, :])
                mm.then_inc(c_attT, 1)

            def project(t, k):
                pe.wait_ge(c_attTc, t + 1)
                if k:
                    pe.wait_ge(x_new, t + XB)
                for m in range(KD):
                    mm = pe.matmul(bank(6)[:, 0:D], attT[:, m, :], wo1[:, m, :], start=(m == 0), stop=(m == KD - 1))
                mm.then_inc(c_proj, 1)

            def attend(t, k, base=None, at_tile=0):
                b0 = 0 if base is None else base
                if k < NT:
                    scores(t, k)
                if k >= 2:
                    turn_att(t - 2, k - 2)
                if k >= 1:
                    turn_probs(t - 1, k - 1)
                if k >= 2:
                    project(t - 2, k - 2)
                if k >= 1:
                    values(t - 1, k - 1, b0 + (at_tile - 1) // TB)

            for t in range(4):
                attend(t, t, 0, t)
            with pe.Fori(0, B // 2 - 1) as pair:
                for j in range(4):
                    attend(pair * 4 + (4 + j), 4 + j, pair * 2 + 2, j)
                    if j % 2:
                        turn_rows(3, pair * 2 + j // 2, j // 2)
            turn_att(NT - 2, 2)
            turn_probs(NT - 1, 3)
            project(NT - 2, 2)
            values(NT - 1, 3, B - 1)
            def route1(b):
                pe.wait_ge(ln_copied, 3 * B + b + 1)
                for t in range(b * TB, (b + 1) * TB):
                    for h in range(KD):
                        mm = pe.matmul(bank(0)[:, t * E1:(t + 1) * E1], xnT[:, h, t * P:(t + 1) * P], wg1[:, h, :],
                                       start=(h == 0), stop=(h == KD - 1))
                if b == B - 1:
                    mm.then_inc(d_logits, 1)
            pe.wait_ge(c_shift, NT)
            route1(0)
            turn_att(NT - 1, 3)
            route1(1)
            project(NT - 1, 3)
            turn_rows(3, B - 2, 0)
            route1(2)
            route1(3)
            turn_rows(3, B - 1, 1)
            for b in range(4, B):
                route1(b)
            pe.wait_ge(pool_slot, 5)
            pe.wait_ge(kept, 1)
            pe.matmul(bank(4)[:, 0:NT * E1], upper[:, :], keep.rearrange("p t e -> p (t e)"), start=True, stop=True)
            pe.matmul(bank(5)[:, 0:NT * E1], ones[:, :], keep.rearrange("p t e -> p (t e)"),
                      start=True, stop=True).then_inc(counted, 1)

            for n in range(NSRC):
                if n % BATCH == 0:
                    pe.wait_ge(d_onehot, n // BATCH + 1)
                    pe.wait_ge(d_values, 3 * (n // BATCH + 1))
                mm = pe.matmul(bank(6)[:, 0:3 * COLS], onehot[:, n // BATCH % 2, n % BATCH, :],
                               placed[:, n // BATCH % 2, n % BATCH, :], start=(n == 0), stop=(n == NSRC - 1))
                if n % BATCH == BATCH - 1:
                    mm.then_inc(d_placed, 1)

            def turn_slots(i, k):
                pe.wait_ge(xg_in[k % 2], ((i // 2) * 16 if isinstance(i, int) else (i - k % 2) * 8) + 16)
                if k:
                    pe.wait_ge(d_xt, i)
                for h in range(KD):
                    mm = pe.transpose(bank(7)[:, h * P:(h + 1) * P], xg[:, k % 2, h * P:(h + 1) * P], ident[:, :])
                mm.then_inc(d_xturned, 1)

            def up1(i, k, expert):
                pe.wait_ge(d_xt, i + 1)
                if k:
                    pe.wait_ge(d_hidden, i)
                for part in range(2):
                    for half in range(2):
                        for h in range(KD):
                            col = h * W13 + part * I1 + half * HALF1
                            mm = pe.matmul(bank(2 * part + half)[:, 0:HALF1], xt1[:, k % 2, h, :],
                                           wexp[:, bass.ds(expert + col, HALF1)], start=(h == 0), stop=(h == KD - 1))
                mm.then_inc(d_up, 1)

            def turn_hidden(i, k):
                pe.wait_ge(d_hidden, i + 1)
                if k:
                    pe.wait_ge(d_hT, i * 2)
                for c in range(C1):
                    n = min(P, I1 - c * P)
                    mm = pe.transpose(bank(4, 2)[0:n, c * P:(c + 1) * P], h1[:, c * P:c * P + n], ident[:, :])
                mm.then_inc(d_turned, 1)

            def down1(i, k, expert):
                pe.wait_ge(d_hT, i * 2 + 2)
                if k:
                    pe.wait_ge(d_y, i)
                for c in range(C1):
                    n = min(P, I1 - c * P)
                    mm = pe.matmul(bank(6)[:, 0:D], hT[0:n, c, :], wexp[0:n, bass.ds(expert + (KD * W13 + c * D), D)],
                                   start=(c == 0), stop=(c == C1 - 1))
                mm.then_inc(d_down, 1)

            def expert_of(i):
                at = blk_i[0:1, i:i + 1] if isinstance(i, int) else blk_i[0:1, bass.ds(i, 1)]
                return pe.value_load(at, min_val=0, max_val=(E1 - 1) * WE)

            def block_pe(i, k, more=True):
                up1(i, k, expert_of(i))
                if k:
                    down1(i - 1, k - 1, expert_of(i - 1))
                if more:
                    turn_slots(i + 1, k + 1)
                turn_hidden(i, k)
            pe.wait_ge(in_exp0, 16 * 7)
            pe.wait_ge(in_exp7, 16)
            turn_slots(0, 0)
            pe.wait_ge(blk_ready, 1)
            each(pe, NBLK - 1, 2, 2, block_pe)
            block_pe(NBLK - 1, 2, False)
            down1(NBLK - 1, 2, expert_of(NBLK - 1))

        @block.vector
        def _(dve):
            def stats(norm, b):
                dve.memset(carrier[:, :], 0.0)
                for j in range(TB):
                    dve.bn_stats(st6[:, j, :], x_sb[:, b * TB + j, :]).then_inc(ln_stats, 1)
                dve.wait_ge(ln_stats, (norm * B + b) * TB + TB)
                dve.memset(carrier[:, :], 0.0)
                for j in range(TB):
                    dve.bn_aggr(mv[:, j, :], st6[:, j, :]).then_inc(ln_mv, 1)
                dve.wait_ge(ln_mv, (norm * B + b) * TB + TB)
                dve.tensor_copy(mean[:, bass.ds(b * TB, TB)], mv[:, :, 0])
                dve.tensor_scalar(ve[:, bass.ds(b * TB, TB)], mv[:, :, 1], 1e-5, None,
                                  ALU.add).then_inc(ln_var, 1)

            def rows_of(norm, b, k):
                dve.wait_ge(ln_rstd, norm * B + b + 1)
                if k >= 2 or norm >= 2:
                    dve.wait_ge(ln_turned, norm * B + b - 1)
                for j in range(TB):
                    t = b * TB + j
                    to = xn_of[norm]
                    r = dve.tensor_scalar(to[:, k % 2, j, :], x_sb[:, t, :], mean[:, bass.ds(t, 1)],
                                          rstd[:, bass.ds(t, 1)], ALU.subtract, ALU.mult)
                r.then_inc(ln_rows, 1)

            dve.memset(t8[:, :, :], NEG).then_inc(dve_const, 1)
            dve.memset(pmask[:, :], 0.0).then_inc(dve_const, 1)
            dve.wait_ge(dve_const, 2)
            dve.memset(pmask[0:NK, 0:1], 1.0).then_inc(dve_const, 1)
            dve.memset(pmask[NK:P, 1:2], 1.0).then_inc(dve_const, 1)
            def first_norm(b, k):
                if k == 2:
                    dve.wait_ge(in_x1, 16)
                stats(0, b)
                if k >= 1:
                    rows_of(0, b - 1, k - 1)
            dve.wait_ge(in_x0, 16)
            for b in range(4):
                first_norm(b, b)
            with dve.Fori(2, B // 2) as pair:
                for j in range(2):
                    first_norm(pair * 2 + j, 4 + j)
            rows_of(0, B - 1, 3)

            dve.wait_ge(in_itok, 16)
            dve.wait_ge(pool_step, 9)
            dve.tensor_copy(hit[:, 0, 0:TB * TOPK_SETS], itok[:, :, :].rearrange("p j k -> p (j k)")).then_inc(s_mask, 1)
            dve.wait_ge(s_mask, 1)
            for j in range(TB):
                dve.tensor_scalar(negmask[:, j, :], iota[:, 0:NK], hit[:, 0, j * TOPK_SETS:j * TOPK_SETS + 1], None,
                                  ALU.is_equal).then_inc(s_mask, 1)
            for n in range(1, TOPK_SETS):
                dve.wait_ge(s_mask, 1 + TB * n)
                for j in range(TB):
                    o = j * TOPK_SETS + n
                    dve.scalar_tensor_tensor(out=negmask[:, j, :], in0=iota[:, 0:NK], scalar=hit[:, 0, o:o + 1],
                                             in1=negmask[:, j, :], op0=ALU.is_equal, op1=ALU.max).then_inc(s_mask, 1)
            dve.wait_ge(s_mask, 1 + TB * TOPK_SETS)
            dve.tensor_scalar(negmask, negmask, 1.0, -NEG, ALU.subtract, ALU.mult).then_inc(s_mask, 1)
            dve.wait_ge(s_mask, 2 + TB * TOPK_SETS)
            dve.wait_ge(a_bias, 1)
            dve.tensor_tensor(negmask, negmask, bank(7)[:, 0:NK].unsqueeze(1).broadcast_to([P, TB, NK]),
                              ALU.add).then_inc(s_mask, 1)
            dve.wait_ge(s_mask, 3 + TB * TOPK_SETS)

            def pick(b, k):
                dve.wait_ge(a_scored, 4 * (b // 4 + 1))
                pair = bass.ds(b * TB, TB)
                dve.tensor_tensor(ms[:, pair, :], bank(2, 2).rearrange("p (t n) -> p t n", t=NT)[:, pair, :],
                                  negmask, ALU.add).then_inc(a_masked, 1)
                dve.wait_ge(a_masked, b + 1)
                for j in range(TB):
                    dve.max(m8[:, b * TB + j, :], ms[:, b * TB + j, :]).then_inc(a_max, 1)
                dve.wait_ge(a_max, b * TB + TB)
                dve.tensor_copy(t8[:, pair, 0:2], m8[:, pair, 0:2]).then_inc(a_top, 1)
                dve.tensor_scalar(negm[:, pair], m8[:, pair, 0], -1.0, None, ALU.mult).then_inc(a_top, 1)
                dve.wait_ge(a_top, b * 2 + 2)
                for j in range(TB):
                    dve.match_replace(picked[:, b * TB + j, :], t8[:, b * TB + j, :], ms[:, b * TB + j, :],
                                      FOUND).then_inc(a_picked, 1)
            for b in range(B):
                pick(b, b)

            dve.wait_ge(in_kv, 16 * 13)
            dve.tensor_tensor(gg[:, :], vecs[:, 1, :], vecs[:, 3, :], ALU.mult).then_inc(gg_ready, 1)

            def mix_values(b, k):
                dve.wait_ge(v_psum, b + 1)
                o = vbd[:, b, :, :].rearrange("p a (r n) -> p a r n", r=2)
                half = pmask[:, :].unsqueeze(1)
                dve.tensor_tensor(o[:, :, :, 0:HD], bank(4 + k % 2)[:, 0:D].rearrange("p (a r n) -> p a r n", a=8, r=2),
                                  half.unsqueeze(3).broadcast_to([P, 8, 2, HD]), ALU.mult).then_inc(v_ready, 1)
                dve.tensor_copy(o[:, :, :, HD], half.broadcast_to([P, 8, 2])).then_inc(v_ready, 1)
            dve.wait_ge(dve_const, 4)
            each(dve, B, 0, 2, mix_values)
            dve.wait_ge(k_sum, 1)
            dve.tensor_scalar(kvar, bank(0)[:, 0:B * NK // P], 1.0 / D, 1e-6, ALU.mult, ALU.add).then_inc(k_var, 1)

            def weigh_sets(t, k):
                dve.wait_ge(a_exp, t + 1)
                dve.wait_ge(a_picked, t + 1)
                dve.scalar_tensor_tensor(out=ms[:, t, :], in0=picked[:, t, :], scalar=1.0e38, in1=ex[:, t, :],
                                         op0=ALU.is_gt, op1=ALU.mult, accum_out=sums[:, bass.ds(t, 1)]).then_inc(a_wts, 1)
            for t in range(NT):
                weigh_sets(t, t)
            dve.wait_ge(a_wts, NT)
            dve.reciprocal(recs[:, :], sums[:, :]).then_inc(a_rec, 1)
            dve.wait_ge(k_pow, 1)
            for q in range(B * NK // P):
                dve.tensor_scalar(kdiag[:, q, :], ident[:, :], krst[:, q:q + 1], None, ALU.mult).then_inc(k_diag, 1)
            dve.wait_ge(k_spread, 1)
            dve.wait_ge(k_copied, 4)
            dve.wait_ge(gg_ready, 1)
            for m in range(KD):
                dve.scalar_tensor_tensor(out=kT[:, m, :], in0=kT[:, m, :], scalar=gg[:, m:m + 1], in1=bank(1),
                                         op0=ALU.mult, op1=ALU.mult).then_inc(k_scaled, 1)
            dve.wait_ge(a_rec, 1)

            def mix_sets(b, k):
                dve.wait_ge(a_mixed, b + 1)
                for j in range(TB):
                    t = b * TB + j
                    dve.scalar_tensor_tensor(out=x_sb[:, t, :], in0=bank(6 + k % 2)[:, j * D:(j + 1) * D],
                                             scalar=recs[:, bass.ds(t, 1)], in1=x_sb[:, t, :],
                                             op0=ALU.mult, op1=ALU.add).then_inc(x_new, 1)
                dve.wait_ge(x_new, b * TB + TB)
                stats(1, b)
                if k >= 1:
                    rows_of(1, b - 1, k - 1)
            each(dve, B, 4, 2, mix_sets)
            rows_of(1, B - 1, 3)

            dve.wait_ge(ln_turned, 2 * B)
            dve.wait_ge(in_rest, 16 * 5)
            dve.memset(sel0[:, :, E0:E0 + 4], NEG).then_inc(b_step, 1)
            dve.wait_ge(fill_done, 16)
            dve.wait_ge(rest_done, 16)
            dve.memset(arena[:, 1024:1792], 0.0).then_inc(b_step, 1)
            dve.wait_ge(b_sig, 1)
            dve.tensor_tensor(sel0[:, :, 0:E0], sc0, ebias[:, :].unsqueeze(1).broadcast_to([P, NT, E0]),
                              ALU.add).then_inc(b_step, 1)
            dve.wait_ge(b_step, 3)
            for t in range(NT):
                dve.max(m8[:, t, :], sel0[:, t, :]).then_inc(b_max, 1)
            dve.wait_ge(b_max, NT)
            dve.tensor_copy(t8[:, :, 0:4], m8[:, :, 0:4]).then_inc(b_step, 1)
            dve.wait_ge(b_step, 4)
            for t in range(NT):
                dve.match_replace(rep0[:, t, :], t8[:, t, :], sel0[:, t, :], FOUND).then_inc(b_max, 1)
            dve.wait_ge(b_max, 2 * NT)
            dve.scalar_tensor_tensor(out=cw0, in0=rep0[:, :, 0:E0], scalar=1.0e38, in1=sc0,
                                     op0=ALU.is_gt, op1=ALU.mult).then_inc(b_step, 1)
            dve.wait_ge(b_step, 5)
            dve.tensor_reduce(sums[:, :], cw0, AX.X, ALU.add).then_inc(b_step, 1)
            dve.wait_ge(b_step, 6)
            dve.tensor_scalar(sums[:, :], sums[:, :], 1e-20, None, ALU.add).then_inc(b_step, 1)
            dve.wait_ge(b_step, 7)
            dve.reciprocal(recs[:, :], sums[:, :]).then_inc(b_step, 1)
            dve.wait_ge(b_step, 8)
            dve.tensor_tensor(cw0, cw0, recs[:, :].unsqueeze(2).broadcast_to([P, NT, E0]), ALU.mult).then_inc(b_step, 1)
            dve.wait_ge(b_step, 9)
            dve.tensor_copy(c3[:, :, 0:E0], cw0).then_inc(b_c3, 1)
            dve.wait_ge(b_c3, 1)
            dve.tensor_tensor(res0, cw0, c3[:, :, 0:E0], ALU.subtract).then_inc(b_step, 1)
            dve.wait_ge(b_step, 10)
            dve.tensor_copy(c3[:, :, 32:32 + E0], res0).then_inc(b_c3, 1)
            dve.wait_ge(b_c3, 2)
            dve.tensor_tensor(c3[:, :, 64:64 + E0], res0, c3[:, :, 32:32 + E0], ALU.subtract).then_inc(b_c3, 1)

            def add_ffn0(g):
                dve.wait_ge(b_down, g * C0 + C0)
                for j in range(2):
                    t = g * 4 + j * 2
                    o = x_sb[:, bass.ds(t, 2), :].rearrange("p t d -> p (t d)")
                    dve.tensor_tensor(o, o, bank(6 + j), ALU.add).then_inc(x_new, 1)

            def ffn0_group(g, k):
                if k:
                    add_ffn0(g - 1)
                for c in range(C0):
                    i, rows_ = g * C0 + c, P if c < C0 - 1 else I0
                    dve.wait_ge(b_silu, i + 1)
                    dve.tensor_tensor(hm0[0:rows_, c % 2, :], sg0[0:rows_, c % 2, :], bank(2 + c % 2)[0:rows_, :],
                                      ALU.mult).then_inc(b_prod, 1)
                    dve.wait_ge(b_prod, i + 1)
                    if c < C0 - 1:
                        dve.wait_ge(b_spread, g * (C0 - 1) + c + 1)
                        dve.tensor_tensor(hm0[:, c % 2, :], hm0[:, c % 2, :], bank(4), ALU.mult).then_inc(b_mult, 1)
                        dve.wait_ge(b_mult, g * (C0 - 1) + c + 1)
                    if k or c >= 2:
                        dve.wait_ge(b_down, i if c == 0 else i - 1)
                    dve.tensor_copy(h_high[0:rows_, c % 2, :], hm0[0:rows_, c % 2, :]).then_inc(b_high, 1)
                    dve.wait_ge(b_high, i + 1)
                    for j in range(2):
                        cols = slice(j * 256, (j + 1) * 256)
                        dve.tensor_tensor(h_low[0:rows_, c % 2, cols], hm0[0:rows_, c % 2, cols],
                                          h_high[0:rows_, c % 2, cols].bitcast(F32), ALU.subtract).then_inc(b_hidden, 1)
                    if k and c in (1, 3):
                        dve.wait_ge(x_new, g * 2 + XA)
                        stats(2, g * 2 - 2 + c // 2)
                    if k and c in (5, 7):
                        rows_of(2, g * 2 - 2 + (c - 5) // 2, (c - 5) // 2)
            each(dve, NG, 1, 1, ffn0_group)
            add_ffn0(NG - 1)
            dve.wait_ge(x_new, XB)
            for b in range(B - 2, B):
                stats(2, b)

            for b in range(B - 2, B):
                rows_of(2, b, b % 2)
            dve.wait_ge(c_ssq, B)
            dve.tensor_scalar(ssq[:, :], bank(7)[:, 0:NT], HD / D, HD * 1e-6, ALU.mult, ALU.add).then_inc(c_var, 1)

            def centre(t, k):
                dve.wait_ge(c_scores, t + 1)
                s = bank(0, 2).rearrange("p (h n) -> p h n", h=H)
                dve.tensor_reduce(mx1[:, :], s, AX.X, ALU.max).then_inc(c_max, 1)
                dve.wait_ge(c_max, t + 1)
                if k:
                    dve.wait_ge(c_probs, t)
                dve.tensor_tensor(shift.rearrange("p (h n) -> p h n", h=H), s,
                                  mx1[:, :].unsqueeze(2).broadcast_to([P, H, NK]), ALU.subtract).then_inc(c_shift, 1)

            def divide(t, k):
                dve.wait_ge(c_pv, t + 1)
                v = bank(4)[:, 0:H * (HD + 1)].rearrange("p (h n) -> p h n", h=H)
                dve.reciprocal(rec1[:, :], v[:, :, HD]).then_inc(c_rec, 1)
                dve.wait_ge(c_rec, t + 1)
                if k:
                    dve.wait_ge(c_attT, t)
                dve.tensor_tensor(att.rearrange("p (h n) -> p h n", h=H), v[:, :, 0:HD],
                                  rec1[:, :].unsqueeze(2).broadcast_to([P, H, HD]), ALU.mult).then_inc(c_att, 1)

            def add_att(t, k):
                dve.wait_ge(c_proj, t + 1)
                dve.tensor_tensor(x_sb[:, t, :], x_sb[:, t, :], bank(6)[:, 0:D], ALU.add).then_inc(x_new, 1)

            def attend(t, k, b0, j):
                centre(t, k)
                if k >= 2:
                    add_att(t - 2, k - 2)
                if k >= 1:
                    divide(t - 1, k - 1)
                if k >= 2:
                    if k % TB == 1:
                        dve.wait_ge(x_new, t - 2 + XB + 1)
                        stats(3, b0 + (j - 2) // TB)
                    elif k >= 4:
                        rows_of(3, b0 - 2 + j // TB, j // TB)
            for t in range(4):
                if t == 2:
                    dve.wait_ge(c_biased, B)
                attend(t, t, 0, t)
            with dve.Fori(0, B // 2 - 1) as pair:
                for j in range(4):
                    attend(pair * 4 + (4 + j), 4 + j, pair * 2 + 2, j)
            rows_of(3, B - 2, 0)
            add_att(NT - 2, 2)
            divide(NT - 1, 3)
            add_att(NT - 1, 3)
            dve.wait_ge(x_new, XC)
            stats(3, B - 1)
            rows_of(3, B - 1, 1)

            done = [0]

            def step(instruction):
                instruction.then_inc(d_step, 1)
                done[0] += 1
                dve.wait_ge(d_step, done[0])

            def over_experts(a):
                return a.unsqueeze(2).broadcast_to([P, NT, E1])

            dve.scalar_tensor_tensor(out=nmr[:, :], in0=mean[:, :], scalar=-1.0, in1=rstd[:, :],
                                     op0=ALU.mult, op1=ALU.mult).then_inc(xr_shift, 1)
            dve.wait_ge(d_logits, 1)
            logits = bank(0)[:, 0:NT * E1].rearrange("p (t e) -> p t e", t=NT)
            step(dve.tensor_scalar(li, logits, float(Q_IN), ROUND, ALU.mult, ALU.add))
            step(dve.tensor_scalar(li, li, ROUND, None, ALU.subtract))
            step(dve.tensor_reduce(m1[:, :], li, AX.X, ALU.max))
            step(dve.tensor_tensor(sh, li, over_experts(m1[:, :]), ALU.subtract))
            step(dve.tensor_scalar(sh, sh, -float(Q_IN), None, ALU.max))
            step(dve.scalar_tensor_tensor(out=key, in0=sh, scalar=float(E1),
                                          in1=iota[:, 0:E1].unsqueeze(1).broadcast_to([P, NT, E1]),
                                          op0=ALU.mult, op1=ALU.subtract))
            for t in range(NT):
                dve.max(m8[:, t, :], key[:, t, :]).then_inc(d_max, 1)
            dve.wait_ge(d_max, NT)
            dve.tensor_tensor(keep, key, over_experts(m8[:, :, 1]), ALU.is_ge).then_inc(kept, 1)
            dve.wait_ge(kept, 1)
            step(dve.tensor_scalar(zz, sh, 1.0 / Q_IN, None, ALU.mult))
            coef = exp_coefficients()
            step(dve.tensor_scalar(po, zz, coef[-1], None, ALU.mult))
            for c in coef[-2:0:-1]:
                step(dve.scalar_tensor_tensor(out=po, in0=po, scalar=c, in1=zz, op0=ALU.add, op1=ALU.mult))
            step(dve.tensor_scalar(po, po, Q_OUT, Q_OUT - 0.5, ALU.mult, ALU.add))
            step(dve.tensor_scalar(po, po, ROUND, None, ALU.add))
            step(dve.tensor_scalar(po, po, ROUND, None, ALU.subtract))
            step(dve.tensor_tensor(po, po, keep, ALU.mult))
            step(dve.tensor_reduce(m1[:, :], po, AX.X, ALU.add))
            step(dve.reciprocal(m1[:, :], m1[:, :]))
            step(dve.tensor_tensor(po, po, over_experts(m1[:, :]), ALU.mult))

            dve.wait_ge(counted, 1)
            step(dve.tensor_copy(cum[:, 0, :, :], bank(5)[:, 0:NT * E1].rearrange("p (t e) -> p t e", t=NT)))
            for n, d in enumerate((1, 2, 4, 8)):
                a, b = cum[:, n % 2, :, :], cum[:, 1 - n % 2, :, :]
                dve.tensor_copy(b[:, 0:d, :], a[:, 0:d, :])
                step(dve.tensor_tensor(b[:, d:NT, :], a[:, d:NT, :], a[:, 0:NT - d, :], ALU.add))
            cum0 = cum[:, 0, :, :]
            step(dve.tensor_tensor(slot, cum0, bank(5)[:, 0:NT * E1].rearrange("p (t e) -> p t e", t=NT), ALU.subtract))
            step(dve.tensor_tensor(slot, slot, bank(4)[:, 0:NT * E1].rearrange("p (t e) -> p t e", t=NT), ALU.add))
            nb, nbs = small8[:, 0, :], [small8[:, 1, :], small8[:, 2, :]]
            step(dve.tensor_scalar(nb, cum0[:, NT - 1, :], 1.0 / P, (P - 1.0) / P - 0.498, ALU.mult, ALU.add))
            step(dve.tensor_scalar(nb, nb, ROUND, None, ALU.add))
            step(dve.tensor_scalar(nb, nb, ROUND, None, ALU.subtract))
            step(dve.tensor_copy(nbs[0], nb))
            for n, d in enumerate((1, 2, 4)):
                a, b = nbs[n % 2], nbs[1 - n % 2]
                dve.tensor_copy(b[:, 0:d], a[:, 0:d])
                step(dve.tensor_tensor(b[:, d:E1], a[:, d:E1], a[:, 0:E1 - d], ALU.add))
            upto = nbs[1]
            step(dve.tensor_tensor(nb, upto, nb, ALU.subtract))
            step(dve.tensor_scalar(nb, nb, float(P), 1.0, ALU.mult, ALU.add))
            step(dve.tensor_tensor(slot, slot, nb.unsqueeze(1).broadcast_to([P, NT, E1]), ALU.add))
            step(dve.tensor_tensor(slot, slot, keep, ALU.mult))
            step(dve.tensor_reduce(m1[:, :], slot, AX.X, ALU.max))
            step(dve.tensor_reduce(sums[:, :], slot, AX.X, ALU.add))
            dve.tensor_tensor(slot, slot, over_experts(m1[:, :]), ALU.is_equal)
            dve.tensor_scalar(place[:, 0, :], m1[:, :], -1.0, None, ALU.add)
            step(dve.scalar_tensor_tensor(out=place[:, 1, :], in0=sums[:, :], scalar=-1.0, in1=m1[:, :],
                                          op0=ALU.add, op1=ALU.subtract))
            dve.tensor_scalar(column[:, :, :], place[:, :, :], 1.0 / P, -0.498, ALU.mult, ALU.add)
            step(dve.tensor_tensor(slot, slot, po, ALU.mult))
            dve.tensor_reduce(weight[:, 0, :], slot, AX.X, ALU.add)
            dve.tensor_scalar(column[:, :, :], column[:, :, :], ROUND, None, ALU.add)
            step(dve.tensor_tensor(po, po, slot, ALU.subtract))
            dve.tensor_reduce(weight[:, 1, :], po, AX.X, ALU.add)
            step(dve.tensor_scalar(column[:, :, :], column[:, :, :], ROUND, None, ALU.subtract))
            step(dve.scalar_tensor_tensor(out=inblock[:, :, :], in0=column[:, :, :], scalar=-float(P),
                                          in1=place[:, :, :], op0=ALU.mult, op1=ALU.add))
            step(dve.tensor_copy(weight_high[:, :, :], weight[:, :, :]))
            step(dve.tensor_tensor(weight[:, :, :], weight[:, :, :], weight_high[:, :, :].bitcast(F32), ALU.subtract))
            dve.wait_ge(pool_slot, 5)
            step(dve.tensor_tensor(rowval[:, :, :], token[:, :].unsqueeze(1).broadcast_to([P, 2, NT]),
                                   inblock[:, :, :], ALU.subtract))

            for n in range(NSRC // BATCH):
                def over(a, width):
                    return a[:, :, :].rearrange("p w t -> p (w t)")[:, n * BATCH:(n + 1) * BATCH].unsqueeze(
                        2).broadcast_to([P, BATCH, width])
                if n >= 2:
                    dve.wait_ge(d_placed, n - 1)
                dve.tensor_tensor(incolumn[:, n % 2, :, :], blkno[:, :].unsqueeze(1).broadcast_to([P, BATCH, COLS]),
                                  over(column, COLS), ALU.is_equal).then_inc(d_columns, 1)
                dve.tensor_tensor(onehot[:, n % 2, :, :], iota[:, :].unsqueeze(1).broadcast_to([P, BATCH, P]),
                                  over(inblock, P), ALU.is_equal).then_inc(d_onehot, 1)
            dve.wait_ge(d_placed, NSRC // BATCH)
            dve.tensor_scalar(slot_row[:, :], bank(6)[:, 0:NBLK], norow[:, 0:1], None, ALU.add).then_inc(slots_known, 1)
            step(dve.tensor_copy(slot_w[:, :], bank(6)[:, COLS:COLS + NBLK]))
            dve.tensor_tensor(slot_w[:, :], slot_w[:, :], bank(6)[:, 2 * COLS:2 * COLS + NBLK], ALU.add).then_inc(slots_known, 1)
            step(dve.tensor_scalar(blk[:, :], blkno[:, 0:NBLK], upto[:, 0:1], None, ALU.is_ge))
            for e in range(1, E1 - 1):
                step(dve.scalar_tensor_tensor(out=blk[:, :], in0=blkno[:, 0:NBLK], scalar=upto[:, e:e + 1], in1=blk[:, :],
                                              op0=ALU.is_ge, op1=ALU.add))
            dve.tensor_scalar(blk_i[:, :], blk[:, :], float(WE), None, ALU.mult).then_inc(blk_ready, 1)
            dve.wait_ge(slots_known, 2)

            def weighted(i, k):
                dve.wait_ge(d_down, i + 1)
                if k >= 2:
                    dve.wait_ge(d_added, (i - 1) * 16)
                dve.tensor_scalar(yb[:, k % 2, :], bank(6)[:, 0:D], slot_w[:, bass.ds(i, 1)], None,
                                  ALU.mult).then_inc(d_y, 1)

            def block_dve(i, k):
                dve.wait_ge(d_silu, i + 1)
                if k:
                    dve.wait_ge(d_turned, i)
                dve.tensor_tensor(h1.rearrange("p (a n) -> p a n", a=2),
                                  sg1.rearrange("p (a n) -> p a n", a=2),
                                  bank(2, 2).rearrange("p (a n) -> p a n", a=2)[:, :, 0:HALF1],
                                  ALU.mult).then_inc(d_hidden, 1)
                if k:
                    weighted(i - 1, k - 1)
            each(dve, NBLK - 1, 4, 2, block_dve)
            block_dve(NBLK - 1, 4)
            weighted(NBLK - 1, 4)


def kernel(**inputs):
    import concourse.bacc as _bacc
    from concourse.bass_utils import run_bass_kernel_spmd as _run

    g = {name: np.asarray(a) for name, a in inputs.items()}
    gu, dn = g["L0_ffn_gate_up_proj"], g["L0_ffn_down_proj"]
    chunks = E0 * I0 // P
    gate = gu[:, 0:I0, :].reshape(chunks, P, D)
    up = gu[:, I0:2 * I0, :].reshape(chunks, P, D)
    gu0 = np.concatenate([np.stack([gate, up], 1).reshape(2 * E0 * I0, D),
                          g["L0_ffn_shared_gate_w"], g["L0_ffn_shared_up_w"]], 0).T
    dn0 = np.zeros((P, C0, D), dn.dtype)
    dn0[:, 0:chunks] = dn.transpose(0, 2, 1).reshape(chunks, P, D).transpose(1, 0, 2)
    dn0[0:I0, chunks] = g["L0_ffn_shared_down_w"].T
    w1, w2, w3 = g["L1_ffn_w1"], g["L1_ffn_w2"], g["L1_ffn_w3"]
    wexp = np.zeros((P, E1, WE), w1.dtype)
    for e in range(E1):
        for k in range(KD):
            wexp[:, e, k * W13:k * W13 + I1] = w1[e].T[k * P:(k + 1) * P]
            wexp[:, e, k * W13 + I1:(k + 1) * W13] = w3[e].T[k * P:(k + 1) * P]
        for c in range(C1):
            n = min(P, I1 - c * P)
            wexp[0:n, e, KD * W13 + c * D:KD * W13 + (c + 1) * D] = w2[e].T[c * P:c * P + n]
    def columns(vector):
        return vector.reshape(KD, P).T

    arrays = {
        "x": g["x"], "ctx": g["ctx_2048"], "ctxT": g["ctx_2048"].reshape(B * NK, D).T,
        "itok": g["itok_Sx4_0_63"], "descT": g["L0_xattn_desc_router"].T, "wq0": g["L0_xattn_W_q"],
        "bq0": columns(g["L0_xattn_b_q"]), "rw0": g["L0_ffn_router_w"].T, "ebias": g["L0_ffn_e_bias"],
        "gu0": gu0, "dn0": dn0, "wq1": g["L1_xattn_Wq"], "bq1": columns(g["L1_xattn_bq"]),
        "gq1": columns(g["L1_xattn_gq"]), "wk1": g["L1_xattn_Wk_img"], "bk1": columns(g["L1_xattn_bk_img"]),
        "gk1": columns(g["L1_xattn_gk_img"]), "wv1": g["L1_xattn_Wv_img"], "bv1": g["L1_xattn_bv_img"],
        "wo1": g["L1_xattn_Wo"], "bo1": g["L1_xattn_bo"], "wg1": g["L1_ffn_w_gate"].T, "wexp": wexp,
    }
    nc = _bacc.Bacc("TRN2", target_bir_lowering=False, num_devices=1)
    feed, args = {}, []
    for name, a in arrays.items():
        a = np.ascontiguousarray(a)
        feed[f"in_{name}"] = a
        args.append(nc.dram_tensor(f"in_{name}", a.shape, mybir.dt.from_np(a.dtype), kind="ExternalInput").ap())
    args.append(nc.dram_tensor("out_rows", ((NT + 1) * P, D), F32, kind="ExternalOutput").ap())
    program(nc, *args)
    return _run(nc, [feed], core_ids=[0]).results[0]["out_rows"][0:NT * P].reshape(B, S, D)
```
